# Optimizing a Trainium2 kernel written in Bass

```python
import numpy as np
import jax
import jax.numpy as jnp

def _softmax(x, axis=-1):
    return jax.nn.softmax(x, axis=axis)

def _gelu(x):
    return jax.nn.gelu(x, approximate=True)

def _silu(x):
    return jax.nn.silu(x)

def _sigmoid(x):
    return jax.nn.sigmoid(x)

def _layernorm(x, axis=-1, eps=1e-05):
    m = jnp.mean(x, axis=axis, keepdims=True)
    v = jnp.var(x, axis=axis, keepdims=True)
    return (x - m) / jnp.sqrt(v + eps)

def _scatter_add(tgt, idx, src, axis=0):
    return tgt.at[idx].add(src)

def _segment_sum(src, seg, n):
    return jax.ops.segment_sum(src, seg, n)
kernel_name = 'mk_gnn_preln_d4_gnn_r32_1d6e05'

def setup_inputs(seed: int=0):
    np.random.seed(seed)
    _w = jnp.asarray

    def _rec_inputs():
        import jax
        import jax.numpy as jnp
        _gk = jax.random.key(seed)
        x = -0.000202 + 1 * jax.random.normal(jax.random.fold_in(_gk, 1), (50000, 128), jnp.float32)
        src = jax.random.randint(jax.random.fold_in(_gk, 2), (25000,), 0, 50000, jnp.int32)
        dst = jax.random.randint(jax.random.fold_in(_gk, 3), (25000,), 0, 50000, jnp.int32)
        _o = jnp.argsort(dst, stable=True)
        src = src[_o]
        dst = dst[_o]
        edge_type_16 = jax.random.randint(jax.random.fold_in(_gk, 12), (25000,), 0, 16, jnp.int32)
        return (x, src, dst, edge_type_16)
    x, src, dst, edge_type_16 = _rec_inputs()

    def _L0_gnn_setup():
        import jax, jax.numpy as jnp
        import numpy as np
        N = 50000
        E = 25000
        D = 128
        H = 4
        Dh = D // H

        def _transformer_conv(x, src, dst, qw, qb, kw, kb, vw, vb, sw, sb):
            n = x.shape[0]
            q = (x @ qw + qb).reshape(n, H, Dh)
            k = (x @ kw + kb).reshape(n, H, Dh)
            v = (x @ vw + vb).reshape(n, H, Dh)
            logits = jnp.einsum('ehd,ehd->eh', q[dst], k[src]) / jnp.sqrt(jnp.float32(Dh))
            m = jax.ops.segment_max(logits, dst, num_segments=n)
            e = jnp.exp(logits - m[dst])
            s = jax.ops.segment_sum(e, dst, num_segments=n)
            alpha = e / (s[dst] + 1e-16)
            msg = v[src] * alpha[:, :, None]
            out = jax.ops.segment_sum(msg, dst, num_segments=n)
            out = out.reshape(n, H * Dh)
            return out + x @ sw + sb
        key = jax.random.key(seed)
        ks = jax.random.split(key, 12)
        inp = {'x': jax.random.normal(ks[0], (N, D), jnp.float32), 'edge_index': jax.random.randint(ks[1], (2, E), 0, N, dtype=jnp.int64)}
        i = 2
        for l in range(2):
            for nm in ('q', 'k', 'v', 's'):
                inp[f'{nm}_w{l}'] = jax.random.normal(ks[i], (D, D), jnp.float32) / np.float32(np.sqrt(D))
                inp[f'{nm}_b{l}'] = jnp.zeros((D,), jnp.float32)
            i += 1
        return inp
    _L0_gnn_all = _L0_gnn_setup()
    _L0_gnn_in = {k: v for k, v in _L0_gnn_all.items() if k in ('q_w0', 'q_b0', 'k_w0', 'k_b0', 'v_w0', 'v_b0', 's_w0', 's_b0', 'q_w1', 'q_b1', 'k_w1', 'k_b1', 'v_w1', 'v_b1', 's_w1', 's_b1')}
    del _L0_gnn_all

    def _L1_gnn_setup():
        import jax, jax.numpy as jnp
        import numpy as np
        N = 3125
        E = 50000
        D_IN, D_HID, D_OUT = (128, 256, 128)

        def _sage_conv(x, src, dst, W_l, b_l, W_r, num_nodes):
            msg = x[src]
            agg = jax.ops.segment_sum(msg, dst, num_segments=num_nodes)
            deg = jax.ops.segment_sum(jnp.ones((src.shape[0],), x.dtype), dst, num_segments=num_nodes)
            agg = agg / jnp.maximum(deg, 1.0)[:, None]
            return agg @ W_l + b_l + x @ W_r
        key = jax.random.key(seed)
        ks = jax.random.split(key, 8)
        x = jax.random.normal(ks[0], (N, D_IN), dtype=jnp.float32)
        edge_index = jax.random.randint(ks[1], (2, E), 0, N, dtype=jnp.int64)
        s0 = 1.0 / np.sqrt(D_IN)
        s1 = 1.0 / np.sqrt(D_HID)
        Wl0 = jax.random.uniform(ks[2], (D_IN, D_HID), jnp.float32, -s0, s0)
        bl0 = jnp.zeros((D_HID,), jnp.float32)
        Wr0 = jax.random.uniform(ks[3], (D_IN, D_HID), jnp.float32, -s0, s0)
        Wl1 = jax.random.uniform(ks[4], (D_HID, D_OUT), jnp.float32, -s1, s1)
        bl1 = jnp.zeros((D_OUT,), jnp.float32)
        Wr1 = jax.random.uniform(ks[5], (D_HID, D_OUT), jnp.float32, -s1, s1)
        return {'x': x, 'edge_index': edge_index, 'Wl0': Wl0, 'bl0': bl0, 'Wr0': Wr0, 'Wl1': Wl1, 'bl1': bl1, 'Wr1': Wr1}
    _L1_gnn_all = _L1_gnn_setup()
    _L1_gnn_in = {k: v for k, v in _L1_gnn_all.items() if k in ('Wl0', 'bl0', 'Wr0', 'Wl1', 'bl1', 'Wr1')}
    del _L1_gnn_all

    def _L2_gnn_setup():
        import jax, jax.numpy as jnp
        import numpy as np
        N_NODES = 3125
        N_EDGES = 50000
        N_FEAT = 128
        HIDDEN = 128
        N_CLASSES = 128
        N_RATES = 16
        EMBED = 64

        def gcn_conv(x, edge_index, W, b):
            n = x.shape[0]
            src, dst = (edge_index[0], edge_index[1])
            h = x @ W
            deg = jax.ops.segment_sum(jnp.ones(src.shape[0], dtype=h.dtype), dst, num_segments=n) + 1.0
            dinv = jax.lax.rsqrt(deg)
            norm = dinv[src] * dinv[dst]
            agg = jax.ops.segment_sum(h[src] * norm[:, None], dst, num_segments=n)
            agg = agg + h * (dinv * dinv)[:, None]
            return agg + b
        key = jax.random.key(seed)
        ks = jax.random.split(key, 12)
        graph = jax.random.normal(ks[0], (N_NODES, N_FEAT), dtype=jnp.float32)
        edge_index = jax.random.randint(ks[1], (2, N_EDGES), 0, N_NODES, dtype=jnp.int64)
        rates = jax.random.normal(ks[2], (N_RATES,), dtype=jnp.float32)
        s = lambda fan_in: 1.0 / np.sqrt(fan_in)
        W1 = jax.random.normal(ks[3], (N_FEAT, HIDDEN), dtype=jnp.float32) * s(N_FEAT)
        b1 = jnp.zeros((HIDDEN,), dtype=jnp.float32)
        W2 = jax.random.normal(ks[4], (2 * HIDDEN, N_CLASSES), dtype=jnp.float32) * s(2 * HIDDEN)
        b2 = jnp.zeros((N_CLASSES,), dtype=jnp.float32)
        e1_w = jax.random.normal(ks[5], (N_RATES, EMBED), dtype=jnp.float32) * s(N_RATES)
        e1_b = jax.random.normal(ks[6], (EMBED,), dtype=jnp.float32) * s(N_RATES)
        e2_w = jax.random.normal(ks[7], (EMBED, HIDDEN), dtype=jnp.float32) * s(EMBED)
        e2_b = jax.random.normal(ks[8], (HIDDEN,), dtype=jnp.float32) * s(EMBED)
        return {'graph': graph, 'edge_index': edge_index, 'rates': rates, 'W1': W1, 'b1': b1, 'W2': W2, 'b2': b2, 'e1_w': e1_w, 'e1_b': e1_b, 'e2_w': e2_w, 'e2_b': e2_b}
    _L2_gnn_all = _L2_gnn_setup()
    _L2_gnn_in = {k: v for k, v in _L2_gnn_all.items() if k in ('rates', 'W1', 'b1', 'W2', 'b2', 'e1_w', 'e1_b', 'e2_w', 'e2_b')}
    del _L2_gnn_all

    def _L3_gnn_setup():
        import jax, jax.numpy as jnp
        import numpy as np
        N_NODES = 3125
        N_EDGES = 18750
        D_IN = 128
        D_OUT = 128
        N_REL = 16
        N_BASES = 8
        key = jax.random.key(seed)
        ks = jax.random.split(key, 6)
        x = jax.random.normal(ks[0], (N_NODES, D_IN), dtype=jnp.float32)
        edge_index = jax.random.randint(ks[1], (2, N_EDGES), 0, N_NODES, dtype=jnp.int64)
        edge_type = jax.random.randint(ks[2], (N_EDGES,), 0, N_REL, dtype=jnp.int64)
        b_lim = float(np.sqrt(6.0 / (D_IN + D_OUT)))
        c_lim = float(np.sqrt(6.0 / (N_REL + N_BASES)))
        w_lim = float(np.sqrt(6.0 / (D_IN + D_OUT)))
        bases = jax.random.uniform(ks[3], (N_BASES, D_IN, D_OUT), jnp.float32, -b_lim, b_lim)
        coefficients = jax.random.uniform(ks[4], (N_REL, N_BASES), jnp.float32, -c_lim, c_lim)
        w_self = jax.random.uniform(ks[5], (D_OUT, D_IN), jnp.float32, -w_lim, w_lim)
        return {'x': x, 'edge_index': edge_index, 'edge_type': edge_type, 'bases': bases, 'coefficients': coefficients, 'w_self': w_self}
    _L3_gnn_all = _L3_gnn_setup()
    _L3_gnn_in = {k: v for k, v in _L3_gnn_all.items() if k in ('bases', 'coefficients', 'w_self')}
    del _L3_gnn_all
    return {'x': x, 'src': src, 'dst': dst, 'edge_type_16': edge_type_16, 'L0_gnn_q_w0': _L0_gnn_in['q_w0'], 'L0_gnn_q_b0': _L0_gnn_in['q_b0'], 'L0_gnn_k_w0': _L0_gnn_in['k_w0'], 'L0_gnn_k_b0': _L0_gnn_in['k_b0'], 'L0_gnn_v_w0': _L0_gnn_in['v_w0'], 'L0_gnn_v_b0': _L0_gnn_in['v_b0'], 'L0_gnn_s_w0': _L0_gnn_in['s_w0'], 'L0_gnn_s_b0': _L0_gnn_in['s_b0'], 'L0_gnn_q_w1': _L0_gnn_in['q_w1'], 'L0_gnn_q_b1': _L0_gnn_in['q_b1'], 'L0_gnn_k_w1': _L0_gnn_in['k_w1'], 'L0_gnn_k_b1': _L0_gnn_in['k_b1'], 'L0_gnn_v_w1': _L0_gnn_in['v_w1'], 'L0_gnn_v_b1': _L0_gnn_in['v_b1'], 'L0_gnn_s_w1': _L0_gnn_in['s_w1'], 'L0_gnn_s_b1': _L0_gnn_in['s_b1'], 'L1_gnn_Wl0': _L1_gnn_in['Wl0'], 'L1_gnn_bl0': _L1_gnn_in['bl0'], 'L1_gnn_Wr0': _L1_gnn_in['Wr0'], 'L1_gnn_Wl1': _L1_gnn_in['Wl1'], 'L1_gnn_bl1': _L1_gnn_in['bl1'], 'L1_gnn_Wr1': _L1_gnn_in['Wr1'], 'L2_gnn_rates': _L2_gnn_in['rates'], 'L2_gnn_W1': _L2_gnn_in['W1'], 'L2_gnn_b1': _L2_gnn_in['b1'], 'L2_gnn_W2': _L2_gnn_in['W2'], 'L2_gnn_b2': _L2_gnn_in['b2'], 'L2_gnn_e1_w': _L2_gnn_in['e1_w'], 'L2_gnn_e1_b': _L2_gnn_in['e1_b'], 'L2_gnn_e2_w': _L2_gnn_in['e2_w'], 'L2_gnn_e2_b': _L2_gnn_in['e2_b'], 'L3_gnn_bases': _L3_gnn_in['bases'], 'L3_gnn_coefficients': _L3_gnn_in['coefficients'], 'L3_gnn_w_self': _L3_gnn_in['w_self']}

def reference(x, src, dst, edge_type_16, L0_gnn_q_w0, L0_gnn_q_b0, L0_gnn_k_w0, L0_gnn_k_b0, L0_gnn_v_w0, L0_gnn_v_b0, L0_gnn_s_w0, L0_gnn_s_b0, L0_gnn_q_w1, L0_gnn_q_b1, L0_gnn_k_w1, L0_gnn_k_b1, L0_gnn_v_w1, L0_gnn_v_b1, L0_gnn_s_w1, L0_gnn_s_b1, L1_gnn_Wl0, L1_gnn_bl0, L1_gnn_Wr0, L1_gnn_Wl1, L1_gnn_bl1, L1_gnn_Wr1, L2_gnn_rates, L2_gnn_W1, L2_gnn_b1, L2_gnn_W2, L2_gnn_b2, L2_gnn_e1_w, L2_gnn_e1_b, L2_gnn_e2_w, L2_gnn_e2_b, L3_gnn_bases, L3_gnn_coefficients, L3_gnn_w_self):
    import jax
    import jax.numpy as jnp

    def _L0_gnn_ref(x, edge_index, q_w0, q_b0, k_w0, k_b0, v_w0, v_b0, s_w0, s_b0, q_w1, q_b1, k_w1, k_b1, v_w1, v_b1, s_w1, s_b1):
        import jax, jax.numpy as jnp
        import numpy as np
        N = 50000
        E = 25000
        D = 128
        H = 4
        Dh = D // H

        def _transformer_conv(x, src, dst, qw, qb, kw, kb, vw, vb, sw, sb):
            n = x.shape[0]
            q = (x @ qw + qb).reshape(n, H, Dh)
            k = (x @ kw + kb).reshape(n, H, Dh)
            v = (x @ vw + vb).reshape(n, H, Dh)
            logits = jnp.einsum('ehd,ehd->eh', q[dst], k[src]) / jnp.sqrt(jnp.float32(Dh))
            m = jax.ops.segment_max(logits, dst, num_segments=n)
            e = jnp.exp(logits - m[dst])
            s = jax.ops.segment_sum(e, dst, num_segments=n)
            alpha = e / (s[dst] + 1e-16)
            msg = v[src] * alpha[:, :, None]
            out = jax.ops.segment_sum(msg, dst, num_segments=n)
            out = out.reshape(n, H * Dh)
            return out + x @ sw + sb
        src, dst = (edge_index[0], edge_index[1])
        h = _transformer_conv(x, src, dst, q_w0, q_b0, k_w0, k_b0, v_w0, v_b0, s_w0, s_b0)
        h = jax.nn.relu(h)
        h = _transformer_conv(h, src, dst, q_w1, q_b1, k_w1, k_b1, v_w1, v_b1, s_w1, s_b1)
        return h

    def _L1_gnn_ref(x, edge_index, Wl0, bl0, Wr0, Wl1, bl1, Wr1):
        import jax, jax.numpy as jnp
        import numpy as np
        N = 3125
        E = 50000
        D_IN, D_HID, D_OUT = (128, 256, 128)

        def _sage_conv(x, src, dst, W_l, b_l, W_r, num_nodes):
            msg = x[src]
            agg = jax.ops.segment_sum(msg, dst, num_segments=num_nodes)
            deg = jax.ops.segment_sum(jnp.ones((src.shape[0],), x.dtype), dst, num_segments=num_nodes)
            agg = agg / jnp.maximum(deg, 1.0)[:, None]
            return agg @ W_l + b_l + x @ W_r
        src, dst = (edge_index[0], edge_index[1])
        n = x.shape[0]
        h = _sage_conv(x, src, dst, Wl0, bl0, Wr0, n)
        h = jax.nn.relu(h)
        out = _sage_conv(h, src, dst, Wl1, bl1, Wr1, n)
        return out

    def _L2_gnn_ref(graph, edge_index, rates, W1, b1, W2, b2, e1_w, e1_b, e2_w, e2_b):
        import jax, jax.numpy as jnp
        import numpy as np
        N_NODES = 3125
        N_EDGES = 50000
        N_FEAT = 128
        HIDDEN = 128
        N_CLASSES = 128
        N_RATES = 16
        EMBED = 64

        def gcn_conv(x, edge_index, W, b):
            n = x.shape[0]
            src, dst = (edge_index[0], edge_index[1])
            h = x @ W
            deg = jax.ops.segment_sum(jnp.ones(src.shape[0], dtype=h.dtype), dst, num_segments=n) + 1.0
            dinv = jax.lax.rsqrt(deg)
            norm = dinv[src] * dinv[dst]
            agg = jax.ops.segment_sum(h[src] * norm[:, None], dst, num_segments=n)
            agg = agg + h * (dinv * dinv)[:, None]
            return agg + b
        h = jax.nn.relu(gcn_conv(graph, edge_index, W1, b1))
        r = jnp.maximum(rates @ e1_w + e1_b, 0.0) @ e2_w + e2_b
        n = h.shape[0]
        h = jnp.concatenate([h, jnp.broadcast_to(r, (n, r.shape[0]))], axis=1)
        return gcn_conv(h, edge_index, W2, b2)

    def _L3_gnn_ref(x, edge_index, edge_type, bases, coefficients, w_self):
        import jax, jax.numpy as jnp
        import numpy as np
        N_NODES = 3125
        N_EDGES = 18750
        D_IN = 128
        D_OUT = 128
        N_REL = 16
        N_BASES = 8
        out = x @ w_self.T
        weights = jnp.einsum('rb,bio->rio', coefficients, bases)
        row, col = (edge_index[0], edge_index[1])
        xc = x[col]
        n_rel = weights.shape[0]
        msg = jnp.zeros((xc.shape[0], w_self.shape[0]), dtype=x.dtype)
        for r in range(n_rel):
            sel = (edge_type == r)[:, None]
            msg = msg + jnp.where(sel, xc @ weights[r], jnp.zeros((), x.dtype))
        out = out.at[row].add(msg)
        return out
    edge_index = jnp.stack([src, dst])
    h = jnp.maximum(_layernorm(x, axis=-1), 0.0)
    x = x + _L0_gnn_ref(h, edge_index, L0_gnn_q_w0, L0_gnn_q_b0, L0_gnn_k_w0, L0_gnn_k_b0, L0_gnn_v_w0, L0_gnn_v_b0, L0_gnn_s_w0, L0_gnn_s_b0, L0_gnn_q_w1, L0_gnn_q_b1, L0_gnn_k_w1, L0_gnn_k_b1, L0_gnn_v_w1, L0_gnn_v_b1, L0_gnn_s_w1, L0_gnn_s_b1)
    h = jnp.maximum(_layernorm(x, axis=-1), 0.0)
    x = x + _L1_gnn_ref(h, edge_index, L1_gnn_Wl0, L1_gnn_bl0, L1_gnn_Wr0, L1_gnn_Wl1, L1_gnn_bl1, L1_gnn_Wr1)
    h = jnp.maximum(_layernorm(x, axis=-1), 0.0)
    x = x + _L2_gnn_ref(h, edge_index, L2_gnn_rates, L2_gnn_W1, L2_gnn_b1, L2_gnn_W2, L2_gnn_b2, L2_gnn_e1_w, L2_gnn_e1_b, L2_gnn_e2_w, L2_gnn_e2_b)
    h = jnp.maximum(_layernorm(x, axis=-1), 0.0)
    x = x + _L3_gnn_ref(h, edge_index, edge_type_16, L3_gnn_bases, L3_gnn_coefficients, L3_gnn_w_self)
    return x

_drawn_inputs = setup_inputs


def setup_inputs(seed=0):
    import zlib

    import numpy as np

    out = dict(_drawn_inputs(seed))
    spreads = {'L0_gnn_q_b0': (0.0, 2.0),
     'L0_gnn_k_b0': (0.0, 2.0),
     'L0_gnn_v_b0': (0.0, 0.1),
     'L0_gnn_s_b0': (0.0, 0.1),
     'L0_gnn_q_b1': (0.0, 2.0),
     'L0_gnn_k_b1': (0.0, 2.0),
     'L0_gnn_v_b1': (0.0, 0.1),
     'L0_gnn_s_b1': (0.0, 0.1),
     'L1_gnn_bl0': (0.0, 0.1),
     'L1_gnn_bl1': (0.0, 0.1),
     'L2_gnn_b1': (0.0, 0.1),
     'L2_gnn_b2': (0.0, 0.1)}
    factors = {'L0_gnn_q_w0': 2.765, 'L0_gnn_k_w0': 2.828, 'L0_gnn_k_w1': 2.702}
    for name, (base, spread) in spreads.items():
        noise = np.random.default_rng([zlib.crc32(name.encode()), seed]).standard_normal(out[name].shape)
        drawn = base * np.exp(spread * noise) if base else spread * noise
        out[name] = jnp.asarray(drawn.astype(out[name].dtype))
    for name, factor in factors.items():
        out[name] = (out[name] * factor).astype(out[name].dtype)
    return out
```

```python
from contextlib import ExitStack

import concourse.bass as bass
from concourse import mybir

F32 = mybir.dt.float32
I32 = mybir.dt.int32
ALU = mybir.AluOpType
ACT = mybir.ActivationFunctionType

N = 50000
E = 25000
D = 128
P = 128
T = 4
GROUP = T * P
PAIRS = -(-E // (2 * GROUP))
NG = 2 * PAIRS
SLOTS = NG * GROUP
ROWS = SLOTS + N
NODE_TURNS = -(-N // (2 * GROUP))
NODE_TAIL = (N - (2 * NODE_TURNS - 1) * GROUP) // T
HEADS = 4
REL = 16
BASES = 8
FAR = 1e30
NO_ROW = 100000.0
OUT_ROWS = N + GROUP + 1
EPS = 1e-5
SOFT_EPS = 1e-16


class Count:

    def __init__(self, sem, per, unit, primed):
        self.sem, self.unit, self.per, self.primed = sem, unit, per * unit, per * unit if primed else 0

    def at(self, i, k=1):
        return self.sem, i * self.per + (self.primed - self.per + k * self.unit)

    def done(self, i):
        return self.sem, i * self.per + self.primed

    def before(self, i):
        assert self.primed > 0
        return self.sem, i * self.per + (self.primed - self.per)


class Phase:

    def __init__(self, nc, name):
        self.nc, self.name, self.stack, self.sems, self.counts = nc, name, ExitStack(), [], []
        self.waits_stood = self.sem("waits_stood")

    def sb(self, name, shape, dtype=F32):
        return self.stack.enter_context(self.nc.sbuf_tensor(f"{self.name}_{name}", shape, dtype))

    def psum(self, name, shape):
        return self.stack.enter_context(self.nc.psum_tensor(f"{self.name}_{name}", shape, F32))

    def sbs(self, name, shape, dtype=F32):
        return [self.sb(f"{name}{u}", shape, dtype) for u in range(2)]

    def banks(self):
        return [[self.psum(f"bank{u}{k}", [P, T, P]) for k in range(4)] for u in range(2)]

    def sem(self, name):
        s = self.nc.alloc_semaphore(f"{self.name}_{name}")
        self.sems.append(s)
        return s

    def pair(self, name, per=1, unit=1, primed=False, soft=False):
        both = [Count(self.sem(f"{name}{u}"), per, unit, primed) for u in range(2)]
        if primed:
            self.counts += [(c, soft) for c in both]
        return both

    def stand(self, eng):
        eng.sem_inc(self.waits_stood, 1)

    def prime(self, eng, cell, anything, soft=False):
        for n, (c, by_gpsimd) in enumerate(self.counts):
            if by_gpsimd != soft:
                continue
            if c.unit == 16:
                eng.dma_start(cell[0:1, n:n + 1], anything[0:1, n:n + 1]).then_inc(c.sem, c.primed)
            else:
                eng.sem_inc(c.sem, c.primed)

    def end(self):
        self.stack.close()
        self.nc.clear_and_free_semaphores(self.sems)
        self.nc.all_engine_barrier()



class Norm:

    def __init__(self, ph, per=1, name="norm"):
        self.stats = ph.sbs(f"{name}_stats", [P, T, 6])
        self.part = ph.sbs(f"{name}_part", [P, 5, T])
        self.deviation = ph.sbs(f"{name}_deviation", [P, T])
        self.scale = ph.sbs(f"{name}_scale", [P, T])
        self.shift = ph.sbs(f"{name}_shift", [P, T])
        self.step = ph.pair(f"{name}_step", per=6 * per)
        self.root = ph.pair(f"{name}_root", per=per)
        self.out = ph.pair(f"{name}_out", per=per)

    def vector_stats(self, dve, u, i, k, src, w=P):
        st, part, step = self.stats[u], self.part[u], self.step[u]
        for j in range(T):
            ins = dve.bn_stats(st[:w, j, :], src[:w, j, :])
        ins.then_inc(step.sem, 1)
        dve.wait_ge(*step.at(i, 6 * k + 1))
        dve.tensor_tensor(part[:w, 0, :], st[:w, :, 1], st[:w, :, 4], ALU.add)
        dve.tensor_tensor(part[:w, 1, :], st[:w, :, 1], st[:w, :, 4], ALU.subtract)
        dve.tensor_tensor(part[:w, 2, :], st[:w, :, 2], st[:w, :, 5], ALU.add).then_inc(step.sem, 1)
        dve.wait_ge(*step.at(i, 6 * k + 2))
        dve.scalar_tensor_tensor(out=part[:w, 3, :], in0=part[:w, 1, :], scalar=0.25,
                                 in1=part[:w, 1, :], op0=ALU.mult, op1=ALU.mult).then_inc(step.sem, 1)
        dve.wait_ge(*step.at(i, 6 * k + 3))
        dve.scalar_tensor_tensor(out=part[:w, 4, :], in0=part[:w, 2, :], scalar=1.0 / D,
                                 in1=part[:w, 3, :], op0=ALU.mult, op1=ALU.add).then_inc(step.sem, 1)

    def scalar_root(self, act, u, i, k, eps, w=P):
        act.wait_ge(*self.step[u].at(i, 6 * k + 4))
        act.activation(self.deviation[u][:w, :], self.part[u][:w, 4, :], ACT.Sqrt,
                       bias=eps[:w, :]).then_inc(self.root[u].sem, 1)

    def vector_scale(self, dve, u, i, k, w=P):
        step = self.step[u]
        dve.wait_ge(*self.root[u].at(i, k + 1))
        dve.reciprocal(self.scale[u][:w, :], self.deviation[u][:w, :]).then_inc(step.sem, 1)
        dve.wait_ge(*step.at(i, 6 * k + 5))
        dve.scalar_tensor_tensor(out=self.shift[u][:w, :], in0=self.part[u][:w, 0, :], scalar=-0.5,
                                 in1=self.scale[u][:w, :], op0=ALU.mult,
                                 op1=ALU.mult).then_inc(step.sem, 1)

    def scalar_apply(self, act, u, i, k, dst, src, w=P):
        act.wait_ge(*self.step[u].at(i, 6 * k + 6))
        for j in range(T):
            ins = act.activation(dst[:w, j, :], src[:w, j, :], ACT.Relu, bias=self.shift[u][:w, j:j + 1],
                                 scale=self.scale[u][:w, j:j + 1])
        ins.then_inc(self.out[u].sem, 1)



def turn_to_features(pe, bank, tokens, ident, w=P):
    for j in range(T):
        ins = pe.transpose(bank[:, j, :w], tokens[:w, j, :], ident[:w, :w])
    return ins


def turn_to_tokens(pe, bank, features, ident, w=P):
    for j in range(T):
        ins = pe.transpose(bank[:w, j, :], features[:, j, :w], ident[:, :])
    return ins


def product_features(pe, bank, weight, features, start=True, stop=True, w=P):
    return pe.matmul(bank[:, :, :w], weight, features[:, :, :w], start=start, stop=stop)


def product_tokens(pe, bank, features, weight, w=P):
    for j in range(T):
        ins = pe.matmul(bank[:w, j, :], features[:, j, :w], weight, start=True, stop=True)
    return ins


def sum_over_runs(pe, bank, tokens, same):
    for t in range(T):
        ins = pe.matmul(bank[:, t, :], tokens[:, t, :], same[:, 0, t, :], start=True, stop=True)
    return ins


def add_carry(dve, out, bank, same, carry, u, i):
    for n, t in enumerate(reversed(range(T))):
        if n:
            dve.wait_ge(*carry[u].at(i, n))
            col = out[u][:, t + 1, 0:1]
        elif u:
            dve.wait_ge(*carry[0].done(i))
            col = out[0][:, 0, 0:1]
        else:
            dve.wait_ge(*carry[1].before(i))
            col = out[1][:, 0, 0:1]
        dve.scalar_tensor_tensor(out=out[u][:, t, :], in0=same[:, 1, t, :], scalar=col,
                                 in1=bank[:, t, :], op0=ALU.mult, op1=ALU.add).then_inc(carry[u].sem, 1)


def down(i, u):
    return (NG + 1 - u) - 2 * i


def up(i, u):
    return 2 * i + (u - 2)


def group_of(dram, g):
    return dram[bass.ds(g, 1)].rearrange("o p f -> (o p) f")


def table_rows(table, g):
    return table[bass.ds(g * GROUP, GROUP), :].rearrange("(p j) d -> p (j d)", j=T)


def flat(x):
    return x.rearrange("p j d -> p (j d)")


def load_weights(eng, sem, what):
    for to, of in what:
        eng.dma_start(to, of).then_inc(sem, 16)
    return 16 * len(what)


def column(vector):
    return vector.rearrange("(p o) -> p o", o=1)


def over_partitions(vector, n=P):
    return vector.partition_broadcast(n)



def edge_structure(nc, w, s):
    ph = Phase(nc, "edges")
    cell = ph.sb("cell", [1, 32])
    one_col = ph.sb("ones", [P, P])
    row = ph.sbs("dst_row", [P, GROUP + 2], I32)
    col = ph.sbs("dst_col", [P, T], I32)
    rowf = ph.sbs("dst_rowf", [P, GROUP + 2])
    colf = ph.sbs("dst_colf", [P, T])
    same = ph.sbs("same", [P, 2, T, P])
    mask = ph.sbs("mask", [HEADS, 2, GROUP])
    differ = ph.sbs("differ", [HEADS, 2, GROUP])
    deg = ph.sbs("deg", [P, T, P])
    rec = ph.sbs("rec", [1, 2, GROUP])
    clip = ph.sbs("clip", [1, GROUP])
    root = ph.sbs("root", [1, GROUP])
    around = ph.sbs("around", [P, 3, T], I32)
    put = ph.sbs("put", [P, T], I32)
    hit = ph.sbs("hit", [P, T])
    slot_id = ph.sbs("slot_id", [P, T], I32)
    start_rows = ph.sb("start_rows", [N // 400, 400], I32)
    before = ph.sb("before", [P, P])
    spare = ph.sb("spare", [P, T], I32)
    source = ph.sbs("source", [P, GROUP], I32)
    source_col = ph.sbs("source_col", [P, T], I32)
    source_colf = ph.sbs("source_colf", [P, T])
    equal = ph.sbs("equal", [P, T, GROUP])
    equal_before = ph.sbs("equal_before", [P, T, P])
    repeated = ph.sbs("repeated", [P, T])
    to_spare = ph.sbs("to_spare", [P, T])
    offset = ph.sbs("offset", [P, T])
    add_row = ph.sbs("add_row", [P, T], I32)
    bank = ph.banks()
    source_in = ph.pair("source_in", per=2, unit=16)
    source_f = ph.pair("source_f")
    equal_made = ph.pair("equal_made", per=2, primed=True)
    repeats_mm = ph.pair("repeats_mm", primed=True)
    adds = ph.pair("adds", per=2, primed=True)
    adds_out = ph.pair("adds_out", unit=16, primed=True)
    spared = ph.pair("spared")

    ones_in = ph.sem("ones_in")
    row_in = ph.pair("row_in", per=2, unit=16)
    rows_f = ph.pair("rows_f", primed=True)
    same_made = ph.pair("same_made", primed=True)
    mask_made = ph.pair("mask_made", per=2)
    deg_mm = ph.pair("deg_mm")
    carry = ph.pair("deg_carry", per=T, primed=True)
    clipped = ph.pair("clipped")
    rooted = ph.pair("rooted")
    degs = ph.pair("degs")
    same_out = ph.pair("same_out", per=3, unit=16, primed=True)
    around_in = ph.pair("around_in", per=2, unit=16)
    hits = ph.pair("hits")
    puts = ph.pair("puts", primed=True)
    put_out = ph.pair("put_out", unit=16, primed=True, soft=True)
    slots_in = ph.pair("slots_in", per=4, unit=16, primed=True, soft=True)
    rows_made = ph.sem("rows_made")
    rows_out = ph.sem("rows_out")
    turns = ph.sem("scatter_turns")

    with nc.Block() as block:
        @block.sync
        def _(sp):
            ph.prime(sp, cell, w["ident"])
            sp.dma_start(one_col[:, :], w["ones"]).then_inc(ones_in, 16)
            sp.dma_start(before[:, :], w["before"]).then_inc(ones_in, 16)
            sp.dma_start(spare[:, :], w["spare_rows"]).then_inc(ones_in, 16)
            with sp.Fori(1, PAIRS + 1) as i:
                for u in range(2):
                    g = down(i, u)
                    sp.wait_ge(*rows_f[u].before(i))
                    ph.stand(sp)
                    sp.dma_start(row[u][:, :], over_partitions(s["dst_line"][bass.ds(g * GROUP, GROUP + 2)])
                                 ).then_inc(row_in[u].sem, 16)
                    sp.dma_start(col[u][:, :], group_of(s["dst_cols"], g)).then_inc(row_in[u].sem, 16)
                    sp.wait_ge(*puts[u].before(i))
                    ph.stand(sp)
                    sp.wait_ge(*slots_in[u].before(i))
                    ph.stand(sp)
                    sp.dma_start(around[u][:, 0:2, :], group_of(s["dst_around"], g)
                                 .rearrange("p (a j) -> p a j", a=2)).then_inc(around_in[u].sem, 16)
                    sp.dma_start(slot_id[u][:, :], group_of(s["slot_rows"], g)).then_inc(around_in[u].sem, 16)
                    sp.wait_ge(*adds[u].before(i))
                    ph.stand(sp)
                    sp.dma_start(source[u][:, :], over_partitions(s["src_line"][bass.ds(g * GROUP, GROUP)])
                                 ).then_inc(source_in[u].sem, 16)
                    sp.dma_start(source_col[u][:, :], group_of(s["src_cols"], g)).then_inc(source_in[u].sem, 16)

        @block.scalar
        def _(act):
            act.wait_ge(ones_in, 48)
            with act.Fori(1, PAIRS + 1) as i:
                for u in range(2):
                    act.wait_ge(*row_in[u].done(i))
                    act.wait_ge(*same_made[u].before(i))
                    act.activation(colf[u][:, :], col[u][:, :], ACT.Copy)
                    act.activation(rowf[u][:, :], row[u][:, :], ACT.Copy).then_inc(rows_f[u].sem, 1)
                    act.wait_ge(*source_in[u].done(i))
                    act.wait_ge(*equal_made[u].before(i))
                    act.activation(source_colf[u][:, :], source_col[u][:, :], ACT.Copy
                                   ).then_inc(source_f[u].sem, 1)
                for u in range(2):
                    act.wait_ge(*clipped[u].at(i))
                    act.activation(root[u][:, :], deg[u][0:1, :, :].rearrange("p j d -> p (j d)"), ACT.Sqrt,
                                   bias=one_col[0:1, 0:1]).then_inc(rooted[u].sem, 1)
                for u in range(2):
                    g = down(i, u)
                    act.wait_ge(*same_made[u].at(i))
                    act.dma_start(group_of(s["same"], g), same[u][:, :, :, :].rearrange("p a j d -> p (a j d)")
                                  ).then_inc(same_out[u].sem, 16)
                    act.wait_ge(*mask_made[u].at(i, 2))
                    act.dma_start(group_of(s["masks"], g), mask[u][:, :, :].rearrange("p a d -> p (a d)")
                                  ).then_inc(same_out[u].sem, 16)
                    act.wait_ge(*degs[u].at(i))
                    act.dma_start(group_of(s["degrees"], g), rec[u][:, :, :].rearrange("p a d -> p (a d)")
                                  ).then_inc(same_out[u].sem, 16)
                    act.wait_ge(*adds[u].done(i))
                    act.dma_start(group_of(s["add_rows"], g), add_row[u][:, :]).then_inc(adds_out[u].sem, 16)
            for u in range(2):
                act.wait_ge(*same_out[u].done(PAIRS))
                act.wait_ge(*adds_out[u].done(PAIRS))

        @block.tensor
        def _(pe):
            pe.wait_ge(ones_in, 48)
            with pe.Fori(1, PAIRS + 1) as i:
                for u in range(2):
                    pe.wait_ge(*same_made[u].at(i))
                    product_features(pe, bank[u][0], one_col[:, :], same[u][:, 0, :, :]
                                     ).then_inc(deg_mm[u].sem, 1)
                for u in range(2):
                    pe.wait_ge(*equal_made[u].done(i))
                    for t in range(T):
                        for a in range(t):
                            pe.matmul(bank[u][1][:, t, 0:1], equal[u][:, a, t * P:(t + 1) * P],
                                      one_col[:, 0:1], start=(a == 0), stop=False)
                        ins = pe.matmul(bank[u][1][:, t, 0:1], equal_before[u][:, t, :], one_col[:, 0:1],
                                        start=(t == 0), stop=True)
                    ins.then_inc(repeats_mm[u].sem, 1)

        @block.vector
        def _(dve):
            dve.memset(deg[1][:, :, :], 0.0).then_inc(rows_made, 1)
            dve.wait_ge(rows_made, 1)
            dve.wait_ge(ones_in, 48)
            with dve.Fori(1, PAIRS + 1) as i:
                for u in range(2):
                    dve.wait_ge(*rows_f[u].at(i))
                    dve.wait_ge(*same_out[u].before(i))
                    for t in range(T):
                        line = rowf[u][:, 1 + t * P:1 + (t + 1) * P]
                        nxt = 1 + (t + 1) * P
                        dve.tensor_scalar(same[u][:, 0, t, :], line, colf[u][:, t:t + 1], None, ALU.is_equal)
                        dve.tensor_scalar(same[u][:, 1, t, :], line, rowf[u][:, nxt:nxt + 1], None,
                                          ALU.is_equal)
                    at = rowf[u][0:HEADS, 1:GROUP + 1]
                    dve.tensor_tensor(differ[u][:, 0, :], at, rowf[u][0:HEADS, 0:GROUP], ALU.not_equal)
                    dve.tensor_tensor(differ[u][:, 1, :], at, rowf[u][0:HEADS, 2:GROUP + 2],
                                      ALU.not_equal).then_inc(same_made[u].sem, 1)
                    dve.wait_ge(*same_made[u].at(i))
                    dve.tensor_scalar(mask[u][:, 0, :], differ[u][:, 0, :], -FAR, None, ALU.mult
                                      ).then_inc(mask_made[u].sem, 1)
                    dve.tensor_scalar(mask[u][:, 1, :], differ[u][:, 1, :], -FAR, None, ALU.mult
                                      ).then_inc(mask_made[u].sem, 1)
                    dve.wait_ge(*around_in[u].done(i))
                    dve.wait_ge(*put_out[u].before(i))
                    dve.tensor_tensor(hit[u][:, :], around[u][:, 0, :], around[u][:, 1, :],
                                      ALU.is_equal).then_inc(hits[u].sem, 1)
                    dve.wait_ge(*hits[u].at(i))
                    dve.scalar_tensor_tensor(out=put[u][:, :], in0=hit[u][:, :], scalar=NO_ROW,
                                             in1=around[u][:, 0, :], op0=ALU.mult, op1=ALU.add
                                             ).then_inc(puts[u].sem, 1)
                    dve.wait_ge(*source_f[u].at(i))
                    dve.wait_ge(*repeats_mm[u].before(i))
                    for a in range(T):
                        ins = dve.tensor_scalar(equal[u][:, a, :], source[u][:, :], source_colf[u][:, a:a + 1],
                                                None, ALU.is_equal)
                    ins.then_inc(equal_made[u].sem, 1)
                    dve.wait_ge(*equal_made[u].at(i, 1))
                    for a in range(T):
                        ins = dve.tensor_tensor(equal_before[u][:, a, :], equal[u][:, a, a * P:(a + 1) * P],
                                                before[:, :], ALU.mult)
                    ins.then_inc(equal_made[u].sem, 1)
                for u in range(2):
                    dve.wait_ge(*repeats_mm[u].at(i))
                    dve.wait_ge(*adds_out[u].before(i))
                    dve.tensor_scalar(repeated[u][:, :], bank[u][1][:, :, 0], 0.0, None, ALU.is_gt)
                    dve.tensor_tensor(to_spare[u][:, :], spare[:, :], source_col[u][:, :], ALU.subtract
                                      ).then_inc(adds[u].sem, 1)
                for u in range(2):
                    dve.wait_ge(*deg_mm[u].at(i))
                    add_carry(dve, deg, bank[u][0], same[u], carry, u, i)
                    dve.wait_ge(*carry[u].done(i))
                    dve.tensor_scalar(clip[u][:, :], deg[u][0:1, :, :].rearrange("p j d -> p (j d)"), 1.0,
                                      None, ALU.max).then_inc(clipped[u].sem, 1)
                for u in range(2):
                    dve.wait_ge(*clipped[u].at(i))
                    dve.reciprocal(rec[u][:, 0, :], clip[u][:, :])
                    dve.wait_ge(*rooted[u].at(i))
                    dve.reciprocal(rec[u][:, 1, :], root[u][:, :]).then_inc(degs[u].sem, 1)
                for u in range(2):
                    dve.wait_ge(*adds[u].at(i, 1))
                    dve.tensor_tensor(offset[u][:, :], repeated[u][:, :], to_spare[u][:, :],
                                      ALU.mult).then_inc(spared[u].sem, 1)
                for u in range(2):
                    dve.wait_ge(*spared[u].at(i))
                    dve.tensor_tensor(add_row[u][:, :], offset[u][:, :], source_col[u][:, :],
                                      ALU.add).then_inc(adds[u].sem, 1)

        @block.gpsimd
        def _(pl):
            ph.prime(pl, cell, w["ident"], soft=True)
            pl.iota(start_rows[:, :], pattern=[[1, 400]], base=SLOTS, channel_multiplier=400
                    ).then_inc(rows_out, 1)
            pl.wait_ge(rows_out, 1)
            pl.dma_start(s["row_of_node"].rearrange("(p f) o -> p (f o)", p=N // 400), start_rows[:, :]
                         ).then_inc(turns, 16)
            pl.wait_ge(turns, 16)
            with pl.Fori(1, PAIRS + 1) as i:
                for u in range(2):
                    g = down(i, u)
                    pl.wait_ge(*puts[u].at(i))
                    ph.stand(pl)
                    pl.dma_start(group_of(s["put_rows"], g), put[u][:, :]).then_inc(put_out[u].sem, 16)
                    for t in range(T):
                        pl.indirect_dma_start(
                            s["row_of_node"], bass.IndirectOffsetOnAxis(ap=put[u][:, t:t + 1], axis=0),
                            slot_id[u][:, t:t + 1], None, bounds_check=N - 1, oob_is_err=False
                        ).then_inc(slots_in[u].sem, 16)
            for u in range(2):
                pl.wait_ge(*slots_in[u].done(PAIRS))
                pl.wait_ge(*put_out[u].done(PAIRS))
    ph.end()



def dense_chain(nc, x, out, w, s):
    ph = Phase(nc, "dense")
    cell = ph.sb("cell", [1, 32])
    ident = ph.sb("ident", [P, P])
    eps = ph.sb("eps", [P, 1])
    ws0, ws1, w1, w2 = (ph.sb(n, [P, D]) for n in ("ws0", "ws1", "w1", "w2"))
    w_self = ph.sb("w_self", [P, D])
    wr0 = ph.sb("wr0", [P, 2, D])
    w_lr = ph.sb("w_lr", [P, 2, 2 * D])
    b_s0, b_1 = ph.sb("b_s0", [P, 1]), ph.sb("b_1", [P, 1])
    b_l0 = ph.sb("b_l0", [P, 2])
    b_s1, b_l1, b_2 = (ph.sb(n, [P, D]) for n in ("b_s1", "b_l1", "b_2"))
    rate_row = ph.sb("rate_row", [P, D])
    x_in = ph.sbs("x_in", [P, T, D])
    xb = ph.sbs("xb", [P, T, D])
    xr = ph.sbs("xr", [P, T, D])
    h = ph.sbs("h", [P, T, D])
    h_f = ph.sbs("h_f", [P, T, P])
    g_f = ph.sbs("g_f", [P, T, P])
    g3_f = [[ph.sb(f"g3_f{u}{k}", [P, T, P]) for k in range(2)] for u in range(2)]
    tab = {n: ph.sbs(f"tab{n}", [P, T, D]) for n in range(1, 8)}
    bank = ph.banks()
    norm = Norm(ph, 4)

    weights_in = ph.sem("weights_in")
    eps_set = ph.sem("eps_set")
    rate_steps = ph.sem("rate_steps")
    rates_set = ph.sem("rates_set")
    x_loaded = ph.pair("x_loaded", unit=16)
    x_free = ph.pair("x_free", primed=True)
    turned = ph.pair("turned", per=4)
    h_ready = ph.pair("h_ready", per=4)
    g1_mm, g1_ready = ph.pair("g1_mm"), ph.pair("g1_ready")
    xb_ready = ph.pair("xb_ready", per=2)
    x1_mm = ph.pair("x1_mm")
    x_ready = ph.pair("x_ready", per=3)
    t1_turned, t1_ready = ph.pair("t1_turned"), ph.pair("t1_ready")
    g3_mm, g3_ready = ph.pair("g3_mm", per=2), ph.pair("g3_ready", per=2)
    lr_mm, t3_ready = ph.pair("lr_mm", per=2), ph.pair("t3_ready")
    w1_mm, t4_ready = ph.pair("w1_mm", per=2), ph.pair("t4_ready")
    g5_ready = ph.pair("g5_ready")
    w2_mm, t5_ready = ph.pair("w2_mm"), ph.pair("t5_ready")
    self_mm, out_ready = ph.pair("self_mm"), ph.pair("out_ready")
    stored = {n: ph.pair(f"stored{n}", unit=16, primed=True) for n in (1, 2, 3, 4, 5, 7)}

    idx = ph.sbs("idx", [P, 2, T], I32)
    found = ph.sbs("found", [P, 2, T], I32)
    ends = [[ph.sb(f"ends{u}{k}", [P, T, D]) for k in range(2)] for u in range(2)]
    idx_in = ph.pair("idx_in", unit=16)
    gathered = ph.pair("gathered", per=4 * T, unit=16)
    ends_out = ph.pair("ends_out", per=3, unit=16, primed=True, soft=True)

    cw = {}
    WHAT = [(ident[:, :], w["ident"]), (ws0[:, :], w["s_w0"]), (ws1[:, :], w["s_w1"]), (w1[:, :], w["W1"]),
            (w2[:, :], w["W2"][0:D, :]), (w_self[:, :], w["w_self"]),
            (wr0[:, :, :].rearrange("p k d -> p (k d)"), w["Wr0"]),
            (w_lr[:, :, 0:D], w["Wl1"].rearrange("(k p) d -> p k d", p=P)),
            (w_lr[:, :, D:2 * D], w["Wr1"].rearrange("(k p) d -> p k d", p=P)),
            (b_s0[:, :], column(w["s_b0"])), (b_1[:, :], column(w["b1"])),
            (b_l0[:, 0:1], column(w["bl0"][0:D])), (b_l0[:, 1:2], column(w["bl0"][D:2 * D])),
            (b_s1[:, :], over_partitions(w["s_b1"])), (b_l1[:, :], over_partitions(w["bl1"])),
            (b_2[:, :], over_partitions(w["b2"]))]
    loaded = 16 * (len(WHAT) + 1)
    rate_mm = rate_row_steps(nc, ph, w, bank[0][0], weights_in, rate_steps)

    def rows(array, i, u, wd, base=0):
        return array[bass.ds(i * (2 * GROUP) + (base + u * GROUP - 2 * GROUP), T * wd), :] \
            .rearrange("(p j) d -> p (j d)", j=T)

    def widths(i):
        return (P, NODE_TAIL) if isinstance(i, int) and i == NODE_TURNS else (P, P)

    def looped(eng, body):
        with eng.Fori(1, NODE_TURNS - 1) as i:
            body(i, widths(i), widths(i))
        body(NODE_TURNS - 1, widths(NODE_TURNS - 1), widths(NODE_TURNS))
        body(NODE_TURNS, widths(NODE_TURNS), None)

    with nc.Block() as block:
        @block.sync
        def _(sp):
            ph.prime(sp, cell, w["ident"])
            load_weights(sp, weights_in, WHAT)
            rate_mm["load"](sp)

            def load_x(i, u, wd):
                sp.wait_ge(*x_free[u].before(i))
                sp.dma_start(flat(x_in[u][:wd, :, :]), rows(x, i, u, wd)).then_inc(x_loaded[u].sem, 16)

            def store(n, ready, i, u, wd):
                sp.wait_ge(*ready)
                to = rows(out, i, u, wd) if n == 7 else rows(s["table"][n], i, u, wd, base=SLOTS)
                sp.dma_start(to, flat(tab[n][u][:wd, :, :])).then_inc(stored[n][u].sem, 16)

            def body(i, wd, next_wd):
                for u in range(2):
                    store(1, t1_ready[u].at(i), i, u, wd[u])
                if next_wd:
                    for u in range(2):
                        load_x(i + 1, u, next_wd[u])
                for n, ready in ((2, lambda u: norm.out[u].at(i, 2)), (3, lambda u: t3_ready[u].at(i)),
                                 (4, lambda u: t4_ready[u].at(i)), (5, lambda u: t5_ready[u].at(i)),
                                 (7, lambda u: out_ready[u].at(i))):
                    for u in range(2):
                        store(n, ready(u), i, u, wd[u])

            for u in range(2):
                load_x(1, u, P)
            looped(sp, body)
            for n in stored:
                for u in range(2):
                    sp.wait_ge(*stored[n][u].done(NODE_TURNS))

        @block.tensor
        def _(pe):
            pe.wait_ge(weights_in, loaded)
            rate_mm["tensor"](pe)
            pe.wait_ge(rates_set, 1)

            def body(i, wd, _):
                for u in range(2):
                    pe.wait_ge(*norm.out[u].at(i, 1))
                    turn_to_features(pe, bank[u][0], h[u], ident, wd[u]).then_inc(turned[u].sem, 1)
                for u in range(2):
                    pe.wait_ge(*h_ready[u].at(i, 1))
                    product_features(pe, bank[u][1], ws0[:, :], h_f[u], w=wd[u]).then_inc(g1_mm[u].sem, 1)
                for u in range(2):
                    pe.wait_ge(*g1_ready[u].at(i))
                    product_tokens(pe, bank[u][3], g_f[u], ws1[:, :], wd[u]).then_inc(x1_mm[u].sem, 1)
                    turn_to_tokens(pe, bank[u][2], g_f[u], ident, wd[u]).then_inc(t1_turned[u].sem, 1)
                for u in range(2):
                    pe.wait_ge(*norm.out[u].at(i, 2))
                    turn_to_features(pe, bank[u][0], tab[2][u], ident, wd[u]).then_inc(turned[u].sem, 1)
                for u in range(2):
                    pe.wait_ge(*h_ready[u].at(i, 2))
                    pe.wait_ge(*t1_ready[u].at(i))
                    for k in range(2):
                        product_features(pe, bank[u][1 + k], wr0[:, k, :], h_f[u], w=wd[u]
                                         ).then_inc(g3_mm[u].sem, 1)
                for u in range(2):
                    pe.wait_ge(*g3_ready[u].at(i, 2))
                    for b, side in ((3, 1), (0, 0)):
                        for j in range(T):
                            for k in range(2):
                                ins = pe.matmul(bank[u][b][:wd[u], j, :], g3_f[u][k][:, j, :wd[u]],
                                                w_lr[:, k, side * D:(side + 1) * D], start=(k == 0),
                                                stop=(k == 1))
                        ins.then_inc(lr_mm[u].sem, 1)
                for u in range(2):
                    pe.wait_ge(*norm.out[u].at(i, 3))
                    turn_to_features(pe, bank[u][1], h[u], ident, wd[u]).then_inc(turned[u].sem, 1)
                for u in range(2):
                    pe.wait_ge(*h_ready[u].at(i, 3))
                    product_features(pe, bank[u][0], w1[:, :], h_f[u], w=wd[u]).then_inc(w1_mm[u].sem, 1)
                    product_tokens(pe, bank[u][2], h_f[u], w1[:, :], wd[u]).then_inc(w1_mm[u].sem, 1)
                for u in range(2):
                    pe.wait_ge(*g5_ready[u].at(i))
                    product_tokens(pe, bank[u][3], g_f[u], w2[:, :], wd[u]).then_inc(w2_mm[u].sem, 1)
                for u in range(2):
                    pe.wait_ge(*norm.out[u].at(i, 4))
                    turn_to_features(pe, bank[u][1], tab[6][u], ident, wd[u]).then_inc(turned[u].sem, 1)
                for u in range(2):
                    pe.wait_ge(*h_ready[u].at(i, 4))
                    pe.wait_ge(*t4_ready[u].at(i))
                    product_tokens(pe, bank[u][2], h_f[u], w_self[:, :], wd[u]).then_inc(self_mm[u].sem, 1)

            looped(pe, body)

        @block.scalar
        def _(act):
            act.wait_ge(eps_set, 1)
            act.wait_ge(weights_in, loaded)

            def body(i, wd, _):
                def relu(to, of, bias, wd):
                    return act.activation(to[:, :, :wd], of[:, :, :wd], ACT.Relu, bias=bias)

                for u in range(2):
                    norm.scalar_root(act, u, i, 0, eps, wd[u])
                for u in range(2):
                    norm.scalar_apply(act, u, i, 0, h[u], x_in[u], wd[u])
                for u in range(2):
                    act.wait_ge(*g1_mm[u].at(i))
                    relu(g_f[u], bank[u][1], b_s0[:, :], wd[u]).then_inc(g1_ready[u].sem, 1)
                for u in range(2):
                    norm.scalar_root(act, u, i, 1, eps, wd[u])
                for u in range(2):
                    act.wait_ge(*stored[2][u].before(i))
                    norm.scalar_apply(act, u, i, 1, tab[2][u], xr[u], wd[u])
                for u in range(2):
                    for k in range(2):
                        act.wait_ge(*g3_mm[u].at(i, k + 1))
                        relu(g3_f[u][k], bank[u][1 + k], b_l0[:, k:k + 1], wd[u]
                             ).then_inc(g3_ready[u].sem, 1)
                for u in range(2):
                    act.wait_ge(*lr_mm[u].at(i, 2))
                    act.wait_ge(*stored[3][u].before(i))
                    act.activation(flat(tab[3][u][:wd[u], :, :]), flat(bank[u][0][:wd[u], :, :]),
                                   ACT.Copy).then_inc(t3_ready[u].sem, 1)
                    norm.scalar_root(act, u, i, 2, eps, wd[u])
                for u in range(2):
                    norm.scalar_apply(act, u, i, 2, h[u], xr[u], wd[u])
                for u in range(2):
                    act.wait_ge(*w1_mm[u].at(i, 1))
                    relu(g_f[u], bank[u][0], b_1[:, :], wd[u]).then_inc(g5_ready[u].sem, 1)
                    act.wait_ge(*w1_mm[u].at(i, 2))
                    act.wait_ge(*stored[4][u].before(i))
                    act.activation(flat(tab[4][u][:wd[u], :, :]), flat(bank[u][2][:wd[u], :, :]),
                                   ACT.Copy).then_inc(t4_ready[u].sem, 1)
                for u in range(2):
                    norm.scalar_root(act, u, i, 3, eps, wd[u])
                for u in range(2):
                    norm.scalar_apply(act, u, i, 3, tab[6][u], xr[u], wd[u])

            looped(act, body)

        @block.vector
        def _(dve):
            dve.memset(eps[:, :], EPS).then_inc(eps_set, 1)
            dve.wait_ge(weights_in, loaded)
            rate_mm["vector"](dve, rate_row, rates_set)
            dve.wait_ge(rates_set, 1)

            def body(i, wd, _):
                def over_tiles(row, wd):
                    return row[:wd, :].rearrange("p (o d) -> p o d", o=1).to_broadcast((wd, T, D))

                def add(to, a, b, wd):
                    return dve.tensor_tensor(to[:wd, :, :], a, b, ALU.add)

                def to_features(k, b):
                    for u in range(2):
                        dve.wait_ge(*turned[u].at(i, k + 1))
                        dve.tensor_copy(h_f[u][:, :, :wd[u]], bank[u][b][:, :, :wd[u]]
                                        ).then_inc(h_ready[u].sem, 1)

                def norms(k, src):
                    for u in range(2):
                        norm.vector_stats(dve, u, i, k, src[u], wd[u])
                    for u in range(2):
                        norm.vector_scale(dve, u, i, k, wd[u])

                for u in range(2):
                    dve.wait_ge(*x_loaded[u].at(i))
                norms(0, x_in)
                to_features(0, 0)
                for u in range(2):
                    add(xb[u], x_in[u][:wd[u], :, :], over_tiles(b_s1, wd[u]), wd[u]
                        ).then_inc(x_free[u].sem, 1)
                for u in range(2):
                    dve.wait_ge(*x1_mm[u].at(i))
                    dve.wait_ge(*x_free[u].at(i))
                    add(xr[u], bank[u][3][:wd[u], :, :], xb[u][:wd[u], :, :], wd[u]
                        ).then_inc(x_ready[u].sem, 1)
                for u in range(2):
                    dve.wait_ge(*x_ready[u].at(i, 1))
                norms(1, xr)
                for u in range(2):
                    dve.wait_ge(*t1_turned[u].at(i))
                    dve.wait_ge(*stored[1][u].before(i))
                    dve.tensor_copy(flat(tab[1][u][:wd[u], :, :]), flat(bank[u][2][:wd[u], :, :])
                                    ).then_inc(t1_ready[u].sem, 1)
                to_features(1, 0)
                for u in range(2):
                    add(xb[u], xr[u][:wd[u], :, :], over_tiles(b_l1, wd[u]), wd[u]
                        ).then_inc(xb_ready[u].sem, 1)
                for u in range(2):
                    dve.wait_ge(*lr_mm[u].at(i, 1))
                    dve.wait_ge(*xb_ready[u].at(i, 1))
                    add(xr[u], bank[u][3][:wd[u], :, :], xb[u][:wd[u], :, :], wd[u]
                        ).then_inc(x_ready[u].sem, 1)
                for u in range(2):
                    dve.wait_ge(*x_ready[u].at(i, 2))
                norms(2, xr)
                to_features(2, 1)
                for u in range(2):
                    add(xb[u], xr[u][:wd[u], :, :], over_tiles(b_2, wd[u]), wd[u]
                        ).then_inc(xb_ready[u].sem, 1)
                for u in range(2):
                    dve.wait_ge(*w2_mm[u].at(i))
                    dve.wait_ge(*stored[5][u].before(i))
                    add(tab[5][u], bank[u][3][:wd[u], :, :], over_tiles(rate_row, wd[u]), wd[u]
                        ).then_inc(t5_ready[u].sem, 1)
                for u in range(2):
                    dve.wait_ge(*t5_ready[u].at(i))
                    dve.wait_ge(*xb_ready[u].at(i, 2))
                    add(xr[u], tab[5][u][:wd[u], :, :], xb[u][:wd[u], :, :], wd[u]
                        ).then_inc(x_ready[u].sem, 1)
                for u in range(2):
                    dve.wait_ge(*x_ready[u].at(i, 3))
                norms(3, xr)
                to_features(3, 1)
                for u in range(2):
                    dve.wait_ge(*self_mm[u].at(i))
                    dve.wait_ge(*stored[7][u].before(i))
                    add(tab[7][u], bank[u][2][:wd[u], :, :], xr[u][:wd[u], :, :], wd[u]
                        ).then_inc(out_ready[u].sem, 1)

            looped(dve, body)

        @block.gpsimd
        def _(pl):
            ph.prime(pl, cell, w["ident"], soft=True)
            def load_indices(i, u):
                g = up(i, u)
                pl.dma_start(idx[u][:, :, :].rearrange("p a j -> p (a j)"), group_of(s["edge_ends"], g)
                             ).then_inc(idx_in[u].sem, 16)

            for u in range(2):
                load_indices(1, u)

            def body(i, more):
                for u in range(2):
                    pl.wait_ge(*idx_in[u].at(i))
                    pl.wait_ge(*ends_out[u].before(i))
                    ph.stand(pl)
                    for t in range(T):
                        for to, of, k in ((found[u][:, 0, t:t + 1], s["row_of_node"], 0),
                                          (found[u][:, 1, t:t + 1], s["row_of_node"], 1),
                                          (ends[u][0][:, t, :], x, 0), (ends[u][1][:, t, :], x, 1)):
                            pl.indirect_dma_start(to, None, of, bass.IndirectOffsetOnAxis(
                                ap=idx[u][:, k, t:t + 1], axis=0)).then_inc(gathered[u].sem, 16)
                for u in range(2):
                    g = up(i, u)
                    pl.wait_ge(*gathered[u].done(i))
                    ph.stand(pl)
                    pl.dma_start(group_of(s["end_rows"], g), found[u][:, :, :].rearrange("p a j -> p (a j)")
                                 ).then_inc(ends_out[u].sem, 16)
                    for k in range(2):
                        pl.dma_start(group_of(s["x_ends"][k], g), flat(ends[u][k][:, :, :])
                                     ).then_inc(ends_out[u].sem, 16)
                    if more:
                        load_indices(i + 1, u)

            with pl.Fori(1, PAIRS) as i:
                body(i, True)
            body(PAIRS, False)
            for u in range(2):
                pl.wait_ge(*ends_out[u].done(PAIRS))
    ph.end()


def rate_row_steps(nc, ph, w, bank, weights_in, steps):
    rates = ph.sb("rates", [REL, 1])
    e1w, e1b = ph.sb("e1w", [REL, 64]), ph.sb("e1b", [64, 1])
    e2w, e2b = ph.sb("e2w", [64, D]), ph.sb("e2b", [P, 1])
    w2b = ph.sb("w2b", [P, D])
    hidden, r_col, r_mat = ph.sb("rate_hidden", [64, 1]), ph.sb("r_col", [P, 1]), ph.sb("r_mat", [P, P])
    what = [(rates[:, :], column(w["rates"])), (e1w[:, :], w["e1_w"]), (e1b[:, :], column(w["e1_b"])),
            (e2w[:, :], w["e2_w"]), (e2b[:, :], column(w["e2_b"])), (w2b[:, :], w["W2"][D:2 * D, :])]
    rates_in = ph.sem("rates_in")

    def load(sp):
        load_weights(sp, rates_in, what)
        sp.wait_ge(rates_in, 16 * len(what))
        ph.stand(sp)
        sp.dma_start(ph_cell[:, :], w["ident"][0:1, 0:1]).then_inc(weights_in, 16)

    ph_cell = ph.sb("rates_cell", [1, 1])

    def tensor(pe):
        pe.matmul(bank[0:64, 0, 0:1], e1w[:, :], rates[:, :], start=True, stop=True).then_inc(steps, 1)
        pe.wait_ge(steps, 3)
        pe.matmul(bank[:, 1, 0:1], e2w[:, :], hidden[:, :], start=True, stop=True).then_inc(steps, 1)
        pe.wait_ge(steps, 6)
        pe.matmul(bank[:, 3, :], r_mat[:, :], w2b[:, :], start=True, stop=True)
        pe.matmul(bank[:, 2, 0:1], w2b[:, :], r_col[:, :], start=True, stop=True).then_inc(steps, 1)

    def vector(dve, row, done, col=None):
        dve.wait_ge(steps, 1)
        dve.tensor_scalar(hidden[:, :], bank[0:64, 0, 0:1], e1b[:, :], None, ALU.add).then_inc(steps, 1)
        dve.wait_ge(steps, 2)
        dve.tensor_scalar(hidden[:, :], hidden[:, :], 0.0, None, ALU.max).then_inc(steps, 1)
        dve.wait_ge(steps, 4)
        dve.tensor_scalar(r_col[:, :], bank[:, 1, 0:1], e2b[:, :], None, ALU.add).then_inc(steps, 1)
        dve.wait_ge(steps, 5)
        dve.tensor_copy(r_mat[:, :], r_col[:, :].to_broadcast((P, P))).then_inc(steps, 1)
        dve.wait_ge(steps, 7)
        if row is not None:
            dve.tensor_copy(row[:, :], bank[:, 3, :]).then_inc(done, 1)
        else:
            dve.tensor_copy(col[:, :], bank[:, 2, 0:1]).then_inc(done, 1)

    return {"load": load, "tensor": tensor, "vector": vector}



def attend_edges(nc, w, s, level):
    first = level == 0
    ph = Phase(nc, f"logits{level}")
    cell = ph.sb("cell", [1, 32])
    ident = ph.sb("ident", [P, P])
    eps = ph.sb("eps", [P, 1])
    wq, wk, wv, b_v = (ph.sb(n, [P, D]) for n in ("wq", "wk", "wv", "b_v"))
    head_sum = ph.sb("head_sum", [P, HEADS])
    b_q, b_k = ph.sb("b_q", [P, 1]), ph.sb("b_k", [P, 1])
    src = ph.sbs("src", [P, T, D])
    dst = ph.sbs("dst", [P, T, D])
    h_src, h_dst = (ph.sbs(n, [P, T, D]) for n in ("h_src", "h_dst"))
    src_f, dst_f, x_f = (ph.sbs(n, [P, T, P]) for n in ("src_f", "dst_f", "x_f"))
    q_f, qk_f, value = (ph.sbs(n, [P, T, P]) for n in ("q_f", "qk_f", "value"))
    mask = ph.sbs("mask", [HEADS, 2, GROUP])
    logit = ph.sbs("logit", [HEADS, 2, GROUP])
    idx = ph.sbs("idx", [P, 2, T], I32)
    bank = ph.banks()
    norm_src, norm_dst = (Norm(ph, 1, f"norm_{n}") for n in ("src", "dst")) if first else (None, None)

    weights_in, eps_set, runs_set = ph.sem("weights_in"), ph.sem("eps_set"), ph.sem("runs_set")
    src_in = ph.pair("src_in", per=1 if first else T, unit=16, soft=not first)
    dst_in = ph.pair("dst_in", per=1 if first else T, unit=16, soft=not first)
    mask_in = ph.pair("mask_in", unit=16)
    idx_in = ph.pair("idx_in", unit=16)
    turned = ph.pair("turned", per=3 if first else 2, primed=True)
    src_ready = ph.pair("src_ready")
    dst_ready = ph.pair("dst_ready", per=2 if first else 1)
    q_mm, k_mm, v_mm = ph.pair("q_mm"), ph.pair("k_mm"), ph.pair("v_mm")
    q_ready, qk_ready, v_ready = ph.pair("q_ready"), ph.pair("qk_ready"), ph.pair("v_ready", primed=True)
    logit_mm, logit_ready = ph.pair("logit_mm"), ph.pair("logit_ready")
    running = ph.pair("running", primed=True)
    stored = ph.pair("stored", per=4 if first else 2, unit=16, primed=True)
    WHAT = [(ident[:, :], w["ident"]), (wq[:, :], w[f"q_w{level}"]), (wk[:, :], w[f"k_w{level}"]),
            (wv[:, :], w[f"v_w{level}"]), (b_v[:, :], over_partitions(w[f"v_b{level}"])),
            (head_sum[:, :], w["head_sum"]), (b_q[:, :], column(w[f"q_b{level}"])),
            (b_k[:, :], column(w[f"k_b{level}"]))]
    loaded = 16 * len(WHAT)

    with nc.Block() as block:
        @block.sync
        def _(sp):
            ph.prime(sp, cell, w["ident"])
            load_weights(sp, weights_in, WHAT)
            with sp.Fori(1, PAIRS + 1) as i:
                for u in range(2):
                    g = up(i, u)
                    sp.wait_ge(*running[u].before(i))
                    ph.stand(sp)
                    sp.dma_start(mask[u][:, :, :].rearrange("p a d -> p (a d)"), group_of(s["masks"], g)
                                 ).then_inc(mask_in[u].sem, 16)
                    if first:
                        sp.wait_ge(*turned[u].before(i))
                        ph.stand(sp)
                        sp.dma_start(flat(src[u][:, :, :]), group_of(s["x_ends"][0], g)
                                     ).then_inc(src_in[u].sem, 16)
                        sp.dma_start(flat(dst[u][:, :, :]), group_of(s["x_ends"][1], g)
                                     ).then_inc(dst_in[u].sem, 16)
                    else:
                        sp.wait_ge(*turned[u].before(i))
                        ph.stand(sp)
                        sp.dma_start(idx[u][:, :, :].rearrange("p a j -> p (a j)"), group_of(s["end_rows"], g)
                                     ).then_inc(idx_in[u].sem, 16)

        if not first:
            @block.gpsimd
            def _(pl):
                ph.prime(pl, cell, w["ident"], soft=True)
                with pl.Fori(1, PAIRS + 1) as i:
                    for u in range(2):
                        pl.wait_ge(*idx_in[u].at(i))
                        pl.wait_ge(*turned[u].before(i))
                        ph.stand(pl)
                        for end, (rows, rows_in) in enumerate(((src, src_in), (dst, dst_in))):
                            for t in range(T):
                                pl.indirect_dma_start(
                                    rows[u][:, t, :], None, s["table"][1],
                                    bass.IndirectOffsetOnAxis(ap=idx[u][:, end, t:t + 1], axis=0)
                                ).then_inc(rows_in[u].sem, 16)

        @block.tensor
        def _(pe):
            pe.wait_ge(weights_in, loaded)
            with pe.Fori(1, PAIRS + 1) as i:
                for u in range(2):
                    if first:
                        pe.wait_ge(*norm_src.out[u].at(i))
                        turn_to_features(pe, bank[u][0], h_src[u], ident).then_inc(turned[u].sem, 1)
                        pe.wait_ge(*norm_dst.out[u].at(i))
                        turn_to_features(pe, bank[u][1], h_dst[u], ident).then_inc(turned[u].sem, 1)
                        turn_to_features(pe, bank[u][2], dst[u], ident).then_inc(turned[u].sem, 1)
                    else:
                        pe.wait_ge(*src_in[u].done(i))
                        pe.wait_ge(*v_ready[u].before(i))
                        turn_to_features(pe, bank[u][0], src[u], ident).then_inc(turned[u].sem, 1)
                        pe.wait_ge(*dst_in[u].done(i))
                        turn_to_features(pe, bank[u][1], dst[u], ident).then_inc(turned[u].sem, 1)
                for u in range(2):
                    pe.wait_ge(*dst_ready[u].done(i))
                    product_features(pe, bank[u][1], wq[:, :], dst_f[u]).then_inc(q_mm[u].sem, 1)
                    pe.wait_ge(*src_ready[u].at(i))
                    product_features(pe, bank[u][3], wk[:, :], src_f[u]).then_inc(k_mm[u].sem, 1)
                    product_tokens(pe, bank[u][0], src_f[u], wv[:, :]).then_inc(v_mm[u].sem, 1)
                for u in range(2):
                    pe.wait_ge(*qk_ready[u].at(i))
                    pe.matmul(bank[u][2][0:HEADS, :, :], head_sum[:, :], qk_f[u][:, :, :], start=True,
                              stop=True).then_inc(logit_mm[u].sem, 1)

        @block.scalar
        def _(act):
            act.wait_ge(weights_in, loaded)
            act.wait_ge(eps_set, 1)
            with act.Fori(1, PAIRS + 1) as i:
                if first:
                    for u in range(2):
                        norm_src.scalar_root(act, u, i, 0, eps)
                        norm_dst.scalar_root(act, u, i, 0, eps)
                    for u in range(2):
                        norm_src.scalar_apply(act, u, i, 0, h_src[u], src[u])
                        norm_dst.scalar_apply(act, u, i, 0, h_dst[u], dst[u])
                    for u in range(2):
                        act.wait_ge(*stored[u].before(i))
                        act.wait_ge(*turned[u].at(i, 2))
                        act.activation(flat(dst_f[u][:, :, :]), flat(bank[u][1][:, :, :]), ACT.Copy
                                       ).then_inc(dst_ready[u].sem, 1)
                        act.wait_ge(*turned[u].at(i, 3))
                        act.activation(flat(x_f[u][:, :, :]), flat(bank[u][2][:, :, :]), ACT.Copy
                                       ).then_inc(dst_ready[u].sem, 1)
                else:
                    for u in range(2):
                        act.wait_ge(*turned[u].at(i, 2))
                        act.activation(flat(dst_f[u][:, :, :]), flat(bank[u][1][:, :, :]), ACT.Copy
                                       ).then_inc(dst_ready[u].sem, 1)
                for u in range(2):
                    act.wait_ge(*q_mm[u].at(i))
                    act.activation(flat(q_f[u][:, :, :]), flat(bank[u][1][:, :, :]), ACT.Identity,
                                   bias=b_q[:, :]).then_inc(q_ready[u].sem, 1)
                for u in range(2):
                    act.wait_ge(*logit_mm[u].at(i))
                    act.wait_ge(*stored[u].before(i))
                    act.activation(logit[u][:, 0, :], flat(bank[u][2][0:HEADS, :, :]), ACT.Copy
                                   ).then_inc(logit_ready[u].sem, 1)
                for u in range(2):
                    g = up(i, u)
                    if first:
                        act.wait_ge(*dst_ready[u].done(i))
                        act.dma_start(group_of(s["h_f"], g), flat(dst_f[u][:, :, :])).then_inc(stored[u].sem, 16)
                        act.dma_start(group_of(s["x_f"], g), flat(x_f[u][:, :, :])).then_inc(stored[u].sem, 16)
                    act.wait_ge(*v_ready[u].at(i))
                    act.dma_start(group_of(s["value"], g), flat(value[u][:, :, :])).then_inc(stored[u].sem, 16)
                    act.wait_ge(*running[u].at(i))
                    act.dma_start(group_of(s["logit"], g), logit[u][:, :, :].rearrange("p a d -> p (a d)")
                                  ).then_inc(stored[u].sem, 16)
            for u in range(2):
                act.wait_ge(*stored[u].done(PAIRS))

        @block.vector
        def _(dve):
            dve.memset(eps[:, :], EPS).then_inc(eps_set, 1)
            dve.memset(logit[1][:, :, :], 0.0).then_inc(runs_set, 1)
            dve.wait_ge(weights_in, loaded)
            dve.wait_ge(runs_set, 1)
            with dve.Fori(1, PAIRS + 1) as i:
                if first:
                    for u in range(2):
                        dve.wait_ge(*src_in[u].at(i))
                        norm_src.vector_stats(dve, u, i, 0, src[u])
                        dve.wait_ge(*dst_in[u].at(i))
                        norm_dst.vector_stats(dve, u, i, 0, dst[u])
                    for u in range(2):
                        norm_src.vector_scale(dve, u, i, 0)
                        norm_dst.vector_scale(dve, u, i, 0)
                for u in range(2):
                    dve.wait_ge(*turned[u].at(i, 1))
                    dve.tensor_copy(flat(src_f[u][:, :, :]), flat(bank[u][0][:, :, :])
                                    ).then_inc(src_ready[u].sem, 1)
                for u in range(2):
                    dve.wait_ge(*q_ready[u].at(i))
                    dve.wait_ge(*k_mm[u].at(i))
                    dve.scalar_tensor_tensor(out=flat(qk_f[u][:, :, :]), in0=flat(bank[u][3][:, :, :]),
                                             scalar=b_k[:, :], in1=flat(q_f[u][:, :, :]), op0=ALU.add,
                                             op1=ALU.mult).then_inc(qk_ready[u].sem, 1)
                for u in range(2):
                    dve.wait_ge(*v_mm[u].at(i))
                    dve.wait_ge(*stored[u].before(i))
                    dve.tensor_tensor(value[u][:, :, :], bank[u][0][:, :, :],
                                      b_v[:, :].rearrange("p (o d) -> p o d", o=1).to_broadcast((P, T, D)),
                                      ALU.add).then_inc(v_ready[u].sem, 1)
                for u in range(2):
                    dve.wait_ge(*logit_ready[u].at(i))
                    dve.wait_ge(*mask_in[u].at(i))
                    dve.wait_ge(*(running[0].at(i) if u else running[1].before(i)))
                    dve.tensor_tensor_scan(out=logit[u][:, 1, :], data0=mask[u][:, 0, :],
                                           data1=logit[u][:, 0, :],
                                           initial=logit[1 - u][:, 1, GROUP - 1:GROUP], op0=ALU.add,
                                           op1=ALU.max).then_inc(running[u].sem, 1)
    ph.end()



def attend_nodes(nc, w, s, level):
    first = level == 0
    ph = Phase(nc, f"softmax{level}")
    cell = ph.sb("cell", [1, 32])
    ident, ws = ph.sb("ident", [P, P]), ph.sb("ws", [P, D])
    head_row = ph.sb("head_row", [HEADS, D])
    b_s = ph.sb("b_s", [P, 1])
    eps = ph.sb("eps", [P, 1])
    value = ph.sbs("value", [P, T, D])
    h_f, x_f = ph.sbs("h_f", [P, T, P]), ph.sbs("x_f", [P, T, P])
    same = ph.sbs("same", [P, 2, T, P])
    mask = ph.sbs("mask", [HEADS, 2, GROUP])
    logit = ph.sbs("logit", [HEADS, 2, GROUP])
    top, shifted, power = (ph.sbs(n, [HEADS, GROUP]) for n in ("top", "shifted", "power"))
    weight, message = ph.sbs("weight", [P, T, D]), ph.sbs("message", [P, T, D])
    total, summed = ph.sbs("total", [P, T, P]), ph.sbs("summed", [P, T, P])
    inverse, mean, mixed, g_f = (ph.sbs(n, [P, T, P]) for n in ("inverse", "mean", "mixed", "g_f"))
    row, h1_f = ph.sbs("row", [P, T, D]), ph.sbs("h1_f", [P, T, P])
    bank = ph.banks()
    norm = None if first else Norm(ph)

    weights_in, zeros_set = ph.sem("weights_in"), ph.sem("zeros_set")
    logits_in, value_in, same_in = ph.pair("logits_in", per=2, unit=16), ph.pair("value_in", unit=16), \
        ph.pair("same_in", unit=16)
    h_in, x_in = ph.pair("h_in", unit=16), ph.pair("x_in", unit=16)
    top_ready = ph.pair("top_ready", primed=True)
    shift_ready = ph.pair("shift_ready", primed=True)
    power_ready, weight_mm, weight_ready = ph.pair("power_ready"), ph.pair("weight_mm"), ph.pair("weight_ready")
    message_ready = ph.pair("message_ready", primed=True)
    sums_mm, skip_mm = ph.pair("sums_mm", per=2), ph.pair("skip_mm", primed=True)
    carry_total = ph.pair("carry_total", per=T, primed=True)
    carry_sum = ph.pair("carry_sum", per=T, primed=True)
    soft = ph.pair("soft", per=4)
    g_ready = ph.pair("g_ready", primed=True)
    out_turned, row_ready = ph.pair("out_turned", per=1 if first else 2), ph.pair("row_ready")
    stored = ph.pair("stored", per=2 if first else 3, unit=16, primed=True)
    WHAT = [(ident[:, :], w["ident"]), (ws[:, :], w[f"s_w{level}"]), (head_row[:, :], w["head_row"]),
            (b_s[:, :], column(w[f"s_b{level}"]))]
    loaded = 16 * len(WHAT)

    with nc.Block() as block:
        @block.sync
        def _(sp):
            ph.prime(sp, cell, w["ident"])
            load_weights(sp, weights_in, WHAT)
            with sp.Fori(1, PAIRS + 1) as i:
                for u in range(2):
                    g = down(i, u)
                    sp.wait_ge(*shift_ready[u].before(i))
                    ph.stand(sp)
                    sp.dma_start(mask[u][:, :, :].rearrange("p a d -> p (a d)"), group_of(s["masks"], g)
                                 ).then_inc(logits_in[u].sem, 16)
                    sp.dma_start(logit[u][:, :, :].rearrange("p a d -> p (a d)"), group_of(s["logit"], g)
                                 ).then_inc(logits_in[u].sem, 16)
                    sp.wait_ge(*message_ready[u].before(i))
                    ph.stand(sp)
                    sp.dma_start(flat(value[u][:, :, :]), group_of(s["value"], g)).then_inc(value_in[u].sem, 16)
                    sp.wait_ge(*skip_mm[u].before(i))
                    ph.stand(sp)
                    sp.dma_start(flat(h_f[u][:, :, :]), group_of(s["h_f"] if first else s["g_f"], g)
                                 ).then_inc(h_in[u].sem, 16)
                    sp.wait_ge(*carry_sum[u].before(i))
                    ph.stand(sp)
                    sp.dma_start(same[u][:, :, :, :].rearrange("p a j d -> p (a j d)"),
                                 group_of(s["same"], g)).then_inc(same_in[u].sem, 16)
                    if not first:
                        sp.wait_ge(*g_ready[u].before(i))
                        ph.stand(sp)
                        sp.dma_start(flat(x_f[u][:, :, :]), group_of(s["x_f"], g)).then_inc(x_in[u].sem, 16)

        @block.tensor
        def _(pe):
            pe.wait_ge(weights_in, loaded)
            with pe.Fori(1, PAIRS + 1) as i:
                for u in range(2):
                    pe.wait_ge(*h_in[u].at(i))
                    product_features(pe, bank[u][3], ws[:, :], h_f[u]).then_inc(skip_mm[u].sem, 1)
                    pe.wait_ge(*power_ready[u].at(i))
                    for t in range(T):
                        ins = pe.matmul(bank[u][0][:, t, :], power[u][:, t * P:(t + 1) * P], head_row[:, :],
                                        start=True, stop=True)
                    ins.then_inc(weight_mm[u].sem, 1)
                for u in range(2):
                    pe.wait_ge(*same_in[u].at(i))
                    pe.wait_ge(*weight_ready[u].at(i))
                    sum_over_runs(pe, bank[u][2], weight[u], same[u]).then_inc(sums_mm[u].sem, 1)
                    pe.wait_ge(*message_ready[u].at(i))
                    sum_over_runs(pe, bank[u][1], message[u], same[u]).then_inc(sums_mm[u].sem, 1)
                for u in range(2):
                    pe.wait_ge(*g_ready[u].at(i))
                    turn_to_tokens(pe, bank[u][0], g_f[u], ident).then_inc(out_turned[u].sem, 1)
                if not first:
                    for u in range(2):
                        pe.wait_ge(*norm.out[u].at(i))
                        turn_to_features(pe, bank[u][2], row[u], ident).then_inc(out_turned[u].sem, 1)

        @block.scalar
        def _(act):
            act.wait_ge(weights_in, loaded)
            act.wait_ge(zeros_set, 4)
            with act.Fori(1, PAIRS + 1) as i:
                for u in range(2):
                    act.wait_ge(*shift_ready[u].at(i))
                    act.activation(power[u][:, :], shifted[u][:, :], ACT.Exp).then_inc(power_ready[u].sem, 1)
                for u in range(2):
                    act.wait_ge(*weight_mm[u].at(i))
                    act.activation(flat(weight[u][:, :, :]), flat(bank[u][0][:, :, :]), ACT.Copy
                                   ).then_inc(weight_ready[u].sem, 1)
                if first:
                    for u in range(2):
                        act.wait_ge(*soft[u].at(i, 4))
                        act.wait_ge(*stored[u].before(i))
                        act.activation(flat(g_f[u][:, :, :]), flat(mixed[u][:, :, :]), ACT.Relu,
                                       bias=b_s[:, :]).then_inc(g_ready[u].sem, 1)
                else:
                    for u in range(2):
                        norm.scalar_root(act, u, i, 0, eps)
                    for u in range(2):
                        act.wait_ge(*stored[u].before(i))
                        norm.scalar_apply(act, u, i, 0, row[u], bank[u][0])
                for u in range(2):
                    g = down(i, u)
                    act.wait_ge(*g_ready[u].at(i))
                    act.dma_start(group_of(s["g_f"] if first else s["x1_f"], g), flat(g_f[u][:, :, :])
                                  ).then_inc(stored[u].sem, 16)
                    if first:
                        act.wait_ge(*row_ready[u].at(i))
                        act.dma_start(table_rows(s["table"][1], g), flat(row[u][:, :, :])
                                      ).then_inc(stored[u].sem, 16)
                    else:
                        act.wait_ge(*norm.out[u].at(i))
                        act.dma_start(table_rows(s["table"][2], g), flat(row[u][:, :, :])
                                      ).then_inc(stored[u].sem, 16)
                        act.wait_ge(*row_ready[u].at(i))
                        act.dma_start(group_of(s["h_f"], g), flat(h1_f[u][:, :, :])).then_inc(stored[u].sem, 16)
            for u in range(2):
                act.wait_ge(*stored[u].done(PAIRS))

        @block.vector
        def _(dve):
            dve.memset(eps[:, :], EPS).then_inc(zeros_set, 1)
            for z in (top[1][:, :], total[1][:, :, :], summed[1][:, :, :]):
                dve.memset(z, 0.0).then_inc(zeros_set, 1)
            dve.wait_ge(weights_in, loaded)
            dve.wait_ge(zeros_set, 4)
            with dve.Fori(1, PAIRS + 1) as i:
                for u in range(2):
                    dve.wait_ge(*logits_in[u].done(i))
                    dve.wait_ge(*(top_ready[0].at(i) if u else top_ready[1].before(i)))
                    dve.tensor_tensor_scan(out=top[u][:, ::-1], data0=mask[u][:, 1, ::-1],
                                           data1=logit[u][:, 1, ::-1], initial=top[1 - u][:, 0:1],
                                           op0=ALU.add, op1=ALU.max).then_inc(top_ready[u].sem, 1)
                for u in range(2):
                    dve.wait_ge(*top_ready[u].at(i))
                    dve.tensor_tensor(shifted[u][:, :], logit[u][:, 0, :], top[u][:, :], ALU.subtract
                                      ).then_inc(shift_ready[u].sem, 1)
                for u in range(2):
                    dve.wait_ge(*weight_ready[u].at(i))
                    dve.wait_ge(*value_in[u].at(i))
                    dve.tensor_tensor(flat(message[u][:, :, :]), flat(weight[u][:, :, :]),
                                      flat(value[u][:, :, :]), ALU.mult).then_inc(message_ready[u].sem, 1)
                for u in range(2):
                    dve.wait_ge(*sums_mm[u].at(i, 1))
                    add_carry(dve, total, bank[u][2], same[u], carry_total, u, i)
                    dve.wait_ge(*sums_mm[u].at(i, 2))
                    add_carry(dve, summed, bank[u][1], same[u], carry_sum, u, i)
                    dve.wait_ge(*carry_total[u].done(i))
                    dve.tensor_scalar(flat(inverse[u][:, :, :]), flat(total[u][:, :, :]), SOFT_EPS, None,
                                      ALU.add).then_inc(soft[u].sem, 1)
                for u in range(2):
                    dve.wait_ge(*soft[u].at(i, 1))
                    dve.reciprocal(flat(mean[u][:, :, :]), flat(inverse[u][:, :, :])).then_inc(soft[u].sem, 1)
                for u in range(2):
                    dve.wait_ge(*soft[u].at(i, 2))
                    dve.wait_ge(*carry_sum[u].done(i))
                    dve.tensor_tensor(flat(inverse[u][:, :, :]), flat(summed[u][:, :, :]),
                                      flat(mean[u][:, :, :]), ALU.mult).then_inc(soft[u].sem, 1)
                for u in range(2):
                    dve.wait_ge(*soft[u].at(i, 3))
                    dve.wait_ge(*skip_mm[u].at(i))
                    dve.tensor_tensor(flat(mixed[u][:, :, :]), flat(bank[u][3][:, :, :]),
                                      flat(inverse[u][:, :, :]), ALU.add).then_inc(soft[u].sem, 1)
                if first:
                    for u in range(2):
                        dve.wait_ge(*out_turned[u].at(i, 1))
                        dve.wait_ge(*stored[u].before(i))
                        dve.tensor_copy(flat(row[u][:, :, :]), flat(bank[u][0][:, :, :])
                                        ).then_inc(row_ready[u].sem, 1)
                else:
                    for u in range(2):
                        dve.wait_ge(*soft[u].at(i, 4))
                        dve.wait_ge(*x_in[u].at(i))
                        dve.wait_ge(*stored[u].before(i))
                        dve.scalar_tensor_tensor(out=flat(g_f[u][:, :, :]), in0=flat(mixed[u][:, :, :]),
                                                 scalar=b_s[:, :], in1=flat(x_f[u][:, :, :]), op0=ALU.add,
                                                 op1=ALU.add).then_inc(g_ready[u].sem, 1)
                    for u in range(2):
                        dve.wait_ge(*out_turned[u].at(i, 1))
                        norm.vector_stats(dve, u, i, 0, bank[u][0])
                    for u in range(2):
                        norm.vector_scale(dve, u, i, 0)
                    for u in range(2):
                        dve.wait_ge(*out_turned[u].at(i, 2))
                        dve.tensor_copy(flat(h1_f[u][:, :, :]), flat(bank[u][2][:, :, :])
                                        ).then_inc(row_ready[u].sem, 1)
    ph.end()



class Gather:

    def __init__(self, ph, s, level):
        self.ph, self.s, self.table = ph, s, s["table"][level]
        self.idx = ph.sbs("idx", [P, T], I32)
        self.rows = ph.sbs("rows", [P, T, D])
        self.same = ph.sbs("same", [P, 2, T, P])
        self.sums = ph.sbs("sums", [P, T, P])
        self.idx_in = ph.pair("idx_in", unit=16)
        self.rows_in = ph.pair("rows_in", per=T, unit=16, primed=True, soft=True)
        self.same_in = ph.pair("same_in", unit=16)
        self.mm = ph.pair("sums_mm", primed=True)
        self.carry = ph.pair("carry", per=T, primed=True)
        self.zeros_set = ph.sem("sums_zero")

    def load(self, sp, u, i):
        sp.wait_ge(*self.rows_in[u].before(i))
        self.ph.stand(sp)
        sp.dma_start(self.idx[u][:, :], group_of(self.s["end_rows"], down(i, u))[:, 0:T]
                     ).then_inc(self.idx_in[u].sem, 16)
        sp.wait_ge(*self.carry[u].before(i))
        self.ph.stand(sp)
        sp.dma_start(self.same[u][:, :, :, :].rearrange("p a j d -> p (a j d)"),
                     group_of(self.s["same"], down(i, u))).then_inc(self.same_in[u].sem, 16)

    def gather(self, pl, u, i):
        pl.wait_ge(*self.idx_in[u].at(i))
        pl.wait_ge(*self.mm[u].before(i))
        self.ph.stand(pl)
        for t in range(T):
            pl.indirect_dma_start(self.rows[u][:, t, :], None, self.table,
                                  bass.IndirectOffsetOnAxis(ap=self.idx[u][:, t:t + 1], axis=0)
                                  ).then_inc(self.rows_in[u].sem, 16)

    def multiply(self, pe, u, i, bank):
        pe.wait_ge(*self.same_in[u].at(i))
        pe.wait_ge(*self.rows_in[u].done(i))
        sum_over_runs(pe, bank, self.rows[u], self.same[u]).then_inc(self.mm[u].sem, 1)

    def zero(self, dve):
        dve.memset(self.sums[1][:, :, :], 0.0).then_inc(self.zeros_set, 1)
        dve.wait_ge(self.zeros_set, 1)

    def collect(self, dve, u, i, bank):
        dve.wait_ge(*self.mm[u].at(i))
        add_carry(dve, self.sums, bank, self.same[u], self.carry, u, i)


def degree_row(s, g, which, n=P):
    row = s["degrees"][bass.ds(g, 1)].rearrange("o p f -> (o p f)")[which * GROUP:(which + 1) * GROUP]
    return over_partitions(row, n)


def sage_hidden(nc, w, s):
    ph = Phase(nc, "sage0")
    cell = ph.sb("cell", [1, 32])
    wl0, wr0 = ph.sb("wl0", [P, 2, D]), ph.sb("wr0", [P, 2, D])
    wl1, wr1 = ph.sb("wl1", [P, 2, D]), ph.sb("wr1", [P, 2, D])
    b_l0, b_l1 = ph.sb("b_l0", [P, 2]), ph.sb("b_l1", [P, 1])
    h_f, x_f, rate = (ph.sbs(n, [P, T, P]) for n in ("h_f", "x_f", "rate"))
    mean, next_x, row = (ph.sbs(n, [P, T, P]) for n in ("mean", "next_x", "row"))
    g3_f = [[ph.sb(f"g3_f{u}{k}", [P, T, P]) for k in range(2)] for u in range(2)]
    bank = ph.banks()
    ga = Gather(ph, s, 2)
    weights_in = ph.sem("weights_in")
    h_in, x_in = ph.pair("h_in", unit=16), ph.pair("x_in", per=2, unit=16)
    mean_ready = ph.pair("mean_ready")
    g3_mm, g3_ready = ph.pair("g3_mm", per=2, primed=True), ph.pair("g3_ready", per=2)
    t3_mm, skip_mm = ph.pair("t3_mm"), ph.pair("skip_mm")
    x_ready, row_ready = ph.pair("x_ready", primed=True), ph.pair("row_ready")
    stored = ph.pair("stored", per=2, unit=16, primed=True)
    split = lambda a: a.rearrange("(k p) d -> p k d", p=P)
    WHAT = [(wl0[:, :, :].rearrange("p k d -> p (k d)"), w["Wl0"]),
            (wr0[:, :, :].rearrange("p k d -> p (k d)"), w["Wr0"]),
            (wl1[:, :, :], split(w["Wl1"])), (wr1[:, :, :], split(w["Wr1"])),
            (b_l0[:, 0:1], column(w["bl0"][0:D])), (b_l0[:, 1:2], column(w["bl0"][D:2 * D])),
            (b_l1[:, :], column(w["bl1"]))]
    loaded = 16 * len(WHAT)
    with nc.Block() as block:
        @block.sync
        def _(sp):
            ph.prime(sp, cell, w["ident"])
            load_weights(sp, weights_in, WHAT)
            with sp.Fori(1, PAIRS + 1) as i:
                for u in range(2):
                    g = down(i, u)
                    ga.load(sp, u, i)
                    sp.wait_ge(*g3_mm[u].before(i))
                    ph.stand(sp)
                    sp.dma_start(flat(h_f[u][:, :, :]), group_of(s["h_f"], g)).then_inc(h_in[u].sem, 16)
                    sp.wait_ge(*x_ready[u].before(i))
                    ph.stand(sp)
                    sp.dma_start(flat(rate[u][:, :, :]), degree_row(s, g, 0)).then_inc(x_in[u].sem, 16)
                    sp.dma_start(flat(x_f[u][:, :, :]), group_of(s["x1_f"], g)).then_inc(x_in[u].sem, 16)

        @block.gpsimd
        def _(pl):
            ph.prime(pl, cell, w["ident"], soft=True)
            with pl.Fori(1, PAIRS + 1) as i:
                for u in range(2):
                    ga.gather(pl, u, i)

        @block.tensor
        def _(pe):
            pe.wait_ge(weights_in, loaded)
            with pe.Fori(1, PAIRS + 1) as i:
                for u in range(2):
                    pe.wait_ge(*x_ready[u].before(i))
                    ga.multiply(pe, u, i, bank[u][0])
                for u in range(2):
                    pe.wait_ge(*h_in[u].at(i))
                    pe.wait_ge(*mean_ready[u].at(i))
                    for k in range(2):
                        product_features(pe, bank[u][1 + k], wr0[:, k, :], h_f[u], stop=False)
                        product_features(pe, bank[u][1 + k], wl0[:, k, :], mean[u], start=False
                                         ).then_inc(g3_mm[u].sem, 1)
                for u in range(2):
                    pe.wait_ge(*g3_ready[u].done(i))
                    for j in range(T):
                        for k in range(2):
                            ins = pe.matmul(bank[u][3][:, j, :], g3_f[u][k][:, j, :], wl1[:, k, :],
                                            start=(k == 0), stop=(k == 1))
                    ins.then_inc(t3_mm[u].sem, 1)
                    product_features(pe, bank[u][0], wr1[:, 0, :], g3_f[u][0], stop=False)
                    product_features(pe, bank[u][0], wr1[:, 1, :], g3_f[u][1], start=False
                                     ).then_inc(skip_mm[u].sem, 1)

        @block.scalar
        def _(act):
            act.wait_ge(weights_in, loaded)
            with act.Fori(1, PAIRS + 1) as i:
                for u in range(2):
                    for k in range(2):
                        act.wait_ge(*g3_mm[u].at(i, k + 1))
                        act.activation(flat(g3_f[u][k][:, :, :]), flat(bank[u][1 + k][:, :, :]), ACT.Relu,
                                       bias=b_l0[:, k:k + 1]).then_inc(g3_ready[u].sem, 1)
                for u in range(2):
                    act.wait_ge(*t3_mm[u].at(i))
                    act.wait_ge(*stored[u].before(i))
                    act.activation(flat(row[u][:, :, :]), flat(bank[u][3][:, :, :]), ACT.Copy
                                   ).then_inc(row_ready[u].sem, 1)
                for u in range(2):
                    g = down(i, u)
                    act.wait_ge(*row_ready[u].at(i))
                    act.dma_start(table_rows(s["table"][3], g), flat(row[u][:, :, :])).then_inc(stored[u].sem, 16)
                    act.wait_ge(*x_ready[u].at(i))
                    act.dma_start(group_of(s["x_f"], g), flat(next_x[u][:, :, :])).then_inc(stored[u].sem, 16)
            for u in range(2):
                act.wait_ge(*stored[u].done(PAIRS))

        @block.vector
        def _(dve):
            ga.zero(dve)
            dve.wait_ge(weights_in, loaded)
            with dve.Fori(1, PAIRS + 1) as i:
                for u in range(2):
                    ga.collect(dve, u, i, bank[u][0])
                for u in range(2):
                    dve.wait_ge(*ga.carry[u].done(i))
                    dve.wait_ge(*x_in[u].done(i))
                    dve.tensor_tensor(mean[u][:, :, :], ga.sums[u][:, :, :], rate[u][:, :, :], ALU.mult
                                      ).then_inc(mean_ready[u].sem, 1)
                for u in range(2):
                    dve.wait_ge(*skip_mm[u].at(i))
                    dve.wait_ge(*stored[u].before(i))
                    dve.scalar_tensor_tensor(out=flat(next_x[u][:, :, :]), in0=flat(bank[u][0][:, :, :]),
                                             scalar=b_l1[:, :], in1=flat(x_f[u][:, :, :]), op0=ALU.add,
                                             op1=ALU.add).then_inc(x_ready[u].sem, 1)
    ph.end()


def sage_out(nc, w, s):
    ph = Phase(nc, "sage1")
    cell = ph.sb("cell", [1, 32])
    ident, w1, eps = ph.sb("ident", [P, P]), ph.sb("w1", [P, D]), ph.sb("eps", [P, 1])
    x_f, rate, root = (ph.sbs(n, [P, T, P]) for n in ("x_f", "rate", "root"))
    mean, next_x, h, h_f, scaled, row = (ph.sbs(n, [P, T, P]) for n in
                                         ("mean", "next_x", "h", "h_f", "scaled", "row"))
    bank = ph.banks()
    ga = Gather(ph, s, 3)
    norm = Norm(ph)
    weights_in, eps_set = ph.sem("weights_in"), ph.sem("eps_set")
    x_in, root_in = ph.pair("x_in", per=2, unit=16), ph.pair("root_in", unit=16)
    mean_ready, x_ready = ph.pair("mean_ready"), ph.pair("x_ready", primed=True)
    turned, h_ready = ph.pair("turned", per=3), ph.pair("h_ready")
    w1_mm, scaled_ready = ph.pair("w1_mm"), ph.pair("scaled_ready", primed=True)
    row_ready = ph.pair("row_ready")
    stored = ph.pair("stored", per=3, unit=16, primed=True)
    WHAT = [(ident[:, :], w["ident"]), (w1[:, :], w["W1"])]
    loaded = 16 * len(WHAT)
    with nc.Block() as block:
        @block.sync
        def _(sp):
            ph.prime(sp, cell, w["ident"])
            load_weights(sp, weights_in, WHAT)
            with sp.Fori(1, PAIRS + 1) as i:
                for u in range(2):
                    g = down(i, u)
                    ga.load(sp, u, i)
                    sp.wait_ge(*x_ready[u].before(i))
                    ph.stand(sp)
                    sp.dma_start(flat(rate[u][:, :, :]), degree_row(s, g, 0)).then_inc(x_in[u].sem, 16)
                    sp.dma_start(flat(x_f[u][:, :, :]), group_of(s["x_f"], g)).then_inc(x_in[u].sem, 16)
                    sp.wait_ge(*scaled_ready[u].before(i))
                    ph.stand(sp)
                    sp.dma_start(flat(root[u][:, :, :]), degree_row(s, g, 1)).then_inc(root_in[u].sem, 16)

        @block.gpsimd
        def _(pl):
            ph.prime(pl, cell, w["ident"], soft=True)
            with pl.Fori(1, PAIRS + 1) as i:
                for u in range(2):
                    ga.gather(pl, u, i)

        @block.tensor
        def _(pe):
            pe.wait_ge(weights_in, loaded)
            with pe.Fori(1, PAIRS + 1) as i:
                for u in range(2):
                    ga.multiply(pe, u, i, bank[u][0])
                for u in range(2):
                    pe.wait_ge(*x_ready[u].at(i))
                    turn_to_tokens(pe, bank[u][1], next_x[u], ident).then_inc(turned[u].sem, 1)
                for u in range(2):
                    pe.wait_ge(*norm.out[u].at(i))
                    turn_to_features(pe, bank[u][2], h[u], ident).then_inc(turned[u].sem, 1)
                for u in range(2):
                    pe.wait_ge(*h_ready[u].at(i))
                    product_features(pe, bank[u][3], w1[:, :], h_f[u]).then_inc(w1_mm[u].sem, 1)
                for u in range(2):
                    pe.wait_ge(*scaled_ready[u].at(i))
                    turn_to_tokens(pe, bank[u][1], scaled[u], ident).then_inc(turned[u].sem, 1)

        @block.scalar
        def _(act):
            act.wait_ge(weights_in, loaded)
            act.wait_ge(eps_set, 1)
            with act.Fori(1, PAIRS + 1) as i:
                for u in range(2):
                    norm.scalar_root(act, u, i, 0, eps)
                for u in range(2):
                    norm.scalar_apply(act, u, i, 0, h[u], bank[u][1])
                for u in range(2):
                    act.wait_ge(*turned[u].at(i, 3))
                    act.wait_ge(*stored[u].before(i))
                    act.activation(flat(row[u][:, :, :]), flat(bank[u][1][:, :, :]), ACT.Copy
                                   ).then_inc(row_ready[u].sem, 1)
                for u in range(2):
                    g = down(i, u)
                    act.dma_start(group_of(s["x1_f"], g), flat(next_x[u][:, :, :])).then_inc(stored[u].sem, 16)
                    act.dma_start(group_of(s["g_f"], g), flat(scaled[u][:, :, :])).then_inc(stored[u].sem, 16)
                    act.wait_ge(*row_ready[u].at(i))
                    act.dma_start(table_rows(s["table"][4], g), flat(row[u][:, :, :])).then_inc(stored[u].sem, 16)
            for u in range(2):
                act.wait_ge(*stored[u].done(PAIRS))

        @block.vector
        def _(dve):
            dve.memset(eps[:, :], EPS).then_inc(eps_set, 1)
            ga.zero(dve)
            with dve.Fori(1, PAIRS + 1) as i:
                for u in range(2):
                    ga.collect(dve, u, i, bank[u][0])
                for u in range(2):
                    dve.wait_ge(*ga.carry[u].done(i))
                    dve.wait_ge(*x_in[u].done(i))
                    dve.tensor_tensor(mean[u][:, :, :], ga.sums[u][:, :, :], rate[u][:, :, :], ALU.mult
                                      ).then_inc(mean_ready[u].sem, 1)
                for u in range(2):
                    dve.wait_ge(*mean_ready[u].at(i))
                    dve.wait_ge(*stored[u].before(i))
                    dve.tensor_tensor(next_x[u][:, :, :], mean[u][:, :, :], x_f[u][:, :, :], ALU.add
                                      ).then_inc(x_ready[u].sem, 1)
                for u in range(2):
                    dve.wait_ge(*turned[u].at(i, 1))
                    norm.vector_stats(dve, u, i, 0, bank[u][1])
                for u in range(2):
                    norm.vector_scale(dve, u, i, 0)
                for u in range(2):
                    dve.wait_ge(*turned[u].at(i, 2))
                    dve.tensor_copy(flat(h_f[u][:, :, :]), flat(bank[u][2][:, :, :])).then_inc(h_ready[u].sem, 1)
                for u in range(2):
                    dve.wait_ge(*w1_mm[u].at(i))
                    dve.wait_ge(*root_in[u].at(i))
                    dve.tensor_tensor(scaled[u][:, :, :], bank[u][3][:, :, :], root[u][:, :, :], ALU.mult
                                      ).then_inc(scaled_ready[u].sem, 1)
    ph.end()


def gcn_hidden(nc, w, s):
    ph = Phase(nc, "gcn0")
    cell = ph.sb("cell", [1, 32])
    ident, w2 = ph.sb("ident", [P, P]), ph.sb("w2", [P, D])
    b_1, rate_col = ph.sb("b_1", [P, 1]), ph.sb("rate_col", [P, 1])
    own, root = ph.sbs("own", [P, T, P]), ph.sbs("root", [P, T, P])
    both, mean, g_f, scaled, row = (ph.sbs(n, [P, T, P]) for n in ("both", "mean", "g_f", "scaled", "row"))
    bank = ph.banks()
    ga = Gather(ph, s, 4)
    weights_in, rate_steps, rates_set = ph.sem("weights_in"), ph.sem("rate_steps"), ph.sem("rates_set")
    own_in = ph.pair("own_in", per=2, unit=16)
    both_ready, mean_ready, g_ready = ph.pair("both_ready"), ph.pair("mean_ready"), ph.pair("g_ready")
    w2_mm, scaled_ready = ph.pair("w2_mm"), ph.pair("scaled_ready", primed=True)
    turned, row_ready = ph.pair("turned"), ph.pair("row_ready", primed=True)
    stored = ph.pair("stored", per=2, unit=16, primed=True)
    WHAT = [(ident[:, :], w["ident"]), (w2[:, :], w["W2"][0:D, :]), (b_1[:, :], column(w["b1"]))]
    loaded = 16 * (len(WHAT) + 1)
    rates = rate_row_steps(nc, ph, w, bank[0][0], weights_in, rate_steps)
    with nc.Block() as block:
        @block.sync
        def _(sp):
            ph.prime(sp, cell, w["ident"])
            load_weights(sp, weights_in, WHAT)
            rates["load"](sp)
            with sp.Fori(1, PAIRS + 1) as i:
                for u in range(2):
                    g = down(i, u)
                    ga.load(sp, u, i)
                    sp.wait_ge(*scaled_ready[u].before(i))
                    ph.stand(sp)
                    sp.dma_start(flat(own[u][:, :, :]), group_of(s["g_f"], g)).then_inc(own_in[u].sem, 16)
                    sp.dma_start(flat(root[u][:, :, :]), degree_row(s, g, 1)).then_inc(own_in[u].sem, 16)

        @block.gpsimd
        def _(pl):
            ph.prime(pl, cell, w["ident"], soft=True)
            with pl.Fori(1, PAIRS + 1) as i:
                for u in range(2):
                    ga.gather(pl, u, i)

        @block.tensor
        def _(pe):
            pe.wait_ge(weights_in, loaded)
            rates["tensor"](pe)
            pe.wait_ge(rates_set, 1)
            with pe.Fori(1, PAIRS + 1) as i:
                for u in range(2):
                    ga.multiply(pe, u, i, bank[u][0])
                for u in range(2):
                    pe.wait_ge(*g_ready[u].at(i))
                    product_features(pe, bank[u][1], w2[:, :], g_f[u]).then_inc(w2_mm[u].sem, 1)
                for u in range(2):
                    pe.wait_ge(*scaled_ready[u].at(i))
                    pe.wait_ge(*row_ready[u].before(i))
                    turn_to_tokens(pe, bank[u][2], scaled[u], ident).then_inc(turned[u].sem, 1)

        @block.scalar
        def _(act):
            act.wait_ge(weights_in, loaded)
            with act.Fori(1, PAIRS + 1) as i:
                for u in range(2):
                    act.wait_ge(*mean_ready[u].at(i))
                    act.activation(flat(g_f[u][:, :, :]), flat(mean[u][:, :, :]), ACT.Relu, bias=b_1[:, :]
                                   ).then_inc(g_ready[u].sem, 1)
                for u in range(2):
                    act.wait_ge(*turned[u].at(i))
                    act.wait_ge(*stored[u].before(i))
                    act.activation(flat(row[u][:, :, :]), flat(bank[u][2][:, :, :]), ACT.Copy
                                   ).then_inc(row_ready[u].sem, 1)
                for u in range(2):
                    g = down(i, u)
                    act.dma_start(group_of(s["h_f"], g), flat(scaled[u][:, :, :])).then_inc(stored[u].sem, 16)
                    act.wait_ge(*row_ready[u].at(i))
                    act.dma_start(table_rows(s["table"][5], g), flat(row[u][:, :, :])).then_inc(stored[u].sem, 16)
            for u in range(2):
                act.wait_ge(*stored[u].done(PAIRS))

        @block.vector
        def _(dve):
            ga.zero(dve)
            dve.wait_ge(weights_in, loaded)
            rates["vector"](dve, None, rates_set, rate_col)
            dve.wait_ge(rates_set, 1)
            with dve.Fori(1, PAIRS + 1) as i:
                for u in range(2):
                    ga.collect(dve, u, i, bank[u][0])
                for u in range(2):
                    dve.wait_ge(*ga.carry[u].done(i))
                    dve.wait_ge(*own_in[u].done(i))
                    dve.tensor_tensor(both[u][:, :, :], ga.sums[u][:, :, :], own[u][:, :, :], ALU.add
                                      ).then_inc(both_ready[u].sem, 1)
                for u in range(2):
                    dve.wait_ge(*both_ready[u].at(i))
                    dve.tensor_tensor(mean[u][:, :, :], both[u][:, :, :], root[u][:, :, :], ALU.mult
                                      ).then_inc(mean_ready[u].sem, 1)
                for u in range(2):
                    dve.wait_ge(*w2_mm[u].at(i))
                    dve.wait_ge(*stored[u].before(i))
                    dve.scalar_tensor_tensor(out=flat(scaled[u][:, :, :]), in0=flat(bank[u][1][:, :, :]),
                                             scalar=rate_col[:, :], in1=flat(root[u][:, :, :]), op0=ALU.add,
                                             op1=ALU.mult).then_inc(scaled_ready[u].sem, 1)
    ph.end()


def gcn_out(nc, out, w, s):
    ph = Phase(nc, "gcn1")
    cell = ph.sb("cell", [1, 32])
    ident, b_2, eps = ph.sb("ident", [P, P]), ph.sb("b_2", [P, 1]), ph.sb("eps", [P, 1])
    w_self = ph.sb("w_self", [P, D])
    own, root, x_f = (ph.sbs(n, [P, T, P]) for n in ("own", "root", "x_f"))
    both, mean, next_x, row, h_f = (ph.sbs(n, [P, T, P]) for n in ("both", "mean", "next_x", "row", "h_f"))
    last, out_row = ph.sbs("last", [P, T, P]), ph.sbs("out_row", [P, T, D])
    put = ph.sbs("put", [P, T], I32)
    bank = ph.banks()
    ga = Gather(ph, s, 5)
    norm = Norm(ph)
    weights_in, eps_set = ph.sem("weights_in"), ph.sem("eps_set")
    own_in, put_in = ph.pair("own_in", per=3, unit=16), ph.pair("put_in", unit=16)
    both_ready, mean_ready = ph.pair("both_ready"), ph.pair("mean_ready")
    x_ready = ph.pair("x_ready", primed=True)
    turned, h_ready = ph.pair("turned", per=3), ph.pair("h_ready")
    self_mm, last_ready = ph.pair("self_mm"), ph.pair("last_ready")
    out_ready = ph.pair("out_ready")
    stored = ph.pair("stored", unit=16, primed=True)
    scattered = ph.pair("scattered", per=T, unit=16, primed=True, soft=True)
    WHAT = [(ident[:, :], w["ident"]), (b_2[:, :], column(w["b2"])), (w_self[:, :], w["w_self"])]
    loaded = 16 * len(WHAT)
    with nc.Block() as block:
        @block.sync
        def _(sp):
            ph.prime(sp, cell, w["ident"])
            load_weights(sp, weights_in, WHAT)
            with sp.Fori(1, PAIRS + 1) as i:
                for u in range(2):
                    g = down(i, u)
                    ga.load(sp, u, i)
                    sp.wait_ge(*x_ready[u].before(i))
                    ph.stand(sp)
                    sp.dma_start(flat(own[u][:, :, :]), group_of(s["h_f"], g)).then_inc(own_in[u].sem, 16)
                    sp.dma_start(flat(root[u][:, :, :]), degree_row(s, g, 1)).then_inc(own_in[u].sem, 16)
                    sp.dma_start(flat(x_f[u][:, :, :]), group_of(s["x1_f"], g)).then_inc(own_in[u].sem, 16)
                    sp.wait_ge(*scattered[u].before(i))
                    ph.stand(sp)
                    sp.dma_start(put[u][:, :], group_of(s["put_rows"], g)).then_inc(put_in[u].sem, 16)

        @block.gpsimd
        def _(pl):
            ph.prime(pl, cell, w["ident"], soft=True)

            def scatter(i, u):
                pl.wait_ge(*put_in[u].at(i))
                pl.wait_ge(*out_ready[u].at(i))
                ph.stand(pl)
                for t in range(T):
                    pl.indirect_dma_start(
                        out, bass.IndirectOffsetOnAxis(ap=put[u][:, t:t + 1], axis=0), out_row[u][:, t, :],
                        None, bounds_check=N - 1, oob_is_err=False).then_inc(scattered[u].sem, 16)

            for u in range(2):
                ga.gather(pl, u, 1)
            with pl.Fori(1, PAIRS) as i:
                for u in range(2):
                    ga.gather(pl, u, i + 1)
                    scatter(i, u)
            for u in range(2):
                scatter(PAIRS, u)
            for u in range(2):
                pl.wait_ge(*scattered[u].done(PAIRS))

        @block.tensor
        def _(pe):
            pe.wait_ge(weights_in, loaded)
            with pe.Fori(1, PAIRS + 1) as i:
                for u in range(2):
                    ga.multiply(pe, u, i, bank[u][0])
                for u in range(2):
                    pe.wait_ge(*x_ready[u].at(i))
                    turn_to_tokens(pe, bank[u][1], next_x[u], ident).then_inc(turned[u].sem, 1)
                for u in range(2):
                    pe.wait_ge(*norm.out[u].at(i))
                    turn_to_features(pe, bank[u][2], row[u], ident).then_inc(turned[u].sem, 1)
                for u in range(2):
                    pe.wait_ge(*h_ready[u].at(i))
                    product_features(pe, bank[u][3], w_self[:, :], h_f[u]).then_inc(self_mm[u].sem, 1)
                for u in range(2):
                    pe.wait_ge(*last_ready[u].at(i))
                    turn_to_tokens(pe, bank[u][2], last[u], ident).then_inc(turned[u].sem, 1)

        @block.scalar
        def _(act):
            act.wait_ge(weights_in, loaded)
            act.wait_ge(eps_set, 1)
            with act.Fori(1, PAIRS + 1) as i:
                for u in range(2):
                    norm.scalar_root(act, u, i, 0, eps)
                for u in range(2):
                    act.wait_ge(*stored[u].before(i))
                    norm.scalar_apply(act, u, i, 0, row[u], bank[u][1])
                for u in range(2):
                    g = down(i, u)
                    act.wait_ge(*norm.out[u].at(i))
                    act.dma_start(table_rows(s["table"][6], g), flat(row[u][:, :, :])).then_inc(stored[u].sem, 16)
                for u in range(2):
                    act.wait_ge(*turned[u].at(i, 3))
                    act.wait_ge(*scattered[u].before(i))
                    act.activation(flat(out_row[u][:, :, :]), flat(bank[u][2][:, :, :]), ACT.Copy
                                   ).then_inc(out_ready[u].sem, 1)
            for u in range(2):
                act.wait_ge(*stored[u].done(PAIRS))

        @block.vector
        def _(dve):
            dve.memset(eps[:, :], EPS).then_inc(eps_set, 1)
            ga.zero(dve)
            dve.wait_ge(weights_in, loaded)
            with dve.Fori(1, PAIRS + 1) as i:
                for u in range(2):
                    ga.collect(dve, u, i, bank[u][0])
                for u in range(2):
                    dve.wait_ge(*ga.carry[u].done(i))
                    dve.wait_ge(*own_in[u].done(i))
                    dve.tensor_tensor(both[u][:, :, :], ga.sums[u][:, :, :], own[u][:, :, :], ALU.add
                                      ).then_inc(both_ready[u].sem, 1)
                for u in range(2):
                    dve.wait_ge(*both_ready[u].at(i))
                    dve.tensor_tensor(mean[u][:, :, :], both[u][:, :, :], root[u][:, :, :], ALU.mult
                                      ).then_inc(mean_ready[u].sem, 1)
                for u in range(2):
                    dve.wait_ge(*mean_ready[u].at(i))
                    dve.scalar_tensor_tensor(out=flat(next_x[u][:, :, :]), in0=flat(mean[u][:, :, :]),
                                             scalar=b_2[:, :], in1=flat(x_f[u][:, :, :]), op0=ALU.add,
                                             op1=ALU.add).then_inc(x_ready[u].sem, 1)
                for u in range(2):
                    dve.wait_ge(*turned[u].at(i, 1))
                    norm.vector_stats(dve, u, i, 0, bank[u][1])
                for u in range(2):
                    norm.vector_scale(dve, u, i, 0)
                for u in range(2):
                    dve.wait_ge(*turned[u].at(i, 2))
                    dve.tensor_copy(flat(h_f[u][:, :, :]), flat(bank[u][2][:, :, :])).then_inc(h_ready[u].sem, 1)
                for u in range(2):
                    dve.wait_ge(*self_mm[u].at(i))
                    dve.tensor_tensor(last[u][:, :, :], bank[u][3][:, :, :], next_x[u][:, :, :], ALU.add
                                      ).then_inc(last_ready[u].sem, 1)
    ph.end()


def relations(nc, out, w, s):
    ph = Phase(nc, "relational")
    cell = ph.sb("cell", [1, 32])
    ident = ph.sb("ident", [P, P])
    bases, table = ph.sb("bases", [P, BASES, D]), ph.sb("coefficients", [REL, BASES])
    number = ph.sb("number", [REL, 1], I32)
    numberf = ph.sb("numberf", [REL, 1])
    idx, rows, row_f = ph.sbs("idx", [P, T], I32), ph.sbs("rows", [P, T, D]), ph.sbs("row_f", [P, T, P])
    message, total = ph.sbs("message", [P, T, D]), ph.sbs("total", [P, T, D])
    kind, one_hot = ph.sbs("kind", [REL, GROUP], I32), ph.sbs("one_hot", [REL, GROUP])
    source, source_col = ph.sbs("source", [P, GROUP], I32), ph.sbs("source_col", [P, T], I32)
    source_colf = ph.sbs("source_colf", [P, T])
    equal = ph.sbs("equal", [P, T, GROUP])
    coef = ph.sbs("coef", [P, T, BASES])
    add_row = ph.sbs("add_row", [P, T], I32)
    turn_bank = [ph.psum(f"turn_bank{u}", [P, T, P]) for u in range(2)]
    based = [ph.psum(f"based{u}", [P, BASES, D]) for u in range(2)]
    sum_bank = [ph.psum(f"sum_bank{u}", [P, T, P]) for u in range(2)]
    weights_in, number_set = ph.sem("weights_in"), ph.sem("number_set")
    kind_in, source_in = ph.pair("kind_in", unit=16), ph.pair("source_in", per=2, unit=16)
    idx_in, add_row_in = ph.pair("idx_in", unit=16), ph.pair("add_row_in", unit=16)
    rows_in = ph.pair("rows_in", per=T, unit=16, soft=True)
    hot_ready = ph.pair("hot_ready", primed=True)
    source_f, equal_ready = ph.pair("source_f"), ph.pair("equal_ready", primed=True)
    coef_mm, coef_ready = ph.pair("coef_mm"), ph.pair("coef_ready")
    turned, row_ready = ph.pair("turned", primed=True), ph.pair("row_ready")
    based_mm = ph.pair("based_mm", per=T)
    weighted = ph.pair("weighted", per=T * BASES)
    total_mm, total_ready = ph.pair("total_mm", primed=True), ph.pair("total_ready", primed=True)
    added = ph.pair("added", per=T, unit=16, primed=True, soft=True)
    WHAT = [(ident[:, :], w["ident"]), (bases[:, :, :], w["bases"].rearrange("b i o -> i b o")),
            (table[:, :], w["coefficients"])]
    loaded = 16 * len(WHAT)
    with nc.Block() as block:
        @block.sync
        def _(sp):
            ph.prime(sp, cell, w["ident"])
            load_weights(sp, weights_in, WHAT)
            with sp.Fori(1, PAIRS + 1) as i:
                for u in range(2):
                    g = down(i, u)
                    sp.wait_ge(*turned[u].before(i))
                    ph.stand(sp)
                    sp.dma_start(idx[u][:, :], group_of(s["end_rows"], g)[:, T:2 * T]).then_inc(idx_in[u].sem, 16)
                    sp.wait_ge(*hot_ready[u].before(i))
                    ph.stand(sp)
                    sp.dma_start(kind[u][:, :], over_partitions(s["edge_type"][bass.ds(g * GROUP, GROUP)], REL)
                                 ).then_inc(kind_in[u].sem, 16)
                    sp.wait_ge(*equal_ready[u].before(i))
                    ph.stand(sp)
                    sp.dma_start(source[u][:, :], over_partitions(s["src_line"][bass.ds(g * GROUP, GROUP)])
                                 ).then_inc(source_in[u].sem, 16)
                    sp.dma_start(source_col[u][:, :], group_of(s["src_cols"], g)).then_inc(source_in[u].sem, 16)
                    sp.wait_ge(*added[u].before(i))
                    ph.stand(sp)
                    sp.dma_start(add_row[u][:, :], group_of(s["add_rows"], g)).then_inc(add_row_in[u].sem, 16)

        @block.gpsimd
        def _(pl):
            ph.prime(pl, cell, w["ident"], soft=True)
            pl.iota(number[:, :], pattern=[[0, 1]], base=0, channel_multiplier=1).then_inc(number_set, 1)

            def gather(i, u):
                pl.wait_ge(*idx_in[u].at(i))
                pl.wait_ge(*turned[u].before(i))
                ph.stand(pl)
                for t in range(T):
                    pl.indirect_dma_start(rows[u][:, t, :], None, s["table"][6],
                                          bass.IndirectOffsetOnAxis(ap=idx[u][:, t:t + 1], axis=0)
                                          ).then_inc(rows_in[u].sem, 16)

            def add(i, u):
                pl.wait_ge(*add_row_in[u].at(i))
                pl.wait_ge(*total_ready[u].at(i))
                pl.wait_ge(*(added[0].done(i) if u else added[1].before(i)))
                ph.stand(pl)
                for t in range(T):
                    pl.indirect_dma_start(
                        out, bass.IndirectOffsetOnAxis(ap=add_row[u][:, t:t + 1], axis=0), total[u][:, t, :],
                        None, compute_op=ALU.add).then_inc(added[u].sem, 16)

            for u in range(2):
                gather(1, u)
            with pl.Fori(1, PAIRS) as i:
                for u in range(2):
                    gather(i + 1, u)
                    add(i, u)
            for u in range(2):
                add(PAIRS, u)
            for u in range(2):
                pl.wait_ge(*added[u].done(PAIRS))

        @block.tensor
        def _(pe):
            pe.wait_ge(weights_in, loaded)
            with pe.Fori(1, PAIRS + 1) as i:
                for u in range(2):
                    pe.wait_ge(*rows_in[u].done(i))
                    turn_to_features(pe, turn_bank[u], rows[u], ident).then_inc(turned[u].sem, 1)
                    pe.wait_ge(*hot_ready[u].at(i))
                    pe.wait_ge(*total_ready[u].before(i))
                    for t in range(T):
                        ins = pe.matmul(sum_bank[u][:, t, 0:BASES], one_hot[u][:, t * P:(t + 1) * P],
                                        table[:, :], start=True, stop=True)
                    ins.then_inc(coef_mm[u].sem, 1)
                for t in range(T):
                    for u in range(2):
                        if t == 0:
                            pe.wait_ge(*row_ready[u].at(i))
                        else:
                            pe.wait_ge(*weighted[u].at(i, t * BASES))
                        for half in range(2):
                            ins = pe.matmul(based[u][:, 4 * half:4 * half + 4, :], row_f[u][:, t, :],
                                            bases[:, 4 * half:4 * half + 4, :], start=True, stop=True)
                        ins.then_inc(based_mm[u].sem, 1)
                for u in range(2):
                    pe.wait_ge(*equal_ready[u].at(i))
                    pe.wait_ge(*weighted[u].done(i))
                    for t in range(T):
                        for a in range(T):
                            ins = pe.matmul(sum_bank[u][:, t, :], equal[u][:, a, t * P:(t + 1) * P],
                                            message[u][:, a, :], start=(a == 0), stop=(a == T - 1))
                    ins.then_inc(total_mm[u].sem, 1)

        @block.scalar
        def _(act):
            with act.Fori(1, PAIRS + 1) as i:
                for u in range(2):
                    act.wait_ge(*source_in[u].done(i))
                    act.wait_ge(*equal_ready[u].before(i))
                    act.activation(source_colf[u][:, :], source_col[u][:, :], ACT.Copy
                                   ).then_inc(source_f[u].sem, 1)
                for u in range(2):
                    act.wait_ge(*coef_mm[u].at(i))
                    act.activation(coef[u][:, :, :], sum_bank[u][:, :, 0:BASES], ACT.Copy
                                   ).then_inc(coef_ready[u].sem, 1)
                for u in range(2):
                    act.wait_ge(*total_mm[u].at(i))
                    act.wait_ge(*added[u].before(i))
                    act.activation(flat(total[u][:, :, :]), flat(sum_bank[u][:, :, :]), ACT.Copy
                                   ).then_inc(total_ready[u].sem, 1)

        @block.vector
        def _(dve):
            dve.wait_ge(number_set, 1)
            dve.tensor_copy(numberf[:, :], number[:, :]).then_inc(number_set, 1)
            dve.wait_ge(number_set, 2)
            with dve.Fori(1, PAIRS + 1) as i:
                for u in range(2):
                    dve.wait_ge(*kind_in[u].at(i))
                    dve.tensor_scalar(one_hot[u][:, :], kind[u][:, :], numberf[:, :], None, ALU.is_equal
                                      ).then_inc(hot_ready[u].sem, 1)
                    dve.wait_ge(*source_f[u].at(i))
                    dve.wait_ge(*total_mm[u].before(i))
                    for a in range(T):
                        ins = dve.tensor_scalar(equal[u][:, a, :], source[u][:, :], source_colf[u][:, a:a + 1],
                                                None, ALU.is_equal)
                    ins.then_inc(equal_ready[u].sem, 1)
                for u in range(2):
                    dve.wait_ge(*turned[u].at(i))
                    dve.tensor_copy(flat(row_f[u][:, :, :]), flat(turn_bank[u][:, :, :])
                                    ).then_inc(row_ready[u].sem, 1)
                for t in range(T):
                    for u in range(2):
                        if t == 0:
                            dve.wait_ge(*coef_ready[u].at(i))
                        dve.wait_ge(*based_mm[u].at(i, t + 1))
                        dve.tensor_scalar(message[u][:, t, :], based[u][:, 0, :], coef[u][:, t, 0:1], None,
                                          ALU.mult).then_inc(weighted[u].sem, 1)
                    for b in range(1, BASES):
                        for u in range(2):
                            dve.wait_ge(*weighted[u].at(i, t * BASES + b))
                            dve.scalar_tensor_tensor(out=message[u][:, t, :], in0=based[u][:, b, :],
                                                     scalar=coef[u][:, t, b:b + 1], in1=message[u][:, t, :],
                                                     op0=ALU.mult, op1=ALU.add).then_inc(weighted[u].sem, 1)
    ph.end()


def gnn(nc, x, out, w, s):
    edge_structure(nc, w, s)
    dense_chain(nc, x, out, w, s)
    for level in range(2):
        attend_edges(nc, w, s, level)
        attend_nodes(nc, w, s, level)
    sage_hidden(nc, w, s)
    sage_out(nc, w, s)
    gcn_hidden(nc, w, s)
    gcn_out(nc, out, w, s)
    relations(nc, out, w, s)


def lay_out(np, inputs):
    def padded(a, fill, before=0, after=0):
        line = np.full(before + SLOTS + after, fill, np.int32)
        line[before:before + E] = a
        return line

    def by_group(line):
        return line.reshape(NG, T, P).transpose(0, 2, 1)

    src, dst = np.asarray(inputs["src"]), np.asarray(inputs["dst"])
    line = padded(dst, N, 1, 1)
    line[0] = line[-1] = -1
    slot = np.arange(SLOTS, dtype=np.int32).reshape(NG, P, T)
    heads = np.repeat(np.eye(HEADS, dtype=np.float32), D // HEADS, axis=1)
    arrays = {
        "x": inputs["x"], "dst_line": line, "dst_cols": by_group(line[1:-1]),
        "dst_around": np.concatenate([by_group(line[1:-1]), by_group(line[:-2])], axis=2),
        "edge_ends": np.concatenate([by_group(padded(src, 0)), by_group(padded(dst, dst[-1]))], axis=2),
        "src_line": padded(src, OUT_ROWS - 1), "src_cols": by_group(padded(src, OUT_ROWS - 1)),
        "spare_rows": np.arange(N, N + GROUP, dtype=np.int32).reshape(T, P).T,
        "before": np.triu(np.ones((P, P), np.float32), 1),
        "slot_rows": slot, "edge_type": padded(np.asarray(inputs["edge_type_16"]), 0),
        "ident": np.eye(P, dtype=np.float32), "ones": np.ones((P, P), np.float32),
        "head_row": heads, "head_sum": heads.T * np.float32((D // HEADS) ** -0.5),
    }
    for name, a in inputs.items():
        if name.startswith("L"):
            arrays[name.split("_gnn_")[1]] = a
    arrays["w_self"] = np.asarray(inputs["L3_gnn_w_self"]).T
    return {k: np.ascontiguousarray(a) for k, a in arrays.items()}


def kernel(**inputs):
    import numpy as np
    import concourse.bacc as bacc
    from concourse.bass_utils import run_bass_kernel_spmd

    nc = bacc.Bacc("TRN2", target_bir_lowering=False, num_devices=1)
    arrays = lay_out(np, inputs)
    w = {k: nc.dram_tensor(f"in_{k}", a.shape, mybir.dt.from_np(a.dtype), kind="ExternalInput").ap()
         for k, a in arrays.items()}
    out = nc.dram_tensor("out_x", (OUT_ROWS, D), F32, kind="ExternalOutput").ap()

    def scratch(name, shape, dtype=F32):
        return nc.dram_tensor(name, shape, dtype, kind="Internal").ap()

    s = {k: w[k] for k in ("dst_line", "dst_cols", "dst_around", "edge_ends", "slot_rows", "edge_type", "src_line",
                           "src_cols")}
    s["table"] = {n: scratch(f"table{n}", (ROWS if n < 6 else SLOTS, D)) for n in range(1, 7)}
    s["row_of_node"] = scratch("row_of_node", (N, 1), I32)
    s["put_rows"] = scratch("put_rows", (NG, P, T), I32)
    s["add_rows"] = scratch("add_rows", (NG, P, T), I32)
    s["end_rows"] = scratch("end_rows", (NG, P, 2 * T), I32)
    s["same"] = scratch("same_runs", (NG, P, 2 * GROUP))
    s["masks"] = scratch("run_masks", (NG, HEADS, 2 * GROUP))
    s["logit"] = scratch("logits", (NG, HEADS, 2 * GROUP))
    s["degrees"] = scratch("degrees", (NG, 1, 2 * GROUP))
    for name in ("h_f", "x_f", "g_f", "x1_f", "value"):
        s[name] = scratch(f"slots_{name}", (NG, P, GROUP))
    s["x_ends"] = [scratch(f"x_ends{k}", (NG, P, GROUP)) for k in range(2)]
    gnn(nc, w["x"], out, w, s)
    r = run_bass_kernel_spmd(nc, [{f"in_{k}": a for k, a in arrays.items()}], core_ids=[0])
    return r.results[0]["out_x"][:N]
```

```python
from contextlib import ExitStack

import concourse.bass as bass
from concourse import mybir

F32 = mybir.dt.float32
I32 = mybir.dt.int32
ALU = mybir.AluOpType
ACT = mybir.ActivationFunctionType

N = 50000
E = 25000
D = 128
P = 128
T = 4
GROUP = T * P
CHAINS = 4
NG = -(-E // (CHAINS * GROUP)) * CHAINS
SLOTS = NG * GROUP
ROWS = SLOTS + N
NODE_TURNS = -(-N // (CHAINS * GROUP))
NODE_ENDS = -(-N // GROUP) - (NODE_TURNS - 1) * CHAINS
NODE_TAIL = (N - ((NODE_TURNS - 1) * CHAINS + NODE_ENDS - 1) * GROUP) // T
HEADS = 4
REL = 16
BASES = 8
FAR = 1e30
NO_ROW = 100000.0
OUT_ROWS = N + GROUP + 1
EPS = 1e-5
SOFT_EPS = 1e-16


class Count:

    def __init__(self, sem, per, unit, primed):
        self.sem, self.unit, self.per, self.primed = sem, unit, per * unit, per * unit if primed else 0

    def at(self, i, k=1):
        return self.sem, i * self.per + (self.primed - self.per + k * self.unit)

    def done(self, i):
        return self.sem, i * self.per + self.primed

    def before(self, i):
        assert self.primed > 0
        return self.sem, i * self.per + (self.primed - self.per)


class Phase:

    def __init__(self, nc, name, chains=CHAINS, late_first=False):
        self.nc, self.name, self.stack, self.sems, self.counts = nc, name, ExitStack(), [], []
        self.chains, self.turns = range(chains), NG // chains
        self.order = list(reversed(self.chains) if late_first else self.chains)
        self.waits_stood = self.sem("waits_stood")

    def sb(self, name, shape, dtype=F32):
        return self.stack.enter_context(self.nc.sbuf_tensor(f"{self.name}_{name}", shape, dtype))

    def psum(self, name, shape):
        return self.stack.enter_context(self.nc.psum_tensor(f"{self.name}_{name}", shape, F32))

    def sbs(self, name, shape, dtype=F32):
        return [self.sb(f"{name}{u}", shape, dtype) for u in self.chains]

    def banks(self):
        return [[self.psum(f"bank{u}{k}", [P, T, P]) for k in range(8 // len(self.chains))]
                for u in self.chains]

    def down(self, i, u):
        return (NG + len(self.chains) - 1 - u) - len(self.chains) * i

    def up(self, i, u):
        return len(self.chains) * i + (u - len(self.chains))

    def sem(self, name):
        s = self.nc.alloc_semaphore(f"{self.name}_{name}")
        self.sems.append(s)
        return s

    def each(self, name, per=1, unit=1, primed=False, soft=False):
        all_chains = [Count(self.sem(f"{name}{u}"), per, unit, primed) for u in self.chains]
        if primed:
            self.counts += [(c, soft) for c in all_chains]
        return all_chains

    def walk(self, eng, steps, step):
        lag = [u * steps // len(self.chains) for u in self.chains]

        def turn(i, last, now):
            for k in range(1, steps + 1):
                for u in self.order:
                    if k > lag[u] and now:
                        step(k - lag[u], i, u)
                    if k <= lag[u] and last:
                        step(k - lag[u] + steps, i - 1, u)

        turn(1, False, True)
        with eng.Fori(2, self.turns + 1) as i:
            turn(i, True, True)
        turn(self.turns + 1, True, False)

    def ahead_and_behind(self, eng, early, late):
        half = len(self.chains) // 2

        def turn(i, last, following):
            for u in self.chains:
                if following:
                    early(i + 1, u)
                if u >= half:
                    late(i, u - half)
                elif last:
                    late(i - 1, u + half)

        for u in self.chains:
            early(1, u)
        turn(1, False, True)
        with eng.Fori(2, self.turns) as i:
            turn(i, True, True)
        turn(self.turns, True, False)
        for u in range(half):
            late(self.turns, u + half)

    def stand(self, eng):
        eng.sem_inc(self.waits_stood, 1)

    def prime(self, eng, cell, anything, soft=False):
        for n, (c, by_gpsimd) in enumerate(self.counts):
            if by_gpsimd != soft:
                continue
            if c.unit == 16:
                eng.dma_start(cell[0:1, n:n + 1], anything[0:1, n:n + 1]).then_inc(c.sem, c.primed)
            else:
                eng.sem_inc(c.sem, c.primed)

    def end(self):
        self.stack.close()
        self.nc.clear_and_free_semaphores(self.sems)
        self.nc.all_engine_barrier()



class Norm:

    def __init__(self, ph, per=1, name="norm"):
        self.stats = ph.sbs(f"{name}_stats", [P, T, 6])
        self.part = ph.sbs(f"{name}_part", [P, 5, T])
        self.deviation = ph.sbs(f"{name}_deviation", [P, T])
        self.scale = ph.sbs(f"{name}_scale", [P, T])
        self.shift = ph.sbs(f"{name}_shift", [P, T])
        self.step = ph.each(f"{name}_step", per=6 * per)
        self.root = ph.each(f"{name}_root", per=per)
        self.out = ph.each(f"{name}_out", per=per)

    def vector_stats(self, dve, u, i, k, src, w=P):
        st, part, step = self.stats[u], self.part[u], self.step[u]
        for j in range(T):
            ins = dve.bn_stats(st[:w, j, :], src[:w, j, :])
        ins.then_inc(step.sem, 1)
        dve.wait_ge(*step.at(i, 6 * k + 1))
        dve.tensor_tensor(part[:w, 0, :], st[:w, :, 1], st[:w, :, 4], ALU.add)
        dve.tensor_tensor(part[:w, 1, :], st[:w, :, 1], st[:w, :, 4], ALU.subtract)
        dve.tensor_tensor(part[:w, 2, :], st[:w, :, 2], st[:w, :, 5], ALU.add).then_inc(step.sem, 1)
        dve.wait_ge(*step.at(i, 6 * k + 2))
        dve.scalar_tensor_tensor(out=part[:w, 3, :], in0=part[:w, 1, :], scalar=0.25,
                                 in1=part[:w, 1, :], op0=ALU.mult, op1=ALU.mult).then_inc(step.sem, 1)
        dve.wait_ge(*step.at(i, 6 * k + 3))
        dve.scalar_tensor_tensor(out=part[:w, 4, :], in0=part[:w, 2, :], scalar=1.0 / D,
                                 in1=part[:w, 3, :], op0=ALU.mult, op1=ALU.add).then_inc(step.sem, 1)

    def scalar_root(self, act, u, i, k, eps, w=P):
        act.wait_ge(*self.step[u].at(i, 6 * k + 4))
        act.activation(self.deviation[u][:w, :], self.part[u][:w, 4, :], ACT.Sqrt,
                       bias=eps[:w, :]).then_inc(self.root[u].sem, 1)

    def vector_scale(self, dve, u, i, k, w=P):
        step = self.step[u]
        dve.wait_ge(*self.root[u].at(i, k + 1))
        dve.reciprocal(self.scale[u][:w, :], self.deviation[u][:w, :]).then_inc(step.sem, 1)
        dve.wait_ge(*step.at(i, 6 * k + 5))
        dve.scalar_tensor_tensor(out=self.shift[u][:w, :], in0=self.part[u][:w, 0, :], scalar=-0.5,
                                 in1=self.scale[u][:w, :], op0=ALU.mult,
                                 op1=ALU.mult).then_inc(step.sem, 1)

    def scalar_apply(self, act, u, i, k, dst, src, w=P):
        act.wait_ge(*self.step[u].at(i, 6 * k + 6))
        for j in range(T):
            ins = act.activation(dst[:w, j, :], src[:w, j, :], ACT.Relu, bias=self.shift[u][:w, j:j + 1],
                                 scale=self.scale[u][:w, j:j + 1])
        ins.then_inc(self.out[u].sem, 1)



def turn_to_features(pe, bank, tokens, ident, w=P):
    for j in range(T):
        ins = pe.transpose(bank[:, j, :w], tokens[:w, j, :], ident[:w, :w])
    return ins


def turn_to_tokens(pe, bank, features, ident, w=P):
    for j in range(T):
        ins = pe.transpose(bank[:w, j, :], features[:, j, :w], ident[:, :])
    return ins


def product_features(pe, bank, weight, features, start=True, stop=True, w=P):
    return pe.matmul(bank[:, :, :w], weight, features[:, :, :w], start=start, stop=stop)


def product_tokens(pe, bank, features, weight, w=P):
    for j in range(T):
        ins = pe.matmul(bank[:w, j, :], features[:, j, :w], weight, start=True, stop=True)
    return ins


def sum_over_runs(pe, bank, tokens, same):
    for t in range(T):
        ins = pe.matmul(bank[:, t, :], tokens[:, t, :], same[:, 0, t, :], start=True, stop=True)
    return ins


def add_carry(dve, out, bank, same, carry, u, i):
    for n, t in enumerate(reversed(range(T))):
        if n:
            dve.wait_ge(*carry[u].at(i, n))
            col = out[u][:, t + 1, 0:1]
        elif u:
            dve.wait_ge(*carry[u - 1].done(i))
            col = out[u - 1][:, 0, 0:1]
        else:
            dve.wait_ge(*carry[-1].before(i))
            col = out[-1][:, 0, 0:1]
        dve.scalar_tensor_tensor(out=out[u][:, t, :], in0=same[:, 1, t, :], scalar=col,
                                 in1=bank[:, t, :], op0=ALU.mult, op1=ALU.add).then_inc(carry[u].sem, 1)


def last_of(signal, u, i):
    return signal[u - 1].done(i) if u else signal[-1].before(i)


def group_of(dram, g):
    return dram[bass.ds(g, 1)].rearrange("o p f -> (o p) f")


def table_rows(table, g):
    return table[bass.ds(g * GROUP, GROUP), :].rearrange("(p j) d -> p (j d)", j=T)


def flat(x):
    return x.rearrange("p j d -> p (j d)")


def load_weights(eng, sem, what):
    for to, of in what:
        eng.dma_start(to, of).then_inc(sem, 16)
    return 16 * len(what)


def column(vector):
    return vector.rearrange("(p o) -> p o", o=1)


def over_partitions(vector, n=P):
    return vector.partition_broadcast(n)



def edge_structure(nc, w, s):
    ph = Phase(nc, "edges")
    cell = ph.sb("cell", [1, P])
    one_col = ph.sb("ones", [P, P])
    row = ph.sbs("dst_row", [P, GROUP + 2], I32)
    col = ph.sbs("dst_col", [P, T], I32)
    rowf = ph.sbs("dst_rowf", [P, GROUP + 2])
    colf = ph.sbs("dst_colf", [P, T])
    same = ph.sbs("same", [P, 2, T, P])
    mask = ph.sbs("mask", [HEADS, 2, GROUP])
    differ = ph.sbs("differ", [HEADS, 2, GROUP])
    deg = ph.sbs("deg", [P, T, P])
    ident = ph.sb("ident", [P, P])
    clip_root = ph.sbs("clip_root", [P, 2, T])
    inverse = ph.sbs("inverse", [P, 2, T])
    deg_row = ph.sbs("deg_row", [2 * T, P])
    around = ph.sbs("around", [P, 3, T], I32)
    put = ph.sbs("put", [P, T], I32)
    hit = ph.sbs("hit", [P, T])
    slot_id = ph.sbs("slot_id", [P, T], I32)
    start_rows = ph.sb("start_rows", [N // 400, 400], I32)
    before = ph.sb("before", [P, P])
    spare = ph.sb("spare", [P, T], I32)
    source = ph.sbs("source", [P, GROUP], I32)
    source_col = ph.sbs("source_col", [P, T], I32)
    source_colf = ph.sbs("source_colf", [P, T])
    equal = ph.sbs("equal", [P, T, GROUP])
    equal_before = ph.sbs("equal_before", [P, T, P])
    repeated = ph.sbs("repeated", [P, T])
    to_spare = ph.sbs("to_spare", [P, T])
    offset = ph.sbs("offset", [P, T])
    add_row = ph.sbs("add_row", [P, T], I32)
    bank = ph.banks()
    source_in = ph.each("source_in", per=2, unit=16)
    source_f = ph.each("source_f")
    equal_made = ph.each("equal_made", per=2, primed=True)
    repeats_mm = ph.each("repeats_mm", primed=True)
    adds = ph.each("adds", per=2, primed=True)
    adds_out = ph.each("adds_out", unit=16, primed=True)
    spared = ph.each("spared")

    ones_in = ph.sem("ones_in")
    row_in = ph.each("row_in", per=2, unit=16)
    rows_f = ph.each("rows_f", primed=True)
    same_made = ph.each("same_made", primed=True)
    mask_made = ph.each("mask_made", primed=True)
    deg_mm = ph.each("deg_mm")
    carry = ph.each("deg_carry", per=T, primed=True)
    clipped = ph.each("clipped")
    rooted = ph.each("rooted")
    deg_turned = ph.each("deg_turned", per=2)
    inverted = ph.each("inverted")
    degs = ph.each("degs", primed=True)
    same_out = ph.each("same_out", per=3, unit=16, primed=True)
    around_in = ph.each("around_in", per=2, unit=16)
    hits = ph.each("hits")
    puts = ph.each("puts", primed=True)
    put_out = ph.each("put_out", unit=16, primed=True, soft=True)
    slots_in = ph.each("slots_in", per=4, unit=16, primed=True, soft=True)
    rows_made = ph.sem("rows_made")
    rows_out = ph.sem("rows_out")
    turns = ph.sem("scatter_turns")

    with nc.Block() as block:
        @block.sync
        def _(sp):
            ph.prime(sp, cell, w["ident"])
            sp.dma_start(one_col[:, :], w["ones"]).then_inc(ones_in, 16)
            sp.dma_start(before[:, :], w["before"]).then_inc(ones_in, 16)
            sp.dma_start(ident[:, :], w["ident"]).then_inc(ones_in, 16)
            sp.dma_start(spare[:, :], w["spare_rows"]).then_inc(ones_in, 16)
            with sp.Fori(1, ph.turns + 1) as i:
                for u in ph.chains:
                    g = ph.down(i, u)
                    sp.wait_ge(*rows_f[u].before(i))
                    ph.stand(sp)
                    sp.dma_start(row[u][:, :], over_partitions(s["dst_line"][bass.ds(g * GROUP, GROUP + 2)])
                                 ).then_inc(row_in[u].sem, 16)
                    sp.dma_start(col[u][:, :], group_of(s["dst_cols"], g)).then_inc(row_in[u].sem, 16)
                    sp.wait_ge(*puts[u].before(i))
                    ph.stand(sp)
                    sp.wait_ge(*slots_in[u].before(i))
                    ph.stand(sp)
                    sp.dma_start(around[u][:, 0:2, :], group_of(s["dst_around"], g)
                                 .rearrange("p (a j) -> p a j", a=2)).then_inc(around_in[u].sem, 16)
                    sp.dma_start(slot_id[u][:, :], group_of(s["slot_rows"], g)).then_inc(around_in[u].sem, 16)
                    sp.wait_ge(*adds[u].before(i))
                    ph.stand(sp)
                    sp.dma_start(source[u][:, :], over_partitions(s["src_line"][bass.ds(g * GROUP, GROUP)])
                                 ).then_inc(source_in[u].sem, 16)
                    sp.dma_start(source_col[u][:, :], group_of(s["src_cols"], g)).then_inc(source_in[u].sem, 16)

        @block.scalar
        def _(act):
            act.wait_ge(ones_in, 64)
            def step(k, i, u):
                if k == 1:
                    act.wait_ge(*row_in[u].done(i))
                    act.wait_ge(*same_made[u].before(i))
                    act.activation(colf[u][:, :], col[u][:, :], ACT.Copy)
                    act.activation(rowf[u][:, :], row[u][:, :], ACT.Copy).then_inc(rows_f[u].sem, 1)
                    act.wait_ge(*source_in[u].done(i))
                    act.wait_ge(*equal_made[u].before(i))
                    act.activation(source_colf[u][:, :], source_col[u][:, :], ACT.Copy
                                   ).then_inc(source_f[u].sem, 1)
                elif k == 2:
                    act.wait_ge(*same_made[u].at(i))
                    act.wait_ge(*same_out[u].before(i))
                    act.activation(mask[u][:, :, :].rearrange("p a d -> p (a d)"),
                                   differ[u][:, :, :].rearrange("p a d -> p (a d)"), ACT.Copy, scale=-FAR
                                   ).then_inc(mask_made[u].sem, 1)
                elif k == 5:
                    act.wait_ge(*clipped[u].at(i))
                    act.activation(clip_root[u][:, 1, :], bank[u][0][:, :, 0], ACT.Sqrt,
                                   bias=one_col[:, 0:1]).then_inc(rooted[u].sem, 1)
                elif k == 7:
                    act.wait_ge(*deg_turned[u].at(i, 2))
                    act.wait_ge(*same_out[u].before(i))
                    act.activation(deg_row[u][:, :], bank[u][0][0:2 * T, 0, :], ACT.Copy
                                   ).then_inc(degs[u].sem, 1)
                elif k == 8:
                    g = ph.down(i, u)
                    act.dma_start(group_of(s["same"], g), same[u][:, :, :, :].rearrange("p a j d -> p (a j d)")
                                  ).then_inc(same_out[u].sem, 16)
                    act.wait_ge(*mask_made[u].at(i))
                    act.dma_start(group_of(s["masks"], g), mask[u][:, :, :].rearrange("p a d -> p (a d)")
                                  ).then_inc(same_out[u].sem, 16)
                    act.wait_ge(*degs[u].at(i))
                    act.dma_start(group_of(s["degrees"], g), deg_row[u][:, :]).then_inc(same_out[u].sem, 16)
                    act.wait_ge(*adds[u].done(i))
                    act.dma_start(group_of(s["add_rows"], g), add_row[u][:, :]).then_inc(adds_out[u].sem, 16)

            ph.walk(act, 8, step)
            for u in ph.chains:
                act.wait_ge(*same_out[u].done(ph.turns))
                act.wait_ge(*adds_out[u].done(ph.turns))

        @block.tensor
        def _(pe):
            pe.wait_ge(ones_in, 64)
            def step(k, i, u):
                if k == 2:
                    pe.wait_ge(*same_made[u].at(i))
                    pe.wait_ge(*degs[u].before(i))
                    product_features(pe, bank[u][0], one_col[:, :], same[u][:, 0, :, :]
                                     ).then_inc(deg_mm[u].sem, 1)
                elif k == 3:
                    pe.wait_ge(*equal_made[u].done(i))
                    pe.wait_ge(*adds[u].before(i))
                    for t in range(T):
                        for a in range(t):
                            pe.matmul(bank[u][1][:, t, 0:1], equal[u][:, a, t * P:(t + 1) * P],
                                      one_col[:, 0:1], start=(a == 0), stop=False)
                        ins = pe.matmul(bank[u][1][:, t, 0:1], equal_before[u][:, t, :], one_col[:, 0:1],
                                        start=(t == 0), stop=True)
                    ins.then_inc(repeats_mm[u].sem, 1)
                elif k == 4:
                    pe.wait_ge(*carry[u].done(i))
                    for t in range(T):
                        ins = pe.matmul(bank[u][0][:, t, 0:1], deg[u][:, t, :], ident[:, 0:1], start=True,
                                        stop=True)
                    ins.then_inc(deg_turned[u].sem, 1)
                elif k == 6:
                    pe.wait_ge(*inverted[u].at(i))
                    pe.transpose(bank[u][0][0:2 * T, 0, :], inverse[u][:, :, :].rearrange("p a j -> p (a j)"),
                                 ident[:, :]).then_inc(deg_turned[u].sem, 1)

            ph.walk(pe, 8, step)

        @block.vector
        def _(dve):
            dve.memset(deg[-1][:, :, :], 0.0).then_inc(rows_made, 1)
            dve.wait_ge(rows_made, 1)
            dve.wait_ge(ones_in, 64)
            def step(k, i, u):
                if k == 1:
                    dve.wait_ge(*rows_f[u].at(i))
                    dve.wait_ge(*same_out[u].before(i))
                    for t in range(T):
                        line = rowf[u][:, 1 + t * P:1 + (t + 1) * P]
                        nxt = 1 + (t + 1) * P
                        dve.tensor_scalar(same[u][:, 0, t, :], line, colf[u][:, t:t + 1], None, ALU.is_equal)
                        dve.tensor_scalar(same[u][:, 1, t, :], line, rowf[u][:, nxt:nxt + 1], None,
                                          ALU.is_equal)
                    dve.wait_ge(*mask_made[u].before(i))
                    at = rowf[u][0:HEADS, 1:GROUP + 1]
                    dve.tensor_tensor(differ[u][:, 0, :], at, rowf[u][0:HEADS, 0:GROUP], ALU.not_equal)
                    dve.tensor_tensor(differ[u][:, 1, :], at, rowf[u][0:HEADS, 2:GROUP + 2],
                                      ALU.not_equal).then_inc(same_made[u].sem, 1)
                    dve.wait_ge(*around_in[u].done(i))
                    dve.wait_ge(*put_out[u].before(i))
                    dve.tensor_tensor(hit[u][:, :], around[u][:, 0, :], around[u][:, 1, :],
                                      ALU.is_equal).then_inc(hits[u].sem, 1)
                elif k == 2:
                    dve.wait_ge(*hits[u].at(i))
                    dve.scalar_tensor_tensor(out=put[u][:, :], in0=hit[u][:, :], scalar=NO_ROW,
                                             in1=around[u][:, 0, :], op0=ALU.mult, op1=ALU.add
                                             ).then_inc(puts[u].sem, 1)
                    dve.wait_ge(*source_f[u].at(i))
                    dve.wait_ge(*repeats_mm[u].before(i))
                    for a in range(T):
                        ins = dve.tensor_scalar(equal[u][:, a, :], source[u][:, :], source_colf[u][:, a:a + 1],
                                                None, ALU.is_equal)
                    ins.then_inc(equal_made[u].sem, 1)
                    dve.wait_ge(*equal_made[u].at(i, 1))
                    for a in range(T):
                        ins = dve.tensor_tensor(equal_before[u][:, a, :], equal[u][:, a, a * P:(a + 1) * P],
                                                before[:, :], ALU.mult)
                    ins.then_inc(equal_made[u].sem, 1)
                elif k == 3:
                    dve.wait_ge(*deg_mm[u].at(i))
                    add_carry(dve, deg, bank[u][0], same[u], carry, u, i)
                elif k == 4:
                    dve.wait_ge(*repeats_mm[u].at(i))
                    dve.wait_ge(*adds_out[u].before(i))
                    dve.tensor_scalar(repeated[u][:, :], bank[u][1][:, :, 0], 0.0, None, ALU.is_gt)
                    dve.tensor_tensor(to_spare[u][:, :], spare[:, :], source_col[u][:, :], ALU.subtract
                                      ).then_inc(adds[u].sem, 1)
                elif k == 5:
                    dve.wait_ge(*deg_turned[u].at(i, 1))
                    dve.tensor_scalar(clip_root[u][:, 0, :], bank[u][0][:, :, 0], 1.0, None, ALU.max
                                      ).then_inc(clipped[u].sem, 1)
                    dve.wait_ge(*adds[u].at(i, 1))
                    dve.tensor_tensor(offset[u][:, :], repeated[u][:, :], to_spare[u][:, :],
                                      ALU.mult).then_inc(spared[u].sem, 1)
                elif k == 6:
                    dve.wait_ge(*rooted[u].at(i))
                    dve.reciprocal(inverse[u][:, :, :], clip_root[u][:, :, :]).then_inc(inverted[u].sem, 1)
                    dve.wait_ge(*spared[u].at(i))
                    dve.tensor_tensor(add_row[u][:, :], offset[u][:, :], source_col[u][:, :],
                                      ALU.add).then_inc(adds[u].sem, 1)

            ph.walk(dve, 8, step)

        @block.gpsimd
        def _(pl):
            ph.prime(pl, cell, w["ident"], soft=True)
            pl.iota(start_rows[:, :], pattern=[[1, 400]], base=SLOTS, channel_multiplier=400
                    ).then_inc(rows_out, 1)
            pl.wait_ge(rows_out, 1)
            pl.dma_start(s["row_of_node"].rearrange("(p f) o -> p (f o)", p=N // 400), start_rows[:, :]
                         ).then_inc(turns, 16)
            pl.wait_ge(turns, 16)
            with pl.Fori(1, ph.turns + 1) as i:
                for u in ph.chains:
                    g = ph.down(i, u)
                    pl.wait_ge(*puts[u].at(i))
                    ph.stand(pl)
                    pl.dma_start(group_of(s["put_rows"], g), put[u][:, :]).then_inc(put_out[u].sem, 16)
                    for t in range(T):
                        pl.indirect_dma_start(
                            s["row_of_node"], bass.IndirectOffsetOnAxis(ap=put[u][:, t:t + 1], axis=0),
                            slot_id[u][:, t:t + 1], None, bounds_check=N - 1, oob_is_err=False
                        ).then_inc(slots_in[u].sem, 16)
            for u in ph.chains:
                pl.wait_ge(*slots_in[u].done(ph.turns))
                pl.wait_ge(*put_out[u].done(ph.turns))
    ph.end()



def dense_chain(nc, x, out, w, s):
    ph = Phase(nc, "dense", late_first=True)
    cell = ph.sb("cell", [1, P])
    ident = ph.sb("ident", [P, P])
    eps = ph.sb("eps", [P, 1])
    ws0, ws1, w1, w2 = (ph.sb(n, [P, D]) for n in ("ws0", "ws1", "w1", "w2"))
    w_self = ph.sb("w_self", [P, D])
    wr0 = ph.sb("wr0", [P, 2, D])
    w_lr = ph.sb("w_lr", [P, 2, 2 * D])
    b_s0, b_1 = ph.sb("b_s0", [P, 1]), ph.sb("b_1", [P, 1])
    b_l0 = ph.sb("b_l0", [P, 2])
    b_s1, b_l1, b_2 = (ph.sb(n, [P, D]) for n in ("b_s1", "b_l1", "b_2"))
    rate_row = ph.sb("rate_row", [P, D])
    x_in = ph.sbs("x_in", [P, T, D])
    xb = ph.sbs("xb", [P, T, D])
    xr = ph.sbs("xr", [P, T, D])
    h = ph.sbs("h", [P, T, D])
    h_f = ph.sbs("h_f", [P, T, P])
    g_f = ph.sbs("g_f", [P, T, P])
    g3_f = [[ph.sb(f"g3_f{u}{k}", [P, T, P]) for k in range(2)] for u in ph.chains]
    tab = {n: ph.sbs(f"tab{n}", [P, T, D]) for n in range(1, 8)}
    bank = ph.banks()
    norm = Norm(ph, 4)

    weights_in = ph.sem("weights_in")
    eps_set = ph.sem("eps_set")
    rate_steps = ph.sem("rate_steps")
    rates_set = ph.sem("rates_set")
    x_loaded = ph.each("x_loaded", unit=16)
    x_free = ph.each("x_free", primed=True)
    turned = ph.each("turned", per=4)
    h_ready = ph.each("h_ready", per=4)
    g1_mm, g1_ready = ph.each("g1_mm"), ph.each("g1_ready")
    xb_ready = ph.each("xb_ready", per=2)
    x1_mm = ph.each("x1_mm")
    x_ready = ph.each("x_ready", per=3)
    t1_turned, t1_ready = ph.each("t1_turned"), ph.each("t1_ready")
    g3_mm, g3_ready = ph.each("g3_mm", per=2), ph.each("g3_ready", per=2)
    lr_mm, t3_ready = ph.each("lr_mm", per=2), ph.each("t3_ready")
    w1_mm, t4_ready = ph.each("w1_mm", per=2), ph.each("t4_ready")
    g5_ready = ph.each("g5_ready")
    w2_mm, t5_ready = ph.each("w2_mm"), ph.each("t5_ready")
    self_mm, out_ready = ph.each("self_mm"), ph.each("out_ready", primed=True)
    stored = {n: ph.each(f"stored{n}", unit=16, primed=True) for n in (1, 2, 3, 4, 5, 7)}

    idx = ph.sbs("idx", [P, 2, T], I32)
    found = ph.sbs("found", [P, 2, T], I32)
    ends = [[ph.sb(f"ends{u}{k}", [P, T, D]) for k in range(2)] for u in ph.chains]
    idx_in = ph.each("idx_in", unit=16)
    gathered = ph.each("gathered", per=4 * T, unit=16)
    ends_out = ph.each("ends_out", per=3, unit=16, primed=True, soft=True)

    cw = {}
    WHAT = [(ident[:, :], w["ident"]), (ws0[:, :], w["s_w0"]), (ws1[:, :], w["s_w1"]), (w1[:, :], w["W1"]),
            (w2[:, :], w["W2"][0:D, :]), (w_self[:, :], w["w_self"]),
            (wr0[:, :, :].rearrange("p k d -> p (k d)"), w["Wr0"]),
            (w_lr[:, :, 0:D], w["Wl1"].rearrange("(k p) d -> p k d", p=P)),
            (w_lr[:, :, D:2 * D], w["Wr1"].rearrange("(k p) d -> p k d", p=P)),
            (b_s0[:, :], column(w["s_b0"])), (b_1[:, :], column(w["b1"])),
            (b_l0[:, 0:1], column(w["bl0"][0:D])), (b_l0[:, 1:2], column(w["bl0"][D:2 * D])),
            (b_s1[:, :], over_partitions(w["s_b1"])), (b_l1[:, :], over_partitions(w["bl1"])),
            (b_2[:, :], over_partitions(w["b2"]))]
    loaded = 16 * (len(WHAT) + 1)
    rate_mm = rate_row_steps(nc, ph, w, bank[0][0], weights_in, rate_steps)

    def rows(array, i, u, wd, base=0):
        return array[bass.ds(i * (CHAINS * GROUP) + (base + (u - CHAINS) * GROUP), T * wd), :] \
            .rearrange("(p j) d -> p (j d)", j=T)

    STEPS, LAG = 16, [5 * u for u in ph.chains]
    assert NODE_ENDS == 2
    FULL, LAST = {u: P for u in ph.chains}, {0: P, 1: NODE_TAIL}

    def walk(eng, step):
        def turn(i, last, now, following):
            for k in range(1, STEPS + 1):
                for u in ph.order:
                    if k > LAG[u] and u in now:
                        step(k - LAG[u], i, u, now[u], following.get(u))
                    if k <= LAG[u] and u in last:
                        step(k - LAG[u] + STEPS, i - 1, u, last[u], now.get(u))

        turn(1, {}, FULL, FULL)
        with eng.Fori(2, NODE_TURNS - 1) as i:
            turn(i, FULL, FULL, FULL)
        turn(NODE_TURNS - 1, FULL, FULL, LAST)
        turn(NODE_TURNS, FULL, LAST, {})
        turn(NODE_TURNS + 1, LAST, {}, {})

    with nc.Block() as block:
        @block.sync
        def _(sp):
            ph.prime(sp, cell, w["ident"])
            load_weights(sp, weights_in, WHAT)
            rate_mm["load"](sp)

            def load_x(i, u, wd):
                sp.wait_ge(*x_free[u].before(i))
                sp.dma_start(flat(x_in[u][:wd, :, :]), rows(x, i, u, wd)).then_inc(x_loaded[u].sem, 16)

            def store(n, ready, i, u, wd):
                sp.wait_ge(*ready)
                to = rows(out, i, u, wd) if n == 7 else rows(s["table"][n], i, u, wd, base=SLOTS)
                sp.dma_start(to, flat(tab[n][u][:wd, :, :])).then_inc(stored[n][u].sem, 16)

            def step(k, i, u, wd, next_wd):
                if k == 4 and next_wd:
                    load_x(i + 1, u, next_wd)
                elif k == 6:
                    store(1, t1_ready[u].at(i), i, u, wd)
                elif k == 7:
                    store(2, norm.out[u].at(i, 2), i, u, wd)
                elif k == 9:
                    store(3, t3_ready[u].at(i), i, u, wd)
                elif k == 12:
                    store(4, t4_ready[u].at(i), i, u, wd)
                elif k == 13:
                    store(5, t5_ready[u].at(i), i, u, wd)
                elif k == 16:
                    store(7, out_ready[u].at(i), i, u, wd)

            for u in ph.chains:
                load_x(1, u, P)
            walk(sp, step)
            for n in stored:
                for u in ph.chains:
                    sp.wait_ge(*stored[n][u].done(NODE_TURNS if u < NODE_ENDS else NODE_TURNS - 1))

        @block.tensor
        def _(pe):
            pe.wait_ge(weights_in, loaded)
            rate_mm["tensor"](pe)
            pe.wait_ge(rates_set, 1)

            def step(k, i, u, wd, _):
                if k == 2:
                    pe.wait_ge(*norm.out[u].at(i, 1))
                    turn_to_features(pe, bank[u][0], h[u], ident, wd).then_inc(turned[u].sem, 1)
                elif k == 3:
                    pe.wait_ge(*h_ready[u].at(i, 1))
                    pe.wait_ge(*out_ready[u].before(i))
                    product_features(pe, bank[u][1], ws0[:, :], h_f[u], w=wd).then_inc(g1_mm[u].sem, 1)
                elif k == 4:
                    pe.wait_ge(*g1_ready[u].at(i))
                    product_tokens(pe, bank[u][0], g_f[u], ws1[:, :], wd).then_inc(x1_mm[u].sem, 1)
                    turn_to_tokens(pe, bank[u][1], g_f[u], ident, wd).then_inc(t1_turned[u].sem, 1)
                elif k == 6:
                    pe.wait_ge(*norm.out[u].at(i, 2))
                    turn_to_features(pe, bank[u][0], tab[2][u], ident, wd).then_inc(turned[u].sem, 1)
                elif k == 7:
                    pe.wait_ge(*h_ready[u].at(i, 2))
                    pe.wait_ge(*t1_ready[u].at(i))
                    for c in range(2):
                        product_features(pe, bank[u][1 - c], wr0[:, c, :], h_f[u], w=wd
                                         ).then_inc(g3_mm[u].sem, 1)
                elif k == 8:
                    pe.wait_ge(*g3_ready[u].at(i, 2))
                    for b, side in ((0, 1), (1, 0)):
                        for j in range(T):
                            for c in range(2):
                                ins = pe.matmul(bank[u][b][:wd, j, :], g3_f[u][c][:, j, :wd],
                                                w_lr[:, c, side * D:(side + 1) * D], start=(c == 0),
                                                stop=(c == 1))
                        ins.then_inc(lr_mm[u].sem, 1)
                elif k == 10:
                    pe.wait_ge(*norm.out[u].at(i, 3))
                    turn_to_features(pe, bank[u][0], h[u], ident, wd).then_inc(turned[u].sem, 1)
                elif k == 11:
                    pe.wait_ge(*h_ready[u].at(i, 3))
                    pe.wait_ge(*t3_ready[u].at(i))
                    product_features(pe, bank[u][1], w1[:, :], h_f[u], w=wd).then_inc(w1_mm[u].sem, 1)
                    product_tokens(pe, bank[u][0], h_f[u], w1[:, :], wd).then_inc(w1_mm[u].sem, 1)
                elif k == 12:
                    pe.wait_ge(*g5_ready[u].at(i))
                    product_tokens(pe, bank[u][1], g_f[u], w2[:, :], wd).then_inc(w2_mm[u].sem, 1)
                elif k == 14:
                    pe.wait_ge(*norm.out[u].at(i, 4))
                    pe.wait_ge(*t4_ready[u].at(i))
                    turn_to_features(pe, bank[u][0], tab[6][u], ident, wd).then_inc(turned[u].sem, 1)
                elif k == 15:
                    pe.wait_ge(*h_ready[u].at(i, 4))
                    pe.wait_ge(*t5_ready[u].at(i))
                    product_tokens(pe, bank[u][1], h_f[u], w_self[:, :], wd).then_inc(self_mm[u].sem, 1)

            walk(pe, step)

        @block.scalar
        def _(act):
            act.wait_ge(eps_set, 1)
            act.wait_ge(weights_in, loaded)

            def relu(to, of, bias, wd):
                return act.activation(to[:, :, :wd], of[:, :, :wd], ACT.Relu, bias=bias)

            def copy(to, of, wd):
                return act.activation(flat(to[:wd, :, :]), flat(of[:wd, :, :]), ACT.Copy)

            def step(k, i, u, wd, _):
                n = k // 4
                if k % 4 == 1:
                    if n == 2:
                        act.wait_ge(*lr_mm[u].at(i, 2))
                        act.wait_ge(*stored[3][u].before(i))
                        copy(tab[3][u], bank[u][1], wd).then_inc(t3_ready[u].sem, 1)
                    norm.scalar_root(act, u, i, n, eps, wd)
                elif k % 4 == 2:
                    if n == 1:
                        act.wait_ge(*stored[2][u].before(i))
                    to = (h, tab[2], h, tab[6])[n][u]
                    norm.scalar_apply(act, u, i, n, to, x_in[u] if n == 0 else xr[u], wd)
                elif k == 4:
                    act.wait_ge(*g1_mm[u].at(i))
                    relu(g_f[u], bank[u][1], b_s0[:, :], wd).then_inc(g1_ready[u].sem, 1)
                elif k == 8:
                    for c in range(2):
                        act.wait_ge(*g3_mm[u].at(i, c + 1))
                        relu(g3_f[u][c], bank[u][1 - c], b_l0[:, c:c + 1], wd).then_inc(g3_ready[u].sem, 1)
                elif k == 12:
                    act.wait_ge(*w1_mm[u].at(i, 1))
                    relu(g_f[u], bank[u][1], b_1[:, :], wd).then_inc(g5_ready[u].sem, 1)
                    act.wait_ge(*w1_mm[u].at(i, 2))
                    act.wait_ge(*stored[4][u].before(i))
                    copy(tab[4][u], bank[u][0], wd).then_inc(t4_ready[u].sem, 1)

            walk(act, step)

        @block.vector
        def _(dve):
            dve.memset(eps[:, :], EPS).then_inc(eps_set, 1)
            dve.wait_ge(weights_in, loaded)
            rate_mm["vector"](dve, rate_row, rates_set)
            dve.wait_ge(rates_set, 1)

            def over_tiles(row, wd):
                return row[:wd, :].rearrange("p (o d) -> p o d", o=1).to_broadcast((wd, T, D))

            def add(to, a, b, wd):
                return dve.tensor_tensor(to[:wd, :, :], a, b, ALU.add)

            def step(k, i, u, wd, _):
                if k == 1:
                    dve.wait_ge(*x_loaded[u].at(i))
                    norm.vector_stats(dve, u, i, 0, x_in[u], wd)
                elif k in (5, 9):
                    dve.wait_ge(*(x1_mm[u].at(i) if k == 5 else lr_mm[u].at(i, 1)))
                    dve.wait_ge(*(x_free[u].at(i) if k == 5 else xb_ready[u].at(i, 1)))
                    add(xr[u], bank[u][0][:wd, :, :], xb[u][:wd, :, :], wd).then_inc(x_ready[u].sem, 1)
                    dve.wait_ge(*x_ready[u].at(i, k // 4))
                    norm.vector_stats(dve, u, i, k // 4, xr[u], wd)
                elif k == 13:
                    dve.wait_ge(*w2_mm[u].at(i))
                    dve.wait_ge(*stored[5][u].before(i))
                    add(tab[5][u], bank[u][1][:wd, :, :], over_tiles(rate_row, wd), wd
                        ).then_inc(t5_ready[u].sem, 1)
                    dve.wait_ge(*t5_ready[u].at(i))
                    dve.wait_ge(*xb_ready[u].at(i, 2))
                    add(xr[u], tab[5][u][:wd, :, :], xb[u][:wd, :, :], wd).then_inc(x_ready[u].sem, 1)
                    dve.wait_ge(*x_ready[u].at(i, 3))
                    norm.vector_stats(dve, u, i, 3, xr[u], wd)
                elif k % 4 == 2:
                    norm.vector_scale(dve, u, i, k // 4, wd)
                    if k == 6:
                        dve.wait_ge(*t1_turned[u].at(i))
                        dve.wait_ge(*stored[1][u].before(i))
                        dve.tensor_copy(flat(tab[1][u][:wd, :, :]), flat(bank[u][1][:wd, :, :])
                                        ).then_inc(t1_ready[u].sem, 1)
                elif k % 4 == 3:
                    dve.wait_ge(*turned[u].at(i, k // 4 + 1))
                    dve.tensor_copy(h_f[u][:, :, :wd], bank[u][0][:, :, :wd]).then_inc(h_ready[u].sem, 1)
                    if k == 3:
                        add(xb[u], x_in[u][:wd, :, :], over_tiles(b_s1, wd), wd).then_inc(x_free[u].sem, 1)
                    elif k < 15:
                        add(xb[u], xr[u][:wd, :, :], over_tiles(b_l1 if k == 7 else b_2, wd), wd
                            ).then_inc(xb_ready[u].sem, 1)
                elif k == 16:
                    dve.wait_ge(*self_mm[u].at(i))
                    dve.wait_ge(*stored[7][u].before(i))
                    add(tab[7][u], bank[u][1][:wd, :, :], xr[u][:wd, :, :], wd).then_inc(out_ready[u].sem, 1)

            walk(dve, step)

        @block.gpsimd
        def _(pl):
            ph.prime(pl, cell, w["ident"], soft=True)
            def load_indices(i, u):
                g = ph.up(i, u)
                pl.dma_start(idx[u][:, :, :].rearrange("p a j -> p (a j)"), group_of(s["edge_ends"], g)
                             ).then_inc(idx_in[u].sem, 16)

            for u in ph.chains:
                load_indices(1, u)

            def body(i, more):
                for u in ph.chains:
                    pl.wait_ge(*idx_in[u].at(i))
                    pl.wait_ge(*ends_out[u].before(i))
                    ph.stand(pl)
                    for t in range(T):
                        for to, of, k in ((found[u][:, 0, t:t + 1], s["row_of_node"], 0),
                                          (found[u][:, 1, t:t + 1], s["row_of_node"], 1),
                                          (ends[u][0][:, t, :], x, 0), (ends[u][1][:, t, :], x, 1)):
                            pl.indirect_dma_start(to, None, of, bass.IndirectOffsetOnAxis(
                                ap=idx[u][:, k, t:t + 1], axis=0)).then_inc(gathered[u].sem, 16)
                for u in ph.chains:
                    g = ph.up(i, u)
                    pl.wait_ge(*gathered[u].done(i))
                    ph.stand(pl)
                    pl.dma_start(group_of(s["end_rows"], g), found[u][:, :, :].rearrange("p a j -> p (a j)")
                                 ).then_inc(ends_out[u].sem, 16)
                    for k in range(2):
                        pl.dma_start(group_of(s["x_ends"][k], g), flat(ends[u][k][:, :, :])
                                     ).then_inc(ends_out[u].sem, 16)
                    if more:
                        load_indices(i + 1, u)

            with pl.Fori(1, ph.turns) as i:
                body(i, True)
            body(ph.turns, False)
            for u in ph.chains:
                pl.wait_ge(*ends_out[u].done(ph.turns))
    ph.end()


def rate_row_steps(nc, ph, w, bank, weights_in, steps):
    rates = ph.sb("rates", [REL, 1])
    e1w, e1b = ph.sb("e1w", [REL, 64]), ph.sb("e1b", [64, 1])
    e2w, e2b = ph.sb("e2w", [64, D]), ph.sb("e2b", [P, 1])
    w2b = ph.sb("w2b", [P, D])
    hidden, r_col, r_mat = ph.sb("rate_hidden", [64, 1]), ph.sb("r_col", [P, 1]), ph.sb("r_mat", [P, P])
    what = [(rates[:, :], column(w["rates"])), (e1w[:, :], w["e1_w"]), (e1b[:, :], column(w["e1_b"])),
            (e2w[:, :], w["e2_w"]), (e2b[:, :], column(w["e2_b"])), (w2b[:, :], w["W2"][D:2 * D, :])]
    rates_in = ph.sem("rates_in")

    def load(sp):
        load_weights(sp, rates_in, what)
        sp.wait_ge(rates_in, 16 * len(what))
        ph.stand(sp)
        sp.dma_start(ph_cell[:, :], w["ident"][0:1, 0:1]).then_inc(weights_in, 16)

    ph_cell = ph.sb("rates_cell", [1, 1])

    def tensor(pe):
        pe.matmul(bank[0:64, 0, 0:1], e1w[:, :], rates[:, :], start=True, stop=True).then_inc(steps, 1)
        pe.wait_ge(steps, 3)
        pe.matmul(bank[:, 1, 0:1], e2w[:, :], hidden[:, :], start=True, stop=True).then_inc(steps, 1)
        pe.wait_ge(steps, 6)
        pe.matmul(bank[:, 3, :], r_mat[:, :], w2b[:, :], start=True, stop=True)
        pe.matmul(bank[:, 2, 0:1], w2b[:, :], r_col[:, :], start=True, stop=True).then_inc(steps, 1)

    def vector(dve, row, done, col=None):
        dve.wait_ge(steps, 1)
        dve.tensor_scalar(hidden[:, :], bank[0:64, 0, 0:1], e1b[:, :], None, ALU.add).then_inc(steps, 1)
        dve.wait_ge(steps, 2)
        dve.tensor_scalar(hidden[:, :], hidden[:, :], 0.0, None, ALU.max).then_inc(steps, 1)
        dve.wait_ge(steps, 4)
        dve.tensor_scalar(r_col[:, :], bank[:, 1, 0:1], e2b[:, :], None, ALU.add).then_inc(steps, 1)
        dve.wait_ge(steps, 5)
        dve.tensor_copy(r_mat[:, :], r_col[:, :].to_broadcast((P, P))).then_inc(steps, 1)
        dve.wait_ge(steps, 7)
        if row is not None:
            dve.tensor_copy(row[:, :], bank[:, 3, :]).then_inc(done, 1)
        else:
            dve.tensor_copy(col[:, :], bank[:, 2, 0:1]).then_inc(done, 1)

    return {"load": load, "tensor": tensor, "vector": vector}



def attend_edges(nc, w, s, level):
    first = level == 0
    ph = Phase(nc, f"logits{level}", late_first=True)
    cell = ph.sb("cell", [1, P])
    ident = ph.sb("ident", [P, P])
    eps = ph.sb("eps", [P, 1])
    wq, wk, wv, b_v = (ph.sb(n, [P, D]) for n in ("wq", "wk", "wv", "b_v"))
    head_sum = ph.sb("head_sum", [P, HEADS])
    b_q, b_k = ph.sb("b_q", [P, 1]), ph.sb("b_k", [P, 1])
    src = ph.sbs("src", [P, T, D])
    dst = ph.sbs("dst", [P, T, D])
    h_src, h_dst = (ph.sbs(n, [P, T, D]) for n in ("h_src", "h_dst"))
    src_f, dst_f, x_f = (ph.sbs(n, [P, T, P]) for n in ("src_f", "dst_f", "x_f"))
    q_f, qk_f, value = (ph.sbs(n, [P, T, P]) for n in ("q_f", "qk_f", "value"))
    mask = ph.sbs("mask", [HEADS, 2, GROUP])
    logit = ph.sbs("logit", [HEADS, 2, GROUP])
    idx = ph.sbs("idx", [P, 2, T], I32)
    bank = ph.banks()
    norm_src, norm_dst = (Norm(ph, 1, f"norm_{n}") for n in ("src", "dst")) if first else (None, None)

    weights_in, eps_set, runs_set = ph.sem("weights_in"), ph.sem("eps_set"), ph.sem("runs_set")
    src_in = ph.each("src_in", per=1 if first else T, unit=16, soft=not first)
    dst_in = ph.each("dst_in", per=1 if first else T, unit=16, soft=not first)
    mask_in = ph.each("mask_in", unit=16)
    idx_in = ph.each("idx_in", unit=16)
    turned = ph.each("turned", per=3 if first else 2, primed=True)
    src_ready = ph.each("src_ready")
    dst_ready = ph.each("dst_ready", per=2 if first else 1)
    q_mm, k_mm, v_mm = ph.each("q_mm"), ph.each("k_mm"), ph.each("v_mm")
    q_ready, qk_ready, v_ready = ph.each("q_ready"), ph.each("qk_ready"), ph.each("v_ready", primed=True)
    logit_mm, logit_ready = ph.each("logit_mm"), ph.each("logit_ready", primed=True)
    running = ph.each("running", primed=True)
    stored = ph.each("stored", per=4 if first else 2, unit=16, primed=True)
    WHAT = [(ident[:, :], w["ident"]), (wq[:, :], w[f"q_w{level}"]), (wk[:, :], w[f"k_w{level}"]),
            (wv[:, :], w[f"v_w{level}"]), (b_v[:, :], over_partitions(w[f"v_b{level}"])),
            (head_sum[:, :], w["head_sum"]), (b_q[:, :], column(w[f"q_b{level}"])),
            (b_k[:, :], column(w[f"k_b{level}"]))]
    loaded = 16 * len(WHAT)

    with nc.Block() as block:
        @block.sync
        def _(sp):
            ph.prime(sp, cell, w["ident"])
            load_weights(sp, weights_in, WHAT)
            with sp.Fori(1, ph.turns + 1) as i:
                for u in ph.chains:
                    g = ph.up(i, u)
                    sp.wait_ge(*running[u].before(i))
                    ph.stand(sp)
                    sp.dma_start(mask[u][:, :, :].rearrange("p a d -> p (a d)"), group_of(s["masks"], g)
                                 ).then_inc(mask_in[u].sem, 16)
                    if first:
                        sp.wait_ge(*turned[u].before(i))
                        ph.stand(sp)
                        sp.dma_start(flat(src[u][:, :, :]), group_of(s["x_ends"][0], g)
                                     ).then_inc(src_in[u].sem, 16)
                        sp.dma_start(flat(dst[u][:, :, :]), group_of(s["x_ends"][1], g)
                                     ).then_inc(dst_in[u].sem, 16)
                    else:
                        sp.wait_ge(*turned[u].before(i))
                        ph.stand(sp)
                        sp.dma_start(idx[u][:, :, :].rearrange("p a j -> p (a j)"), group_of(s["end_rows"], g)
                                     ).then_inc(idx_in[u].sem, 16)

        if not first:
            @block.gpsimd
            def _(pl):
                ph.prime(pl, cell, w["ident"], soft=True)
                with pl.Fori(1, ph.turns + 1) as i:
                    for u in ph.chains:
                        pl.wait_ge(*idx_in[u].at(i))
                        pl.wait_ge(*turned[u].before(i))
                        ph.stand(pl)
                        for end, (rows, rows_in) in enumerate(((src, src_in), (dst, dst_in))):
                            for t in range(T):
                                pl.indirect_dma_start(
                                    rows[u][:, t, :], None, s["table"][1],
                                    bass.IndirectOffsetOnAxis(ap=idx[u][:, end, t:t + 1], axis=0)
                                ).then_inc(rows_in[u].sem, 16)

        @block.tensor
        def _(pe):
            pe.wait_ge(weights_in, loaded)
            def step(k, i, u):
                if k == 2:
                    if first:
                        pe.wait_ge(*norm_src.out[u].at(i))
                    else:
                        pe.wait_ge(*src_in[u].done(i))
                    pe.wait_ge(*logit_ready[u].before(i))
                    turn_to_features(pe, bank[u][0], (h_src if first else src)[u], ident
                                     ).then_inc(turned[u].sem, 1)
                    if first:
                        pe.wait_ge(*norm_dst.out[u].at(i))
                    else:
                        pe.wait_ge(*dst_in[u].done(i))
                    pe.wait_ge(*v_ready[u].before(i))
                    turn_to_features(pe, bank[u][1], (h_dst if first else dst)[u], ident
                                     ).then_inc(turned[u].sem, 1)
                elif k == 3:
                    pe.wait_ge(*src_ready[u].at(i))
                    if first:
                        turn_to_features(pe, bank[u][0], dst[u], ident).then_inc(turned[u].sem, 1)
                    pe.wait_ge(*dst_ready[u].at(i, 1))
                    product_features(pe, bank[u][1], wq[:, :], dst_f[u]).then_inc(q_mm[u].sem, 1)
                elif k == 4:
                    if first:
                        pe.wait_ge(*dst_ready[u].done(i))
                    product_features(pe, bank[u][0], wk[:, :], src_f[u]).then_inc(k_mm[u].sem, 1)
                    pe.wait_ge(*q_ready[u].at(i))
                    product_tokens(pe, bank[u][1], src_f[u], wv[:, :]).then_inc(v_mm[u].sem, 1)
                elif k == 5:
                    pe.wait_ge(*qk_ready[u].at(i))
                    pe.matmul(bank[u][0][0:HEADS, :, :], head_sum[:, :], qk_f[u][:, :, :], start=True,
                              stop=True).then_inc(logit_mm[u].sem, 1)

            ph.walk(pe, 8, step)

        @block.scalar
        def _(act):
            act.wait_ge(weights_in, loaded)
            act.wait_ge(eps_set, 1)
            def step(k, i, u):
                if k == 1 and first:
                    norm_src.scalar_root(act, u, i, 0, eps)
                    norm_dst.scalar_root(act, u, i, 0, eps)
                elif k == 2 and first:
                    norm_src.scalar_apply(act, u, i, 0, h_src[u], src[u])
                    norm_dst.scalar_apply(act, u, i, 0, h_dst[u], dst[u])
                elif k == 3:
                    if first:
                        act.wait_ge(*stored[u].before(i))
                    act.wait_ge(*turned[u].at(i, 2))
                    act.activation(flat(dst_f[u][:, :, :]), flat(bank[u][1][:, :, :]), ACT.Copy
                                   ).then_inc(dst_ready[u].sem, 1)
                elif k == 4:
                    if first:
                        act.wait_ge(*turned[u].at(i, 3))
                        act.activation(flat(x_f[u][:, :, :]), flat(bank[u][0][:, :, :]), ACT.Copy
                                       ).then_inc(dst_ready[u].sem, 1)
                    act.wait_ge(*q_mm[u].at(i))
                    act.activation(flat(q_f[u][:, :, :]), flat(bank[u][1][:, :, :]), ACT.Identity,
                                   bias=b_q[:, :]).then_inc(q_ready[u].sem, 1)
                elif k == 6:
                    act.wait_ge(*logit_mm[u].at(i))
                    act.wait_ge(*stored[u].before(i))
                    act.activation(logit[u][:, 0, :], flat(bank[u][0][0:HEADS, :, :]), ACT.Copy
                                   ).then_inc(logit_ready[u].sem, 1)
                elif k == 7:
                    g = ph.up(i, u)
                    if first:
                        act.wait_ge(*dst_ready[u].done(i))
                        act.dma_start(group_of(s["h_f"], g), flat(dst_f[u][:, :, :])).then_inc(stored[u].sem, 16)
                        act.dma_start(group_of(s["x_f"], g), flat(x_f[u][:, :, :])).then_inc(stored[u].sem, 16)
                    act.wait_ge(*v_ready[u].at(i))
                    act.dma_start(group_of(s["value"], g), flat(value[u][:, :, :])).then_inc(stored[u].sem, 16)
                    act.wait_ge(*running[u].at(i))
                    act.dma_start(group_of(s["logit"], g), logit[u][:, :, :].rearrange("p a d -> p (a d)")
                                  ).then_inc(stored[u].sem, 16)

            ph.walk(act, 8, step)
            for u in ph.chains:
                act.wait_ge(*stored[u].done(ph.turns))

        @block.vector
        def _(dve):
            dve.memset(eps[:, :], EPS).then_inc(eps_set, 1)
            dve.memset(logit[-1][:, :, :], 0.0).then_inc(runs_set, 1)
            dve.wait_ge(weights_in, loaded)
            dve.wait_ge(runs_set, 1)
            def step(k, i, u):
                if k == 1 and first:
                    dve.wait_ge(*src_in[u].at(i))
                    norm_src.vector_stats(dve, u, i, 0, src[u])
                    dve.wait_ge(*dst_in[u].at(i))
                    norm_dst.vector_stats(dve, u, i, 0, dst[u])
                elif k == 2 and first:
                    norm_src.vector_scale(dve, u, i, 0)
                    norm_dst.vector_scale(dve, u, i, 0)
                elif k == 3:
                    dve.wait_ge(*turned[u].at(i, 1))
                    dve.tensor_copy(flat(src_f[u][:, :, :]), flat(bank[u][0][:, :, :])
                                    ).then_inc(src_ready[u].sem, 1)
                elif k == 5:
                    dve.wait_ge(*q_ready[u].at(i))
                    dve.wait_ge(*k_mm[u].at(i))
                    dve.scalar_tensor_tensor(out=flat(qk_f[u][:, :, :]), in0=flat(bank[u][0][:, :, :]),
                                             scalar=b_k[:, :], in1=flat(q_f[u][:, :, :]), op0=ALU.add,
                                             op1=ALU.mult).then_inc(qk_ready[u].sem, 1)
                    dve.wait_ge(*v_mm[u].at(i))
                    dve.wait_ge(*stored[u].before(i))
                    dve.tensor_tensor(value[u][:, :, :], bank[u][1][:, :, :],
                                      b_v[:, :].rearrange("p (o d) -> p o d", o=1).to_broadcast((P, T, D)),
                                      ALU.add).then_inc(v_ready[u].sem, 1)
                elif k == 6:
                    dve.wait_ge(*logit_ready[u].at(i))
                    dve.wait_ge(*mask_in[u].at(i))
                    dve.wait_ge(*last_of(running, u, i))
                    dve.tensor_tensor_scan(out=logit[u][:, 1, :], data0=mask[u][:, 0, :],
                                           data1=logit[u][:, 0, :],
                                           initial=logit[u - 1][:, 1, GROUP - 1:GROUP], op0=ALU.add,
                                           op1=ALU.max).then_inc(running[u].sem, 1)

            ph.walk(dve, 8, step)
    ph.end()



def attend_nodes(nc, w, s, level):
    first = level == 0
    ph = Phase(nc, f"softmax{level}")
    cell = ph.sb("cell", [1, P])
    ident, ws = ph.sb("ident", [P, P]), ph.sb("ws", [P, D])
    head_row, head_first = ph.sb("head_row", [HEADS, D]), ph.sb("head_first", [P, HEADS])
    b_s = ph.sb("b_s", [P, 1])
    eps = ph.sb("eps", [P, 1])
    value = ph.sbs("value", [P, T, D])
    h_f, x_f = ph.sbs("h_f", [P, T, P]), ph.sbs("x_f", [P, T, P])
    same = ph.sbs("same", [P, 2, T, P])
    mask = ph.sbs("mask", [HEADS, 2, GROUP])
    logit = ph.sbs("logit", [HEADS, 2, GROUP])
    top, shifted, power = (ph.sbs(n, [HEADS, GROUP]) for n in ("top", "shifted", "power"))
    weight, message = ph.sbs("weight", [P, T, D]), ph.sbs("message", [P, T, D])
    total, summed = ph.sbs("total", [P, T, P]), ph.sbs("summed", [P, T, P])
    guarded, inverse = (ph.sbs(n, [P, T, HEADS]) for n in ("guarded", "inverse"))
    inverse_row, skip, mean, mixed, g_f = (ph.sbs(n, [P, T, P]) for n in
                                           ("inverse_row", "skip", "mean", "mixed", "g_f"))
    row, h1_f = ph.sbs("row", [P, T, D]), ph.sbs("h1_f", [P, T, P])
    bank = ph.banks()
    norm = None if first else Norm(ph)

    weights_in, zeros_set = ph.sem("weights_in"), ph.sem("zeros_set")
    logits_in, value_in, same_in = ph.each("logits_in", per=2, unit=16), ph.each("value_in", unit=16), \
        ph.each("same_in", unit=16)
    h_in, x_in = ph.each("h_in", unit=16), ph.each("x_in", unit=16)
    top_ready = ph.each("top_ready", primed=True)
    shift_ready = ph.each("shift_ready", primed=True)
    power_ready, weight_mm, weight_ready = ph.each("power_ready"), ph.each("weight_mm"), ph.each("weight_ready")
    message_ready = ph.each("message_ready", primed=True)
    sums_mm, skip_mm = ph.each("sums_mm", per=2), ph.each("skip_mm", primed=True)
    skip_ready, total_turned = ph.each("skip_ready"), ph.each("total_turned")
    inverse_ready, inverse_turned = ph.each("inverse_ready"), ph.each("inverse_turned")
    carry_total = ph.each("carry_total", per=T, primed=True)
    carry_sum = ph.each("carry_sum", per=T, primed=True)
    soft = ph.each("soft", per=4)
    g_ready = ph.each("g_ready", primed=True)
    out_turned, row_ready = ph.each("out_turned", per=1 if first else 2), ph.each("row_ready", primed=True)
    stored = ph.each("stored", per=2 if first else 3, unit=16, primed=True)
    WHAT = [(ident[:, :], w["ident"]), (ws[:, :], w[f"s_w{level}"]), (head_row[:, :], w["head_row"]),
            (head_first[:, :], w["head_first"]),
            (b_s[:, :], column(w[f"s_b{level}"]))]
    loaded = 16 * len(WHAT)
    STEPS = 8 if first else 10

    with nc.Block() as block:
        @block.sync
        def _(sp):
            ph.prime(sp, cell, w["ident"])
            load_weights(sp, weights_in, WHAT)
            with sp.Fori(1, ph.turns + 1) as i:
                for u in ph.chains:
                    g = ph.down(i, u)
                    sp.wait_ge(*shift_ready[u].before(i))
                    ph.stand(sp)
                    sp.dma_start(mask[u][:, :, :].rearrange("p a d -> p (a d)"), group_of(s["masks"], g)
                                 ).then_inc(logits_in[u].sem, 16)
                    sp.dma_start(logit[u][:, :, :].rearrange("p a d -> p (a d)"), group_of(s["logit"], g)
                                 ).then_inc(logits_in[u].sem, 16)
                    sp.wait_ge(*message_ready[u].before(i))
                    ph.stand(sp)
                    sp.dma_start(flat(value[u][:, :, :]), group_of(s["value"], g)).then_inc(value_in[u].sem, 16)
                    sp.wait_ge(*skip_mm[u].before(i))
                    ph.stand(sp)
                    sp.dma_start(flat(h_f[u][:, :, :]), group_of(s["h_f"] if first else s["g_f"], g)
                                 ).then_inc(h_in[u].sem, 16)
                    sp.wait_ge(*carry_sum[u].before(i))
                    ph.stand(sp)
                    sp.dma_start(same[u][:, :, :, :].rearrange("p a j d -> p (a j d)"),
                                 group_of(s["same"], g)).then_inc(same_in[u].sem, 16)
                    if not first:
                        sp.wait_ge(*g_ready[u].before(i))
                        ph.stand(sp)
                        sp.dma_start(flat(x_f[u][:, :, :]), group_of(s["x_f"], g)).then_inc(x_in[u].sem, 16)

        @block.tensor
        def _(pe):
            pe.wait_ge(weights_in, loaded)
            def step(k, i, u):
                if k == 1:
                    pe.wait_ge(*h_in[u].at(i))
                    if first:
                        pe.wait_ge(*row_ready[u].before(i))
                    product_features(pe, bank[u][0], ws[:, :], h_f[u]).then_inc(skip_mm[u].sem, 1)
                elif k == 2:
                    pe.wait_ge(*power_ready[u].at(i))
                    if not first:
                        pe.wait_ge(*row_ready[u].before(i))
                    for t in range(T):
                        ins = pe.matmul(bank[u][1][:, t, :], power[u][:, t * P:(t + 1) * P], head_row[:, :],
                                        start=True, stop=True)
                    ins.then_inc(weight_mm[u].sem, 1)
                elif k == 3:
                    pe.wait_ge(*same_in[u].at(i))
                    pe.wait_ge(*weight_ready[u].at(i))
                    sum_over_runs(pe, bank[u][1], weight[u], same[u]).then_inc(sums_mm[u].sem, 1)
                    pe.wait_ge(*message_ready[u].at(i))
                    pe.wait_ge(*skip_ready[u].at(i))
                    sum_over_runs(pe, bank[u][0], message[u], same[u]).then_inc(sums_mm[u].sem, 1)
                elif k == 4:
                    pe.wait_ge(*carry_total[u].done(i))
                    for t in range(T):
                        ins = pe.matmul(bank[u][1][:, t, 0:HEADS], total[u][:, t, :], head_first[:, :],
                                        start=True, stop=True)
                    ins.then_inc(total_turned[u].sem, 1)
                elif k == 5:
                    pe.wait_ge(*inverse_ready[u].at(i))
                    turn_to_features(pe, bank[u][1], inverse_row[u], ident).then_inc(inverse_turned[u].sem, 1)
                elif k == 6:
                    pe.wait_ge(*g_ready[u].at(i))
                    pe.wait_ge(*carry_sum[u].done(i))
                    turn_to_tokens(pe, bank[u][0], g_f[u], ident).then_inc(out_turned[u].sem, 1)
                elif k == 8 and not first:
                    pe.wait_ge(*norm.out[u].at(i))
                    pe.wait_ge(*soft[u].at(i, 3))
                    turn_to_features(pe, bank[u][1], row[u], ident).then_inc(out_turned[u].sem, 1)

            ph.walk(pe, STEPS, step)

        @block.scalar
        def _(act):
            act.wait_ge(weights_in, loaded)
            act.wait_ge(zeros_set, 4)
            def step(k, i, u):
                g = ph.down(i, u) if k == STEPS else None
                if k == 2:
                    act.wait_ge(*shift_ready[u].at(i))
                    act.activation(power[u][:, :], shifted[u][:, :], ACT.Exp).then_inc(power_ready[u].sem, 1)
                    act.wait_ge(*skip_mm[u].at(i))
                    act.activation(flat(skip[u][:, :, :]), flat(bank[u][0][:, :, :]), ACT.Identity,
                                   bias=b_s[:, :]).then_inc(skip_ready[u].sem, 1)
                elif k == 3:
                    act.wait_ge(*weight_mm[u].at(i))
                    act.activation(flat(weight[u][:, :, :]), flat(bank[u][1][:, :, :]), ACT.Copy
                                   ).then_inc(weight_ready[u].sem, 1)
                elif k == 5:
                    act.wait_ge(*soft[u].at(i, 2))
                    act.activation(inverse_row[u][:, :, :].rearrange("p j (h d) -> p (j h) d", h=HEADS),
                                   inverse[u][:, :, :].rearrange("p j (h o) -> p (j h) o", o=1)
                                   .to_broadcast((P, T * HEADS, D // HEADS)), ACT.Copy
                                   ).then_inc(inverse_ready[u].sem, 1)
                elif k == 6 and first:
                    act.wait_ge(*soft[u].at(i, 4))
                    act.wait_ge(*stored[u].before(i))
                    act.activation(flat(g_f[u][:, :, :]), flat(mixed[u][:, :, :]), ACT.Relu
                                   ).then_inc(g_ready[u].sem, 1)
                elif k == 7 and not first:
                    norm.scalar_root(act, u, i, 0, eps)
                elif k == 8 and not first:
                    act.wait_ge(*stored[u].before(i))
                    norm.scalar_apply(act, u, i, 0, row[u], bank[u][0])
                if k == STEPS:
                    act.wait_ge(*g_ready[u].at(i))
                    act.dma_start(group_of(s["g_f"] if first else s["x1_f"], g), flat(g_f[u][:, :, :])
                                  ).then_inc(stored[u].sem, 16)
                    if first:
                        act.wait_ge(*row_ready[u].at(i))
                        act.dma_start(table_rows(s["table"][1], g), flat(row[u][:, :, :])
                                      ).then_inc(stored[u].sem, 16)
                    else:
                        act.wait_ge(*norm.out[u].at(i))
                        act.dma_start(table_rows(s["table"][2], g), flat(row[u][:, :, :])
                                      ).then_inc(stored[u].sem, 16)
                        act.wait_ge(*row_ready[u].at(i))
                        act.dma_start(group_of(s["h_f"], g), flat(h1_f[u][:, :, :])).then_inc(stored[u].sem, 16)

            ph.walk(act, STEPS, step)
            for u in ph.chains:
                act.wait_ge(*stored[u].done(ph.turns))

        @block.vector
        def _(dve):
            dve.memset(eps[:, :], EPS).then_inc(zeros_set, 1)
            for z in (top[-1][:, :], total[-1][:, :, :], summed[-1][:, :, :]):
                dve.memset(z, 0.0).then_inc(zeros_set, 1)
            dve.wait_ge(weights_in, loaded)
            dve.wait_ge(zeros_set, 4)
            def step(k, i, u):
                if k == 1:
                    dve.wait_ge(*logits_in[u].done(i))
                    dve.wait_ge(*last_of(top_ready, u, i))
                    dve.tensor_tensor_scan(out=top[u][:, ::-1], data0=mask[u][:, 1, ::-1],
                                           data1=logit[u][:, 1, ::-1], initial=top[u - 1][:, 0:1],
                                           op0=ALU.add, op1=ALU.max).then_inc(top_ready[u].sem, 1)
                    dve.wait_ge(*top_ready[u].at(i))
                    dve.tensor_tensor(shifted[u][:, :], logit[u][:, 0, :], top[u][:, :], ALU.subtract
                                      ).then_inc(shift_ready[u].sem, 1)
                elif k == 3:
                    dve.wait_ge(*weight_ready[u].at(i))
                    dve.wait_ge(*value_in[u].at(i))
                    dve.tensor_tensor(flat(message[u][:, :, :]), flat(weight[u][:, :, :]),
                                      flat(value[u][:, :, :]), ALU.mult).then_inc(message_ready[u].sem, 1)
                elif k == 4:
                    dve.wait_ge(*sums_mm[u].at(i, 1))
                    add_carry(dve, total, bank[u][1], same[u], carry_total, u, i)
                    dve.wait_ge(*sums_mm[u].at(i, 2))
                    add_carry(dve, summed, bank[u][0], same[u], carry_sum, u, i)
                elif k == 5:
                    dve.wait_ge(*total_turned[u].at(i))
                    dve.tensor_scalar(guarded[u][:, :, :], bank[u][1][:, :, 0:HEADS], SOFT_EPS, None,
                                      ALU.add).then_inc(soft[u].sem, 1)
                    dve.wait_ge(*soft[u].at(i, 1))
                    dve.reciprocal(inverse[u][:, :, :], guarded[u][:, :, :]).then_inc(soft[u].sem, 1)
                elif k == 6:
                    dve.wait_ge(*inverse_turned[u].at(i))
                    dve.wait_ge(*carry_sum[u].done(i))
                    dve.tensor_tensor(flat(mean[u][:, :, :]), flat(bank[u][1][:, :, :]),
                                      flat(summed[u][:, :, :]), ALU.mult).then_inc(soft[u].sem, 1)
                    dve.wait_ge(*soft[u].at(i, 3))
                    dve.wait_ge(*skip_ready[u].at(i))
                    dve.tensor_tensor(flat(mixed[u][:, :, :]), flat(skip[u][:, :, :]),
                                      flat(mean[u][:, :, :]), ALU.add).then_inc(soft[u].sem, 1)
                    if not first:
                        dve.wait_ge(*soft[u].at(i, 4))
                        dve.wait_ge(*x_in[u].at(i))
                        dve.wait_ge(*stored[u].before(i))
                        dve.tensor_tensor(flat(g_f[u][:, :, :]), flat(mixed[u][:, :, :]),
                                          flat(x_f[u][:, :, :]), ALU.add).then_inc(g_ready[u].sem, 1)
                elif k == 7:
                    dve.wait_ge(*out_turned[u].at(i, 1))
                    if first:
                        dve.wait_ge(*stored[u].before(i))
                        dve.tensor_copy(flat(row[u][:, :, :]), flat(bank[u][0][:, :, :])
                                        ).then_inc(row_ready[u].sem, 1)
                    else:
                        norm.vector_stats(dve, u, i, 0, bank[u][0])
                elif k == 8 and not first:
                    norm.vector_scale(dve, u, i, 0)
                elif k == 9:
                    dve.wait_ge(*out_turned[u].at(i, 2))
                    dve.tensor_copy(flat(h1_f[u][:, :, :]), flat(bank[u][1][:, :, :])
                                    ).then_inc(row_ready[u].sem, 1)

            ph.walk(dve, STEPS, step)
    ph.end()



class Gather:

    def __init__(self, ph, s, level):
        self.ph, self.s, self.table = ph, s, s["table"][level]
        self.idx = ph.sbs("idx", [P, T], I32)
        self.rows = ph.sbs("rows", [P, T, D])
        self.same = ph.sbs("same", [P, 2, T, P])
        self.sums = ph.sbs("sums", [P, T, P])
        self.idx_in = ph.each("idx_in", unit=16)
        self.rows_in = ph.each("rows_in", per=T, unit=16, primed=True, soft=True)
        self.same_in = ph.each("same_in", unit=16)
        self.mm = ph.each("sums_mm", primed=True)
        self.carry = ph.each("carry", per=T, primed=True)
        self.zeros_set = ph.sem("sums_zero")

    def load(self, sp, u, i):
        sp.wait_ge(*self.rows_in[u].before(i))
        self.ph.stand(sp)
        sp.dma_start(self.idx[u][:, :], group_of(self.s["end_rows"], self.ph.down(i, u))[:, 0:T]
                     ).then_inc(self.idx_in[u].sem, 16)
        sp.wait_ge(*self.carry[u].before(i))
        self.ph.stand(sp)
        sp.dma_start(self.same[u][:, :, :, :].rearrange("p a j d -> p (a j d)"),
                     group_of(self.s["same"], self.ph.down(i, u))).then_inc(self.same_in[u].sem, 16)

    def gather(self, pl, u, i):
        pl.wait_ge(*self.idx_in[u].at(i))
        pl.wait_ge(*self.mm[u].before(i))
        self.ph.stand(pl)
        for t in range(T):
            pl.indirect_dma_start(self.rows[u][:, t, :], None, self.table,
                                  bass.IndirectOffsetOnAxis(ap=self.idx[u][:, t:t + 1], axis=0)
                                  ).then_inc(self.rows_in[u].sem, 16)

    def multiply(self, pe, u, i, bank):
        pe.wait_ge(*self.same_in[u].at(i))
        pe.wait_ge(*self.rows_in[u].done(i))
        sum_over_runs(pe, bank, self.rows[u], self.same[u]).then_inc(self.mm[u].sem, 1)

    def zero(self, dve):
        dve.memset(self.sums[-1][:, :, :], 0.0).then_inc(self.zeros_set, 1)
        dve.wait_ge(self.zeros_set, 1)

    def collect(self, dve, u, i, bank):
        dve.wait_ge(*self.mm[u].at(i))
        add_carry(dve, self.sums, bank, self.same[u], self.carry, u, i)


def degree_row(s, g, which, n=P):
    row = s["degrees"][bass.ds(g, 1), which * T:(which + 1) * T].rearrange("o p f -> (o p f)")
    return over_partitions(row, n)


def sage_hidden(nc, w, s):
    ph = Phase(nc, "sage0")
    cell = ph.sb("cell", [1, P])
    wl0, wr0 = ph.sb("wl0", [P, 2, D]), ph.sb("wr0", [P, 2, D])
    wl1, wr1 = ph.sb("wl1", [P, 2, D]), ph.sb("wr1", [P, 2, D])
    b_l0, b_l1 = ph.sb("b_l0", [P, 2]), ph.sb("b_l1", [P, 1])
    h_f, x_f, rate = (ph.sbs(n, [P, T, P]) for n in ("h_f", "x_f", "rate"))
    mean, next_x, row = (ph.sbs(n, [P, T, P]) for n in ("mean", "next_x", "row"))
    g3_f = [[ph.sb(f"g3_f{u}{k}", [P, T, P]) for k in range(2)] for u in ph.chains]
    bank = ph.banks()
    ga = Gather(ph, s, 2)
    weights_in = ph.sem("weights_in")
    h_in, x_in = ph.each("h_in", unit=16), ph.each("x_in", per=2, unit=16)
    mean_ready = ph.each("mean_ready")
    g3_mm, g3_ready = ph.each("g3_mm", per=2, primed=True), ph.each("g3_ready", per=2)
    t3_mm, skip_mm = ph.each("t3_mm"), ph.each("skip_mm")
    x_ready, row_ready = ph.each("x_ready", primed=True), ph.each("row_ready", primed=True)
    stored = ph.each("stored", per=2, unit=16, primed=True)
    split = lambda a: a.rearrange("(k p) d -> p k d", p=P)
    WHAT = [(wl0[:, :, :].rearrange("p k d -> p (k d)"), w["Wl0"]),
            (wr0[:, :, :].rearrange("p k d -> p (k d)"), w["Wr0"]),
            (wl1[:, :, :], split(w["Wl1"])), (wr1[:, :, :], split(w["Wr1"])),
            (b_l0[:, 0:1], column(w["bl0"][0:D])), (b_l0[:, 1:2], column(w["bl0"][D:2 * D])),
            (b_l1[:, :], column(w["bl1"]))]
    loaded = 16 * len(WHAT)
    with nc.Block() as block:
        @block.sync
        def _(sp):
            ph.prime(sp, cell, w["ident"])
            load_weights(sp, weights_in, WHAT)
            with sp.Fori(1, ph.turns + 1) as i:
                for u in ph.chains:
                    g = ph.down(i, u)
                    ga.load(sp, u, i)
                    sp.wait_ge(*g3_mm[u].before(i))
                    ph.stand(sp)
                    sp.dma_start(flat(h_f[u][:, :, :]), group_of(s["h_f"], g)).then_inc(h_in[u].sem, 16)
                    sp.wait_ge(*x_ready[u].before(i))
                    ph.stand(sp)
                    sp.dma_start(flat(rate[u][:, :, :]), degree_row(s, g, 0)).then_inc(x_in[u].sem, 16)
                    sp.dma_start(flat(x_f[u][:, :, :]), group_of(s["x1_f"], g)).then_inc(x_in[u].sem, 16)

        @block.gpsimd
        def _(pl):
            ph.prime(pl, cell, w["ident"], soft=True)
            with pl.Fori(1, ph.turns + 1) as i:
                for u in ph.chains:
                    ga.gather(pl, u, i)

        @block.tensor
        def _(pe):
            pe.wait_ge(weights_in, loaded)
            def step(k, i, u):
                if k == 1:
                    pe.wait_ge(*x_ready[u].before(i))
                    ga.multiply(pe, u, i, bank[u][0])
                elif k == 2:
                    pe.wait_ge(*h_in[u].at(i))
                    pe.wait_ge(*mean_ready[u].at(i))
                    pe.wait_ge(*row_ready[u].before(i))
                    for c in range(2):
                        product_features(pe, bank[u][1 - c], wr0[:, c, :], h_f[u], stop=False)
                        product_features(pe, bank[u][1 - c], wl0[:, c, :], mean[u], start=False
                                         ).then_inc(g3_mm[u].sem, 1)
                elif k == 3:
                    pe.wait_ge(*g3_ready[u].done(i))
                    for j in range(T):
                        for c in range(2):
                            ins = pe.matmul(bank[u][1][:, j, :], g3_f[u][c][:, j, :], wl1[:, c, :],
                                            start=(c == 0), stop=(c == 1))
                    ins.then_inc(t3_mm[u].sem, 1)
                    product_features(pe, bank[u][0], wr1[:, 0, :], g3_f[u][0], stop=False)
                    product_features(pe, bank[u][0], wr1[:, 1, :], g3_f[u][1], start=False
                                     ).then_inc(skip_mm[u].sem, 1)

            ph.walk(pe, 4, step)

        @block.scalar
        def _(act):
            act.wait_ge(weights_in, loaded)
            def step(k, i, u):
                if k == 3:
                    for c in range(2):
                        act.wait_ge(*g3_mm[u].at(i, c + 1))
                        act.activation(flat(g3_f[u][c][:, :, :]), flat(bank[u][1 - c][:, :, :]), ACT.Relu,
                                       bias=b_l0[:, c:c + 1]).then_inc(g3_ready[u].sem, 1)
                elif k == 4:
                    g = ph.down(i, u)
                    act.wait_ge(*t3_mm[u].at(i))
                    act.wait_ge(*stored[u].before(i))
                    act.activation(flat(row[u][:, :, :]), flat(bank[u][1][:, :, :]), ACT.Copy
                                   ).then_inc(row_ready[u].sem, 1)
                    act.wait_ge(*row_ready[u].at(i))
                    act.dma_start(table_rows(s["table"][3], g), flat(row[u][:, :, :])).then_inc(stored[u].sem, 16)
                    act.wait_ge(*x_ready[u].at(i))
                    act.dma_start(group_of(s["x_f"], g), flat(next_x[u][:, :, :])).then_inc(stored[u].sem, 16)

            ph.walk(act, 4, step)
            for u in ph.chains:
                act.wait_ge(*stored[u].done(ph.turns))

        @block.vector
        def _(dve):
            ga.zero(dve)
            dve.wait_ge(weights_in, loaded)
            def step(k, i, u):
                if k == 2:
                    ga.collect(dve, u, i, bank[u][0])
                    dve.wait_ge(*ga.carry[u].done(i))
                    dve.wait_ge(*x_in[u].done(i))
                    dve.tensor_tensor(mean[u][:, :, :], ga.sums[u][:, :, :], rate[u][:, :, :], ALU.mult
                                      ).then_inc(mean_ready[u].sem, 1)
                elif k == 4:
                    dve.wait_ge(*skip_mm[u].at(i))
                    dve.wait_ge(*stored[u].before(i))
                    dve.scalar_tensor_tensor(out=flat(next_x[u][:, :, :]), in0=flat(bank[u][0][:, :, :]),
                                             scalar=b_l1[:, :], in1=flat(x_f[u][:, :, :]), op0=ALU.add,
                                             op1=ALU.add).then_inc(x_ready[u].sem, 1)

            ph.walk(dve, 4, step)
    ph.end()


def sage_out(nc, w, s):
    ph = Phase(nc, "sage1")
    cell = ph.sb("cell", [1, P])
    ident, w1, eps = ph.sb("ident", [P, P]), ph.sb("w1", [P, D]), ph.sb("eps", [P, 1])
    x_f, rate, root = (ph.sbs(n, [P, T, P]) for n in ("x_f", "rate", "root"))
    mean, next_x, h, h_f, scaled, row = (ph.sbs(n, [P, T, P]) for n in
                                         ("mean", "next_x", "h", "h_f", "scaled", "row"))
    bank = ph.banks()
    ga = Gather(ph, s, 3)
    norm = Norm(ph)
    weights_in, eps_set = ph.sem("weights_in"), ph.sem("eps_set")
    x_in, root_in = ph.each("x_in", per=2, unit=16), ph.each("root_in", unit=16)
    mean_ready, x_ready = ph.each("mean_ready"), ph.each("x_ready", primed=True)
    turned, h_ready = ph.each("turned", per=3), ph.each("h_ready")
    w1_mm, scaled_ready = ph.each("w1_mm"), ph.each("scaled_ready", primed=True)
    row_ready = ph.each("row_ready", primed=True)
    stored = ph.each("stored", per=3, unit=16, primed=True)
    WHAT = [(ident[:, :], w["ident"]), (w1[:, :], w["W1"])]
    loaded = 16 * len(WHAT)
    with nc.Block() as block:
        @block.sync
        def _(sp):
            ph.prime(sp, cell, w["ident"])
            load_weights(sp, weights_in, WHAT)
            with sp.Fori(1, ph.turns + 1) as i:
                for u in ph.chains:
                    g = ph.down(i, u)
                    ga.load(sp, u, i)
                    sp.wait_ge(*x_ready[u].before(i))
                    ph.stand(sp)
                    sp.dma_start(flat(rate[u][:, :, :]), degree_row(s, g, 0)).then_inc(x_in[u].sem, 16)
                    sp.dma_start(flat(x_f[u][:, :, :]), group_of(s["x_f"], g)).then_inc(x_in[u].sem, 16)
                    sp.wait_ge(*scaled_ready[u].before(i))
                    ph.stand(sp)
                    sp.dma_start(flat(root[u][:, :, :]), degree_row(s, g, 1)).then_inc(root_in[u].sem, 16)

        @block.gpsimd
        def _(pl):
            ph.prime(pl, cell, w["ident"], soft=True)
            with pl.Fori(1, ph.turns + 1) as i:
                for u in ph.chains:
                    ga.gather(pl, u, i)

        @block.tensor
        def _(pe):
            pe.wait_ge(weights_in, loaded)
            def step(k, i, u):
                if k == 1:
                    pe.wait_ge(*row_ready[u].before(i))
                    ga.multiply(pe, u, i, bank[u][0])
                elif k == 2:
                    pe.wait_ge(*x_ready[u].at(i))
                    turn_to_tokens(pe, bank[u][1], next_x[u], ident).then_inc(turned[u].sem, 1)
                elif k == 4:
                    pe.wait_ge(*norm.out[u].at(i))
                    turn_to_features(pe, bank[u][0], h[u], ident).then_inc(turned[u].sem, 1)
                elif k == 5:
                    pe.wait_ge(*h_ready[u].at(i))
                    product_features(pe, bank[u][1], w1[:, :], h_f[u]).then_inc(w1_mm[u].sem, 1)
                elif k == 6:
                    pe.wait_ge(*scaled_ready[u].at(i))
                    turn_to_tokens(pe, bank[u][0], scaled[u], ident).then_inc(turned[u].sem, 1)

            ph.walk(pe, 8, step)

        @block.scalar
        def _(act):
            act.wait_ge(weights_in, loaded)
            act.wait_ge(eps_set, 1)
            def step(k, i, u):
                if k == 3:
                    norm.scalar_root(act, u, i, 0, eps)
                elif k == 4:
                    norm.scalar_apply(act, u, i, 0, h[u], bank[u][1])
                elif k == 7:
                    g = ph.down(i, u)
                    act.wait_ge(*turned[u].at(i, 3))
                    act.wait_ge(*stored[u].before(i))
                    act.activation(flat(row[u][:, :, :]), flat(bank[u][0][:, :, :]), ACT.Copy
                                   ).then_inc(row_ready[u].sem, 1)
                    act.dma_start(group_of(s["x1_f"], g), flat(next_x[u][:, :, :])).then_inc(stored[u].sem, 16)
                    act.dma_start(group_of(s["g_f"], g), flat(scaled[u][:, :, :])).then_inc(stored[u].sem, 16)
                    act.wait_ge(*row_ready[u].at(i))
                    act.dma_start(table_rows(s["table"][4], g), flat(row[u][:, :, :])).then_inc(stored[u].sem, 16)

            ph.walk(act, 8, step)
            for u in ph.chains:
                act.wait_ge(*stored[u].done(ph.turns))

        @block.vector
        def _(dve):
            dve.memset(eps[:, :], EPS).then_inc(eps_set, 1)
            ga.zero(dve)
            def step(k, i, u):
                if k == 2:
                    ga.collect(dve, u, i, bank[u][0])
                    dve.wait_ge(*ga.carry[u].done(i))
                    dve.wait_ge(*x_in[u].done(i))
                    dve.tensor_tensor(mean[u][:, :, :], ga.sums[u][:, :, :], rate[u][:, :, :], ALU.mult
                                      ).then_inc(mean_ready[u].sem, 1)
                    dve.wait_ge(*mean_ready[u].at(i))
                    dve.wait_ge(*stored[u].before(i))
                    dve.tensor_tensor(next_x[u][:, :, :], mean[u][:, :, :], x_f[u][:, :, :], ALU.add
                                      ).then_inc(x_ready[u].sem, 1)
                elif k == 3:
                    dve.wait_ge(*turned[u].at(i, 1))
                    norm.vector_stats(dve, u, i, 0, bank[u][1])
                elif k == 4:
                    norm.vector_scale(dve, u, i, 0)
                elif k == 5:
                    dve.wait_ge(*turned[u].at(i, 2))
                    dve.tensor_copy(flat(h_f[u][:, :, :]), flat(bank[u][0][:, :, :])).then_inc(h_ready[u].sem, 1)
                elif k == 6:
                    dve.wait_ge(*w1_mm[u].at(i))
                    dve.wait_ge(*root_in[u].at(i))
                    dve.tensor_tensor(scaled[u][:, :, :], bank[u][1][:, :, :], root[u][:, :, :], ALU.mult
                                      ).then_inc(scaled_ready[u].sem, 1)

            ph.walk(dve, 8, step)
    ph.end()


def gcn_hidden(nc, w, s):
    ph = Phase(nc, "gcn0", late_first=True)
    cell = ph.sb("cell", [1, P])
    ident, w2 = ph.sb("ident", [P, P]), ph.sb("w2", [P, D])
    b_1, rate_col = ph.sb("b_1", [P, 1]), ph.sb("rate_col", [P, 1])
    own, root = ph.sbs("own", [P, T, P]), ph.sbs("root", [P, T, P])
    both, mean, g_f, scaled, row = (ph.sbs(n, [P, T, P]) for n in ("both", "mean", "g_f", "scaled", "row"))
    bank = ph.banks()
    ga = Gather(ph, s, 4)
    weights_in, rate_steps, rates_set = ph.sem("weights_in"), ph.sem("rate_steps"), ph.sem("rates_set")
    own_in = ph.each("own_in", per=2, unit=16)
    both_ready, mean_ready, g_ready = ph.each("both_ready"), ph.each("mean_ready"), ph.each("g_ready")
    w2_mm, scaled_ready = ph.each("w2_mm"), ph.each("scaled_ready", primed=True)
    turned, row_ready = ph.each("turned"), ph.each("row_ready", primed=True)
    stored = ph.each("stored", per=2, unit=16, primed=True)
    WHAT = [(ident[:, :], w["ident"]), (w2[:, :], w["W2"][0:D, :]), (b_1[:, :], column(w["b1"]))]
    loaded = 16 * (len(WHAT) + 1)
    rates = rate_row_steps(nc, ph, w, bank[0][0], weights_in, rate_steps)
    with nc.Block() as block:
        @block.sync
        def _(sp):
            ph.prime(sp, cell, w["ident"])
            load_weights(sp, weights_in, WHAT)
            rates["load"](sp)
            with sp.Fori(1, ph.turns + 1) as i:
                for u in ph.chains:
                    g = ph.down(i, u)
                    ga.load(sp, u, i)
                    sp.wait_ge(*scaled_ready[u].before(i))
                    ph.stand(sp)
                    sp.dma_start(flat(own[u][:, :, :]), group_of(s["g_f"], g)).then_inc(own_in[u].sem, 16)
                    sp.dma_start(flat(root[u][:, :, :]), degree_row(s, g, 1)).then_inc(own_in[u].sem, 16)

        @block.gpsimd
        def _(pl):
            ph.prime(pl, cell, w["ident"], soft=True)
            with pl.Fori(1, ph.turns + 1) as i:
                for u in ph.chains:
                    ga.gather(pl, u, i)

        @block.tensor
        def _(pe):
            pe.wait_ge(weights_in, loaded)
            rates["tensor"](pe)
            pe.wait_ge(rates_set, 1)
            def step(k, i, u):
                if k == 1:
                    pe.wait_ge(*row_ready[u].before(i))
                    ga.multiply(pe, u, i, bank[u][0])
                elif k == 2:
                    pe.wait_ge(*g_ready[u].at(i))
                    product_features(pe, bank[u][1], w2[:, :], g_f[u]).then_inc(w2_mm[u].sem, 1)
                elif k == 3:
                    pe.wait_ge(*scaled_ready[u].at(i))
                    turn_to_tokens(pe, bank[u][0], scaled[u], ident).then_inc(turned[u].sem, 1)

            ph.walk(pe, 4, step)

        @block.scalar
        def _(act):
            act.wait_ge(weights_in, loaded)
            def step(k, i, u):
                if k == 2:
                    act.wait_ge(*mean_ready[u].at(i))
                    act.activation(flat(g_f[u][:, :, :]), flat(mean[u][:, :, :]), ACT.Relu, bias=b_1[:, :]
                                   ).then_inc(g_ready[u].sem, 1)
                elif k == 4:
                    g = ph.down(i, u)
                    act.wait_ge(*turned[u].at(i))
                    act.wait_ge(*stored[u].before(i))
                    act.activation(flat(row[u][:, :, :]), flat(bank[u][0][:, :, :]), ACT.Copy
                                   ).then_inc(row_ready[u].sem, 1)
                    act.dma_start(group_of(s["h_f"], g), flat(scaled[u][:, :, :])).then_inc(stored[u].sem, 16)
                    act.wait_ge(*row_ready[u].at(i))
                    act.dma_start(table_rows(s["table"][5], g), flat(row[u][:, :, :])).then_inc(stored[u].sem, 16)

            ph.walk(act, 4, step)
            for u in ph.chains:
                act.wait_ge(*stored[u].done(ph.turns))

        @block.vector
        def _(dve):
            ga.zero(dve)
            dve.wait_ge(weights_in, loaded)
            rates["vector"](dve, None, rates_set, rate_col)
            dve.wait_ge(rates_set, 1)
            def step(k, i, u):
                if k == 2:
                    ga.collect(dve, u, i, bank[u][0])
                    dve.wait_ge(*ga.carry[u].done(i))
                    dve.wait_ge(*own_in[u].done(i))
                    dve.tensor_tensor(both[u][:, :, :], ga.sums[u][:, :, :], own[u][:, :, :], ALU.add
                                      ).then_inc(both_ready[u].sem, 1)
                    dve.wait_ge(*both_ready[u].at(i))
                    dve.tensor_tensor(mean[u][:, :, :], both[u][:, :, :], root[u][:, :, :], ALU.mult
                                      ).then_inc(mean_ready[u].sem, 1)
                elif k == 3:
                    dve.wait_ge(*w2_mm[u].at(i))
                    dve.wait_ge(*stored[u].before(i))
                    dve.scalar_tensor_tensor(out=flat(scaled[u][:, :, :]), in0=flat(bank[u][1][:, :, :]),
                                             scalar=rate_col[:, :], in1=flat(root[u][:, :, :]), op0=ALU.add,
                                             op1=ALU.mult).then_inc(scaled_ready[u].sem, 1)

            ph.walk(dve, 4, step)
    ph.end()


def gcn_out(nc, out, w, s):
    ph = Phase(nc, "gcn1")
    cell = ph.sb("cell", [1, P])
    ident, b_2, eps = ph.sb("ident", [P, P]), ph.sb("b_2", [P, 1]), ph.sb("eps", [P, 1])
    w_self = ph.sb("w_self", [P, D])
    own, root, x_f = (ph.sbs(n, [P, T, P]) for n in ("own", "root", "x_f"))
    both, mean, next_x, row, h_f = (ph.sbs(n, [P, T, P]) for n in ("both", "mean", "next_x", "row", "h_f"))
    last, out_row = ph.sbs("last", [P, T, P]), ph.sbs("out_row", [P, T, D])
    put = ph.sbs("put", [P, T], I32)
    bank = ph.banks()
    ga = Gather(ph, s, 5)
    norm = Norm(ph)
    weights_in, eps_set = ph.sem("weights_in"), ph.sem("eps_set")
    own_in, put_in = ph.each("own_in", per=3, unit=16), ph.each("put_in", unit=16)
    both_ready, mean_ready = ph.each("both_ready"), ph.each("mean_ready")
    x_ready = ph.each("x_ready", primed=True)
    turned, h_ready = ph.each("turned", per=3), ph.each("h_ready")
    self_mm, last_ready = ph.each("self_mm"), ph.each("last_ready")
    out_ready = ph.each("out_ready", primed=True)
    stored = ph.each("stored", unit=16, primed=True)
    scattered = ph.each("scattered", per=T, unit=16, primed=True, soft=True)
    WHAT = [(ident[:, :], w["ident"]), (b_2[:, :], column(w["b2"])), (w_self[:, :], w["w_self"])]
    loaded = 16 * len(WHAT)
    with nc.Block() as block:
        @block.sync
        def _(sp):
            ph.prime(sp, cell, w["ident"])
            load_weights(sp, weights_in, WHAT)
            def load(i, u):
                g = ph.down(i, u)
                ga.load(sp, u, i)
                sp.wait_ge(*x_ready[u].before(i))
                ph.stand(sp)
                sp.dma_start(flat(own[u][:, :, :]), group_of(s["h_f"], g)).then_inc(own_in[u].sem, 16)
                sp.dma_start(flat(root[u][:, :, :]), degree_row(s, g, 1)).then_inc(own_in[u].sem, 16)
                sp.dma_start(flat(x_f[u][:, :, :]), group_of(s["x1_f"], g)).then_inc(own_in[u].sem, 16)

            def load_put(i, u):
                sp.wait_ge(*scattered[u].before(i))
                ph.stand(sp)
                sp.dma_start(put[u][:, :], group_of(s["put_rows"], ph.down(i, u))).then_inc(put_in[u].sem, 16)

            ph.ahead_and_behind(sp, load, load_put)

        @block.gpsimd
        def _(pl):
            ph.prime(pl, cell, w["ident"], soft=True)

            def scatter(i, u):
                pl.wait_ge(*put_in[u].at(i))
                pl.wait_ge(*out_ready[u].at(i))
                ph.stand(pl)
                for t in range(T):
                    pl.indirect_dma_start(
                        out, bass.IndirectOffsetOnAxis(ap=put[u][:, t:t + 1], axis=0), out_row[u][:, t, :],
                        None, bounds_check=N - 1, oob_is_err=False).then_inc(scattered[u].sem, 16)

            ph.ahead_and_behind(pl, lambda i, u: ga.gather(pl, u, i), scatter)
            for u in ph.chains:
                pl.wait_ge(*scattered[u].done(ph.turns))

        @block.tensor
        def _(pe):
            pe.wait_ge(weights_in, loaded)
            def step(k, i, u):
                if k == 1:
                    pe.wait_ge(*out_ready[u].before(i))
                    ga.multiply(pe, u, i, bank[u][0])
                elif k == 3:
                    pe.wait_ge(*x_ready[u].at(i))
                    turn_to_tokens(pe, bank[u][1], next_x[u], ident).then_inc(turned[u].sem, 1)
                elif k == 5:
                    pe.wait_ge(*norm.out[u].at(i))
                    turn_to_features(pe, bank[u][0], row[u], ident).then_inc(turned[u].sem, 1)
                elif k == 6:
                    pe.wait_ge(*h_ready[u].at(i))
                    product_features(pe, bank[u][1], w_self[:, :], h_f[u]).then_inc(self_mm[u].sem, 1)
                elif k == 7:
                    pe.wait_ge(*last_ready[u].at(i))
                    turn_to_tokens(pe, bank[u][0], last[u], ident).then_inc(turned[u].sem, 1)

            ph.walk(pe, 8, step)

        @block.scalar
        def _(act):
            act.wait_ge(weights_in, loaded)
            act.wait_ge(eps_set, 1)
            def step(k, i, u):
                if k == 4:
                    norm.scalar_root(act, u, i, 0, eps)
                elif k == 5:
                    act.wait_ge(*stored[u].before(i))
                    norm.scalar_apply(act, u, i, 0, row[u], bank[u][1])
                elif k == 6:
                    act.wait_ge(*norm.out[u].at(i))
                    act.dma_start(table_rows(s["table"][6], ph.down(i, u)), flat(row[u][:, :, :])
                                  ).then_inc(stored[u].sem, 16)
                elif k == 8:
                    act.wait_ge(*turned[u].at(i, 3))
                    act.wait_ge(*scattered[u].before(i))
                    act.activation(flat(out_row[u][:, :, :]), flat(bank[u][0][:, :, :]), ACT.Copy
                                   ).then_inc(out_ready[u].sem, 1)

            ph.walk(act, 8, step)
            for u in ph.chains:
                act.wait_ge(*stored[u].done(ph.turns))

        @block.vector
        def _(dve):
            dve.memset(eps[:, :], EPS).then_inc(eps_set, 1)
            ga.zero(dve)
            dve.wait_ge(weights_in, loaded)
            def step(k, i, u):
                if k == 2:
                    ga.collect(dve, u, i, bank[u][0])
                    dve.wait_ge(*ga.carry[u].done(i))
                    dve.wait_ge(*own_in[u].done(i))
                    dve.tensor_tensor(both[u][:, :, :], ga.sums[u][:, :, :], own[u][:, :, :], ALU.add
                                      ).then_inc(both_ready[u].sem, 1)
                elif k == 3:
                    dve.wait_ge(*both_ready[u].at(i))
                    dve.tensor_tensor(mean[u][:, :, :], both[u][:, :, :], root[u][:, :, :], ALU.mult
                                      ).then_inc(mean_ready[u].sem, 1)
                    dve.wait_ge(*mean_ready[u].at(i))
                    dve.scalar_tensor_tensor(out=flat(next_x[u][:, :, :]), in0=flat(mean[u][:, :, :]),
                                             scalar=b_2[:, :], in1=flat(x_f[u][:, :, :]), op0=ALU.add,
                                             op1=ALU.add).then_inc(x_ready[u].sem, 1)
                elif k == 4:
                    dve.wait_ge(*turned[u].at(i, 1))
                    norm.vector_stats(dve, u, i, 0, bank[u][1])
                elif k == 5:
                    norm.vector_scale(dve, u, i, 0)
                elif k == 6:
                    dve.wait_ge(*turned[u].at(i, 2))
                    dve.tensor_copy(flat(h_f[u][:, :, :]), flat(bank[u][0][:, :, :])).then_inc(h_ready[u].sem, 1)
                elif k == 7:
                    dve.wait_ge(*self_mm[u].at(i))
                    dve.tensor_tensor(last[u][:, :, :], bank[u][1][:, :, :], next_x[u][:, :, :], ALU.add
                                      ).then_inc(last_ready[u].sem, 1)

            ph.walk(dve, 8, step)
    ph.end()


def relations(nc, out, w, s):
    ph = Phase(nc, "relational", late_first=True)
    cell = ph.sb("cell", [1, P])
    ident = ph.sb("ident", [P, P])
    bases, table = ph.sb("bases", [P, BASES, D]), ph.sb("coefficients", [REL, BASES])
    number = ph.sb("number", [REL, 1], I32)
    numberf = ph.sb("numberf", [REL, 1])
    idx, rows, row_f = ph.sbs("idx", [P, T], I32), ph.sbs("rows", [P, T, D]), ph.sbs("row_f", [P, T, P])
    message, total = ph.sbs("message", [P, T, D]), ph.sbs("total", [P, T, D])
    kind, one_hot = ph.sbs("kind", [REL, GROUP], I32), ph.sbs("one_hot", [REL, GROUP])
    source, source_col = ph.sbs("source", [P, GROUP], I32), ph.sbs("source_col", [P, T], I32)
    source_colf = ph.sbs("source_colf", [P, T])
    equal = ph.sbs("equal", [P, T, GROUP])
    coef = ph.sbs("coef", [P, T, BASES])
    add_row = ph.sbs("add_row", [P, T], I32)
    based = [ph.psum(f"based{u}", [P, BASES, D]) for u in ph.chains]
    turn_bank = sum_bank = [based[u][:, 0:T, :] for u in ph.chains]
    coef_bank = [based[u][:, T:2 * T, :] for u in ph.chains]
    weights_in, number_set = ph.sem("weights_in"), ph.sem("number_set")
    kind_in, source_in = ph.each("kind_in", unit=16), ph.each("source_in", per=2, unit=16)
    idx_in, add_row_in = ph.each("idx_in", unit=16), ph.each("add_row_in", unit=16)
    rows_in = ph.each("rows_in", per=T, unit=16, soft=True)
    hot_ready = ph.each("hot_ready", primed=True)
    source_f, equal_ready = ph.each("source_f"), ph.each("equal_ready", primed=True)
    coef_mm, coef_ready = ph.each("coef_mm"), ph.each("coef_ready")
    turned, row_ready = ph.each("turned", primed=True), ph.each("row_ready")
    based_mm = ph.each("based_mm", per=2 * T)
    weighted = ph.each("weighted", per=T * BASES, primed=True)
    total_mm, total_ready = ph.each("total_mm", primed=True), ph.each("total_ready", primed=True)
    added = ph.each("added", per=T, unit=16, primed=True, soft=True)
    WHAT = [(ident[:, :], w["ident"]), (bases[:, :, :], w["bases"].rearrange("b i o -> i b o")),
            (table[:, :], w["coefficients"])]
    loaded = 16 * len(WHAT)
    STEPS = 4 + T
    with nc.Block() as block:
        @block.sync
        def _(sp):
            ph.prime(sp, cell, w["ident"])
            load_weights(sp, weights_in, WHAT)
            def load(i, u):
                g = ph.down(i, u)
                sp.wait_ge(*turned[u].before(i))
                ph.stand(sp)
                sp.dma_start(idx[u][:, :], group_of(s["end_rows"], g)[:, T:2 * T]).then_inc(idx_in[u].sem, 16)
                sp.wait_ge(*hot_ready[u].before(i))
                ph.stand(sp)
                sp.dma_start(kind[u][:, :], over_partitions(s["edge_type"][bass.ds(g * GROUP, GROUP)], REL)
                             ).then_inc(kind_in[u].sem, 16)
                sp.wait_ge(*equal_ready[u].before(i))
                ph.stand(sp)
                sp.dma_start(source[u][:, :], over_partitions(s["src_line"][bass.ds(g * GROUP, GROUP)])
                             ).then_inc(source_in[u].sem, 16)
                sp.dma_start(source_col[u][:, :], group_of(s["src_cols"], g)).then_inc(source_in[u].sem, 16)

            def load_add_rows(i, u):
                sp.wait_ge(*added[u].before(i))
                ph.stand(sp)
                sp.dma_start(add_row[u][:, :], group_of(s["add_rows"], ph.down(i, u))
                             ).then_inc(add_row_in[u].sem, 16)

            ph.ahead_and_behind(sp, load, load_add_rows)

        @block.gpsimd
        def _(pl):
            ph.prime(pl, cell, w["ident"], soft=True)
            pl.iota(number[:, :], pattern=[[0, 1]], base=0, channel_multiplier=1).then_inc(number_set, 1)

            def gather(i, u):
                pl.wait_ge(*idx_in[u].at(i))
                pl.wait_ge(*turned[u].before(i))
                ph.stand(pl)
                for t in range(T):
                    pl.indirect_dma_start(rows[u][:, t, :], None, s["table"][6],
                                          bass.IndirectOffsetOnAxis(ap=idx[u][:, t:t + 1], axis=0)
                                          ).then_inc(rows_in[u].sem, 16)

            def add(i, u):
                pl.wait_ge(*add_row_in[u].at(i))
                pl.wait_ge(*total_ready[u].at(i))
                pl.wait_ge(*last_of(added, u, i))
                ph.stand(pl)
                for t in range(T):
                    pl.indirect_dma_start(
                        out, bass.IndirectOffsetOnAxis(ap=add_row[u][:, t:t + 1], axis=0), total[u][:, t, :],
                        None, compute_op=ALU.add).then_inc(added[u].sem, 16)

            ph.ahead_and_behind(pl, gather, add)
            for u in ph.chains:
                pl.wait_ge(*added[u].done(ph.turns))

        @block.tensor
        def _(pe):
            pe.wait_ge(weights_in, loaded)
            def step(k, i, u):
                if k == 1:
                    pe.wait_ge(*rows_in[u].done(i))
                    pe.wait_ge(*total_ready[u].before(i))
                    turn_to_features(pe, turn_bank[u], rows[u], ident).then_inc(turned[u].sem, 1)
                    pe.wait_ge(*hot_ready[u].at(i))
                    pe.wait_ge(*weighted[u].before(i))
                    for t in range(T):
                        ins = pe.matmul(coef_bank[u][:, t, 0:BASES], one_hot[u][:, t * P:(t + 1) * P],
                                        table[:, :], start=True, stop=True)
                    ins.then_inc(coef_mm[u].sem, 1)
                elif k <= 1 + T:
                    t = k - 2
                    for half in range(2):
                        if t == 0:
                            pe.wait_ge(*(coef_ready if half else row_ready)[u].at(i))
                        else:
                            pe.wait_ge(*weighted[u].at(i, (t - 1) * BASES + 4 * (half + 1)))
                        ins = pe.matmul(based[u][:, 4 * half:4 * half + 4, :], row_f[u][:, t, :],
                                        bases[:, 4 * half:4 * half + 4, :], start=True, stop=True)
                        ins.then_inc(based_mm[u].sem, 1)
                elif k == 2 + T:
                    pe.wait_ge(*equal_ready[u].at(i))
                    pe.wait_ge(*weighted[u].done(i))
                    for t in range(T):
                        for a in range(T):
                            ins = pe.matmul(sum_bank[u][:, t, :], equal[u][:, a, t * P:(t + 1) * P],
                                            message[u][:, a, :], start=(a == 0), stop=(a == T - 1))
                    ins.then_inc(total_mm[u].sem, 1)

            ph.walk(pe, STEPS, step)

        @block.scalar
        def _(act):
            def step(k, i, u):
                if k == 1:
                    act.wait_ge(*source_in[u].done(i))
                    act.wait_ge(*equal_ready[u].before(i))
                    act.activation(source_colf[u][:, :], source_col[u][:, :], ACT.Copy
                                   ).then_inc(source_f[u].sem, 1)
                elif k == 2:
                    act.wait_ge(*turned[u].at(i))
                    act.activation(flat(row_f[u][:, :, :]), flat(turn_bank[u]), ACT.Copy
                                   ).then_inc(row_ready[u].sem, 1)
                    act.wait_ge(*coef_mm[u].at(i))
                    act.activation(coef[u][:, :, :], coef_bank[u][:, :, 0:BASES], ACT.Copy
                                   ).then_inc(coef_ready[u].sem, 1)
                elif k == STEPS:
                    act.wait_ge(*total_mm[u].at(i))
                    act.wait_ge(*added[u].before(i))
                    act.activation(flat(total[u][:, :, :]), flat(sum_bank[u]), ACT.Copy
                                   ).then_inc(total_ready[u].sem, 1)

            ph.walk(act, STEPS, step)

        @block.vector
        def _(dve):
            dve.wait_ge(number_set, 1)
            dve.tensor_copy(numberf[:, :], number[:, :]).then_inc(number_set, 1)
            dve.wait_ge(number_set, 2)
            def step(k, i, u):
                if k == 1:
                    dve.wait_ge(*kind_in[u].at(i))
                    dve.tensor_scalar(one_hot[u][:, :], kind[u][:, :], numberf[:, :], None, ALU.is_equal
                                      ).then_inc(hot_ready[u].sem, 1)
                    dve.wait_ge(*source_f[u].at(i))
                    dve.wait_ge(*total_mm[u].before(i))
                    for a in range(T):
                        ins = dve.tensor_scalar(equal[u][:, a, :], source[u][:, :], source_colf[u][:, a:a + 1],
                                                None, ALU.is_equal)
                    ins.then_inc(equal_ready[u].sem, 1)
                elif 3 <= k <= 2 + T:
                    t = k - 3
                    if t == 0:
                        dve.wait_ge(*coef_ready[u].at(i))
                    for b in range(BASES):
                        if b % 4 == 0:
                            dve.wait_ge(*based_mm[u].at(i, 2 * t + b // 4 + 1))
                        if b == 0:
                            dve.tensor_scalar(message[u][:, t, :], based[u][:, 0, :], coef[u][:, t, 0:1], None,
                                              ALU.mult).then_inc(weighted[u].sem, 1)
                            continue
                        dve.wait_ge(*weighted[u].at(i, t * BASES + b))
                        dve.scalar_tensor_tensor(out=message[u][:, t, :], in0=based[u][:, b, :],
                                                 scalar=coef[u][:, t, b:b + 1], in1=message[u][:, t, :],
                                                 op0=ALU.mult, op1=ALU.add).then_inc(weighted[u].sem, 1)

            ph.walk(dve, STEPS, step)
    ph.end()


def gnn(nc, x, out, w, s):
    edge_structure(nc, w, s)
    dense_chain(nc, x, out, w, s)
    for level in range(2):
        attend_edges(nc, w, s, level)
        attend_nodes(nc, w, s, level)
    sage_hidden(nc, w, s)
    sage_out(nc, w, s)
    gcn_hidden(nc, w, s)
    gcn_out(nc, out, w, s)
    relations(nc, out, w, s)


def lay_out(np, inputs):
    def padded(a, fill, before=0, after=0):
        line = np.full(before + SLOTS + after, fill, np.int32)
        line[before:before + E] = a
        return line

    def by_group(line):
        return line.reshape(NG, T, P).transpose(0, 2, 1)

    src, dst = np.asarray(inputs["src"]), np.asarray(inputs["dst"])
    line = padded(dst, N, 1, 1)
    line[0] = line[-1] = -1
    slot = np.arange(SLOTS, dtype=np.int32).reshape(NG, P, T)
    heads = np.repeat(np.eye(HEADS, dtype=np.float32), D // HEADS, axis=1)
    arrays = {
        "x": inputs["x"], "dst_line": line, "dst_cols": by_group(line[1:-1]),
        "dst_around": np.concatenate([by_group(line[1:-1]), by_group(line[:-2])], axis=2),
        "edge_ends": np.concatenate([by_group(padded(src, 0)), by_group(padded(dst, dst[-1]))], axis=2),
        "src_line": padded(src, OUT_ROWS - 1), "src_cols": by_group(padded(src, OUT_ROWS - 1)),
        "spare_rows": np.arange(N, N + GROUP, dtype=np.int32).reshape(T, P).T,
        "before": np.triu(np.ones((P, P), np.float32), 1),
        "slot_rows": slot, "edge_type": padded(np.asarray(inputs["edge_type_16"]), 0),
        "ident": np.eye(P, dtype=np.float32), "ones": np.ones((P, P), np.float32),
        "head_row": heads, "head_first": np.ascontiguousarray(heads.T) * (np.arange(D) % (D // HEADS) == 0).astype(np.float32)[:, None],
        "head_sum": heads.T * np.float32((D // HEADS) ** -0.5),
    }
    for name, a in inputs.items():
        if name.startswith("L"):
            arrays[name.split("_gnn_")[1]] = a
    arrays["w_self"] = np.asarray(inputs["L3_gnn_w_self"]).T
    return {k: np.ascontiguousarray(a) for k, a in arrays.items()}


def kernel(**inputs):
    import numpy as np
    import concourse.bacc as bacc
    from concourse.bass_utils import run_bass_kernel_spmd

    nc = bacc.Bacc("TRN2", target_bir_lowering=False, num_devices=1)
    arrays = lay_out(np, inputs)
    w = {k: nc.dram_tensor(f"in_{k}", a.shape, mybir.dt.from_np(a.dtype), kind="ExternalInput").ap()
         for k, a in arrays.items()}
    out = nc.dram_tensor("out_x", (OUT_ROWS, D), F32, kind="ExternalOutput").ap()

    def scratch(name, shape, dtype=F32):
        return nc.dram_tensor(name, shape, dtype, kind="Internal").ap()

    s = {k: w[k] for k in ("dst_line", "dst_cols", "dst_around", "edge_ends", "slot_rows", "edge_type", "src_line",
                           "src_cols")}
    s["table"] = {n: scratch(f"table{n}", (ROWS if n < 6 else SLOTS, D)) for n in range(1, 7)}
    s["row_of_node"] = scratch("row_of_node", (N, 1), I32)
    s["put_rows"] = scratch("put_rows", (NG, P, T), I32)
    s["add_rows"] = scratch("add_rows", (NG, P, T), I32)
    s["end_rows"] = scratch("end_rows", (NG, P, 2 * T), I32)
    s["same"] = scratch("same_runs", (NG, P, 2 * GROUP))
    s["masks"] = scratch("run_masks", (NG, HEADS, 2 * GROUP))
    s["logit"] = scratch("logits", (NG, HEADS, 2 * GROUP))
    s["degrees"] = scratch("degrees", (NG, 2 * T, P))
    for name in ("h_f", "x_f", "g_f", "x1_f", "value"):
        s[name] = scratch(f"slots_{name}", (NG, P, GROUP))
    s["x_ends"] = [scratch(f"x_ends{k}", (NG, P, GROUP)) for k in range(2)]
    gnn(nc, w["x"], out, w, s)
    r = run_bass_kernel_spmd(nc, [{f"in_{k}": a for k, a in arrays.items()}], core_ids=[0])
    return r.results[0]["out_x"][:N]
```
